# Optimizing a Trainium2 kernel written in Bass

```python
import numpy as np
import jax
import jax.numpy as jnp

def _softmax(x, axis=-1):
    return jax.nn.softmax(x, axis=axis)

def _gelu(x):
    return jax.nn.gelu(x, approximate=True)

def _silu(x):
    return jax.nn.silu(x)

def _sigmoid(x):
    return jax.nn.sigmoid(x)

def _layernorm(x, axis=-1, eps=1e-05):
    m = jnp.mean(x, axis=axis, keepdims=True)
    v = jnp.var(x, axis=axis, keepdims=True)
    return (x - m) / jnp.sqrt(v + eps)

def _scatter_add(tgt, idx, src, axis=0):
    return tgt.at[idx].add(src)

def _segment_sum(src, seg, n):
    return jax.ops.segment_sum(src, seg, n)
kernel_name = 'mk_adj_ffn_d2_adj_r2_a63536'

def setup_inputs(seed: int=0):
    np.random.seed(seed)
    _w = jnp.asarray

    def _rec_inputs():
        import jax
        import jax.numpy as jnp
        _gk = jax.random.key(seed)
        x = -0.0002928 + 1 * jax.random.normal(jax.random.fold_in(_gk, 1), (3327, 256), jnp.float32)
        _a = jax.random.bernoulli(jax.random.fold_in(_gk, 2), 0.00480914, (3327, 3327))
        _af = _a.astype(jnp.float32)
        adj = _af
        return (x, adj)
    x, adj = _rec_inputs()

    def _L0_gnn_setup():
        import jax, jax.numpy as jnp
        import numpy as np
        IN_C, HID_C = (256, 256)
        ALPHA = 0.2
        N = 4096
        NEG_BIG = -9000000000000000.0
        key = jax.random.key(seed)
        k1, k2, k3, k4, k5, k6, k7 = jax.random.split(key, 7)
        h = jax.random.normal(k1, (N, IN_C), dtype=jnp.float32)
        adj = jax.random.randint(k2, (N, N), 0, 2).astype(jnp.float32)
        gain = np.sqrt(2.0 / (1.0 + ALPHA ** 2))
        lim_W = gain * np.sqrt(6.0 / (2 * IN_C + HID_C))
        W = jax.random.uniform(k3, (2 * IN_C, HID_C), jnp.float32, -lim_W, lim_W)
        lim_a = np.sqrt(1.0 / HID_C)
        a_w = jax.random.uniform(k4, (HID_C,), jnp.float32, -lim_a, lim_a)
        a_b = jax.random.uniform(k5, (), jnp.float32, -lim_a, lim_a)
        lim_fc = np.sqrt(1.0 / IN_C)
        fc_w = jax.random.uniform(k6, (IN_C, HID_C), jnp.float32, -lim_fc, lim_fc)
        fc_b = jax.random.uniform(k7, (HID_C,), jnp.float32, -lim_fc, lim_fc)
        return {'h': h, 'adj': adj, 'W': W, 'a_w': a_w, 'a_b': a_b, 'fc_w': fc_w, 'fc_b': fc_b}
    _L0_gnn_all = _L0_gnn_setup()
    _L0_gnn_in = {k: v for k, v in _L0_gnn_all.items() if k in ('W', 'a_w', 'a_b', 'fc_w', 'fc_b')}
    del _L0_gnn_all

    def _L0_ffn_setup():
        import jax, jax.numpy as jnp
        import numpy as np
        E = 64
        K = 2
        CAP = 256
        H = 256
        FFN = 1024
        B, S = (8, 2048)
        key = jax.random.key(seed)
        ks = jax.random.split(key, 6)
        hidden_states = jax.random.normal(ks[0], (B, S, H), dtype=jnp.float32)
        router_w = jax.random.normal(ks[1], (E, H), dtype=jnp.float32) * (0.01 / np.sqrt(H))
        w1 = jax.random.normal(ks[2], (FFN, H), dtype=jnp.float32) * (1.0 / np.sqrt(H))
        b1 = jnp.zeros((FFN,), dtype=jnp.float32)
        w2 = jax.random.normal(ks[3], (H, FFN), dtype=jnp.float32) * (1.0 / np.sqrt(FFN))
        b2 = jnp.zeros((H,), dtype=jnp.float32)
        return {'hidden_states': hidden_states, 'router_w': router_w, 'w1': w1, 'b1': b1, 'w2': w2, 'b2': b2}
    _L0_ffn_all = _L0_ffn_setup()
    _L0_ffn_in = {k: v for k, v in _L0_ffn_all.items() if k in ('router_w', 'w1', 'b1', 'w2', 'b2')}
    del _L0_ffn_all

    def _L1_gnn_setup():
        import jax, jax.numpy as jnp
        import numpy as np
        N = 8192
        F_IN = 256
        F_OUT = 256
        key = jax.random.key(seed)
        k = jax.random.split(key, 6)
        h = jax.random.normal(k[0], (N, F_IN), dtype=jnp.float32)
        adj = jax.random.uniform(k[1], (N, N), dtype=jnp.float32)
        W_neigh = jax.random.normal(k[2], (F_OUT, F_IN), dtype=jnp.float32) * (1.0 / np.sqrt(F_IN))
        b_neigh = jax.random.normal(k[3], (F_OUT,), dtype=jnp.float32) * 0.01
        W_self = jax.random.normal(k[4], (F_OUT, F_IN), dtype=jnp.float32) * (1.0 / np.sqrt(F_IN))
        b_self = jax.random.normal(k[5], (F_OUT,), dtype=jnp.float32) * 0.01
        return {'h': h, 'adj': adj, 'W_neigh': W_neigh, 'b_neigh': b_neigh, 'W_self': W_self, 'b_self': b_self}
    _L1_gnn_all = _L1_gnn_setup()
    _L1_gnn_in = {k: v for k, v in _L1_gnn_all.items() if k in ('W_neigh', 'b_neigh', 'W_self', 'b_self')}
    del _L1_gnn_all

    def _L1_ffn_setup():
        import jax, jax.numpy as jnp
        import numpy as np
        B, S, D, DFF, E, K = (4, 1024, 256, 512, 8, 2)
        key = jax.random.key(seed)
        ks = jax.random.split(key, 5)
        x = jax.random.normal(ks[0], (B, S, D), dtype=jnp.float32)
        Wg = jax.random.normal(ks[1], (D, E), dtype=jnp.float32) * 0.02
        bg = jnp.zeros((E,), dtype=jnp.float32)
        W1 = jax.random.normal(ks[2], (E, D, 2 * DFF), dtype=jnp.float32) * 0.02
        b1 = jnp.zeros((E, 2 * DFF), dtype=jnp.float32)
        W2 = jax.random.normal(ks[3], (E, DFF, D), dtype=jnp.float32) * 0.02
        b2 = jnp.zeros((E, D), dtype=jnp.float32)
        return {'x': x, 'Wg': Wg, 'bg': bg, 'W1': W1, 'b1': b1, 'W2': W2, 'b2': b2}
    _L1_ffn_all = _L1_ffn_setup()
    _L1_ffn_in = {k: v for k, v in _L1_ffn_all.items() if k in ('Wg', 'bg', 'W1', 'b1', 'W2', 'b2')}
    del _L1_ffn_all
    return {'x': x, 'adj': adj, 'L0_gnn_W': _L0_gnn_in['W'], 'L0_gnn_a_w': _L0_gnn_in['a_w'], 'L0_gnn_a_b': _L0_gnn_in['a_b'], 'L0_gnn_fc_w': _L0_gnn_in['fc_w'], 'L0_gnn_fc_b': _L0_gnn_in['fc_b'], 'L0_ffn_router_w': _L0_ffn_in['router_w'], 'L0_ffn_w1': _L0_ffn_in['w1'], 'L0_ffn_b1': _L0_ffn_in['b1'], 'L0_ffn_w2': _L0_ffn_in['w2'], 'L0_ffn_b2': _L0_ffn_in['b2'], 'L1_gnn_W_neigh': _L1_gnn_in['W_neigh'], 'L1_gnn_b_neigh': _L1_gnn_in['b_neigh'], 'L1_gnn_W_self': _L1_gnn_in['W_self'], 'L1_gnn_b_self': _L1_gnn_in['b_self'], 'L1_ffn_Wg': _L1_ffn_in['Wg'], 'L1_ffn_bg': _L1_ffn_in['bg'], 'L1_ffn_W1': _L1_ffn_in['W1'], 'L1_ffn_b1': _L1_ffn_in['b1'], 'L1_ffn_W2': _L1_ffn_in['W2'], 'L1_ffn_b2': _L1_ffn_in['b2']}

def reference(x, adj, L0_gnn_W, L0_gnn_a_w, L0_gnn_a_b, L0_gnn_fc_w, L0_gnn_fc_b, L0_ffn_router_w, L0_ffn_w1, L0_ffn_b1, L0_ffn_w2, L0_ffn_b2, L1_gnn_W_neigh, L1_gnn_b_neigh, L1_gnn_W_self, L1_gnn_b_self, L1_ffn_Wg, L1_ffn_bg, L1_ffn_W1, L1_ffn_b1, L1_ffn_W2, L1_ffn_b2):
    import jax
    import jax.numpy as jnp

    def _L0_gnn_ref(h, adj, W, a_w, a_b, fc_w, fc_b):
        import jax, jax.numpy as jnp
        import numpy as np
        IN_C, HID_C = (256, 256)
        ALPHA = 0.2
        N = 4096
        NEG_BIG = -9000000000000000.0
        Wh1 = h @ W[:IN_C]
        Wh2 = h @ W[IN_C:]
        s1 = Wh1 @ a_w
        s2 = Wh2 @ a_w
        e = s1[:, None] + s2[None, :] + a_b
        e = jnp.where(e >= 0, e, ALPHA * e)
        e = jnp.where(adj > 0, e, NEG_BIG)
        att = jax.nn.softmax(e, axis=1)
        return att @ (h @ fc_w + fc_b)

    def _L0_ffn_ref(hidden_states, router_w, w1, b1, w2, b2):
        import jax, jax.numpy as jnp
        import numpy as np
        E = 64
        K = 2
        CAP = 256
        H = 256
        FFN = 1024
        B, S = (8, 2048)
        orig_shape = hidden_states.shape
        x = hidden_states.reshape(-1, orig_shape[-1])
        T = x.shape[0]
        N = T * K
        logits = jnp.einsum('th,eh->te', x, router_w)
        probs_full = jax.nn.softmax(logits, axis=-1)
        probs, idx = jax.lax.top_k(probs_full, K)
        flat_e = idx.reshape(-1)
        flat_p = probs.reshape(-1)
        order = jnp.argsort(flat_e, stable=True)
        sorted_e = flat_e[order]
        counts = jnp.zeros((E,), jnp.int32).at[flat_e].add(1)
        offsets = jnp.concatenate([jnp.zeros((1,), jnp.int32), jnp.cumsum(counts)[:-1]])
        pos = jnp.arange(N, dtype=jnp.int32) - offsets[sorted_e]
        keep = pos < CAP
        slot = sorted_e * CAP + jnp.minimum(pos, CAP - 1)
        dest = jnp.where(keep, slot, E * CAP)
        tok = order // K
        buf = jnp.zeros((E * CAP + 1, x.shape[-1]), x.dtype).at[dest].set(x[tok])
        buf = buf[:-1]
        h = jax.nn.gelu(jnp.einsum('nh,fh->nf', buf, w1) + b1, approximate=False)
        y = jnp.einsum('nf,hf->nh', h, w2) + b2
        gate = jnp.where(keep, flat_p[order], 0.0)
        contrib = y[jnp.minimum(slot, E * CAP - 1)] * gate[:, None]
        out = jnp.zeros_like(x).at[tok].add(contrib)
        return out.reshape(orig_shape)

    def _L1_gnn_ref(h, adj, W_neigh, b_neigh, W_self, b_self):
        import jax, jax.numpy as jnp
        import numpy as np
        N = 8192
        F_IN = 256
        F_OUT = 256
        deg = jnp.sum(adj, axis=1, keepdims=True) + 1e-05
        adj_norm = adj / deg
        h_neigh = adj_norm @ h
        out = h_neigh @ W_neigh.T + b_neigh + h @ W_self.T + b_self
        return jax.nn.relu(out)

    def _L1_ffn_ref(x, Wg, bg, W1, b1, W2, b2):
        import jax, jax.numpy as jnp
        import numpy as np
        B, S, D, DFF, E, K = (4, 1024, 256, 512, 8, 2)
        n_experts = W1.shape[0]
        logits = jnp.einsum('bsd,de->bse', x, Wg) + bg
        topk_vals, topk_idx = jax.lax.top_k(logits, K)
        topk_w = jax.nn.softmax(topk_vals, axis=-1)
        one_hot = jax.nn.one_hot(topk_idx, n_experts, dtype=x.dtype)
        weights_per_expert = jnp.einsum('bske,bsk->bse', one_hot, topk_w)
        h = jnp.einsum('bsd,edf->bsef', x, W1) + b1
        a, g = jnp.split(h, 2, axis=-1)
        act = jax.nn.silu(a) * g
        expert_out = jnp.einsum('bsef,efd->bsed', act, W2) + b2
        return jnp.einsum('bse,bsed->bsd', weights_per_expert, expert_out)
    x = x + _L0_gnn_ref(_layernorm(x, axis=-1), adj, L0_gnn_W, L0_gnn_a_w, L0_gnn_a_b, L0_gnn_fc_w, L0_gnn_fc_b)
    x = x + _L0_ffn_ref(_layernorm(x, axis=-1)[None], L0_ffn_router_w, L0_ffn_w1, L0_ffn_b1, L0_ffn_w2, L0_ffn_b2)[0]
    x = x + _L1_gnn_ref(_layernorm(x, axis=-1), adj, L1_gnn_W_neigh, L1_gnn_b_neigh, L1_gnn_W_self, L1_gnn_b_self)
    x = x + _L1_ffn_ref(_layernorm(x, axis=-1)[None], L1_ffn_Wg, L1_ffn_bg, L1_ffn_W1, L1_ffn_b1, L1_ffn_W2, L1_ffn_b2)[0]
    return x

_drawn_inputs = setup_inputs


def setup_inputs(seed=0):
    import zlib

    import numpy as np

    out = dict(_drawn_inputs(seed))
    spreads = {'L0_ffn_b1': (0.0, 0.8),
     'L0_ffn_b2': (0.0, 0.8),
     'L1_ffn_bg': (0.0, 0.1),
     'L1_ffn_b1': (0.0, 0.8),
     'L1_ffn_b2': (0.0, 0.1)}
    factors = {'L0_ffn_router_w': 8.0,
     'L0_ffn_w1': 2.859,
     'L1_gnn_b_neigh': 8.0,
     'L1_gnn_b_self': 7.915,
     'L1_ffn_W1': 3.789,
     'L1_ffn_W2': 3.783}
    for name, (base, spread) in spreads.items():
        noise = np.random.default_rng([zlib.crc32(name.encode()), seed]).standard_normal(out[name].shape)
        drawn = base * np.exp(spread * noise) if base else spread * noise
        out[name] = jnp.asarray(drawn.astype(out[name].dtype))
    for name, factor in factors.items():
        out[name] = (out[name] * factor).astype(out[name].dtype)
    return out
```

```python
from contextlib import ExitStack

import concourse.bass as bass
from concourse import mybir

ALU = mybir.AluOpType
ACT = mybir.ActivationFunctionType
AX_X = mybir.AxisListType.X
F32 = mybir.dt.float32
F16 = mybir.dt.float16
BF16 = mybir.dt.bfloat16
F8 = mybir.dt.float8e4
I32 = mybir.dt.int32
ds = bass.ds

P = 128
N = 3327
T = -(-N // P)
NP = T * P
D = 256
KD = D // P
EPS = 1e-5
ALPHA = 0.2
FAR = float(2 ** 53)
EDGE_SCALE = float(2 ** 126)
H_SCALE = float(2 ** 11)
P_SCALE = float(2 ** 15)
assert T % 2 == 0 and NP - N < P


def wait(eng, sem, value):
    if not (isinstance(value, int) and value <= 0):
        eng.wait_ge(sem, value)


def steps(eng, body, first, last, total):
    for t in range(first):
        body(t, t % 2)
    with eng.Fori(first, last - 1, 2) as i:
        for u in range(2):
            body(i + u, (first + u) % 2)
    for t in range(last, total):
        body(t, t % 2)


def pairs(eng, body):
    body(0)
    with eng.Fori(2, T - 1, 2) as t:
        body(t)


def semaphores(nc, ctx):
    made = []

    def make(name):
        made.append(nc.alloc_semaphore(name))
        return made[-1]

    def give_back():
        nc.clear_and_free_semaphores(made)
        nc.all_engine_barrier()

    ctx.callback(give_back)
    return make


def settled(eng, passed, *waits):
    for sem, count in waits:
        wait(eng, sem, count)
    eng.sem_inc(passed, 1)


class RowNorm:

    def __init__(self, nc, ctx, make, name, stats):
        sb = lambda n: ctx.enter_context(nc.sbuf_tensor(f"{name}_{n}", [P, T], F32))
        self.nc, self.stats = nc, stats
        self.sum, self.mean, self.gap, self.gap2, self.m2, self.var_in, self.var, self.std, self.rstd = (
            sb(n) for n in ("sum", "mean", "gap", "gap2", "m2", "var_in", "var", "std", "rstd"))
        self.chain, self.var_done, self.std_done = (make(f"{name}_{n}") for n in ("chain", "var_done", "std_done"))

    def deviation(self, act):
        act.wait_ge(self.var_done, 1)
        self.nc.scalar.activation(self.std[:, :], self.var[:, :], ACT.Sqrt).then_inc(self.std_done, 1)

    def finish(self, dve):
        v = self.nc.vector
        step = Chain(dve, self.chain)
        even, odd = (lambda n: self.stats[:, :, n]), (lambda n: self.stats[:, :, 3 + n])
        v.tensor_tensor(self.sum[:, :], even(1), odd(1), ALU.add).then_inc(self.chain, 1)
        v.tensor_tensor(self.gap[:, :], even(1), odd(1), ALU.subtract).then_inc(self.chain, 1)
        v.tensor_tensor(self.m2[:, :], even(2), odd(2), ALU.add).then_inc(self.chain, 1)
        step.count = 3
        dve.wait_ge(self.chain, 3)
        v.tensor_scalar(self.mean[:, :], self.sum[:, :], 0.5, None, ALU.mult).then_inc(self.chain, 1)
        v.tensor_tensor(self.gap2[:, :], self.gap[:, :], self.gap[:, :], ALU.mult).then_inc(self.chain, 1)
        v.tensor_scalar(self.var_in[:, :], self.m2[:, :], 1.0 / D, EPS, ALU.mult, ALU.add).then_inc(self.chain, 1)
        step.count = 6
        dve.wait_ge(self.chain, 6)
        v.scalar_tensor_tensor(self.var[:, :], self.gap2[:, :], 0.25, self.var_in[:, :], ALU.mult,
                               ALU.add).then_inc(self.var_done, 1)
        dve.wait_ge(self.std_done, 1)
        step(v.reciprocal(self.rstd[:, :], self.std[:, :]))

    def normalise(self, h, rows, t):
        return self.nc.vector.tensor_scalar(h, rows, self.mean[:, ds(t, 1)], self.rstd[:, ds(t, 1)],
                                            ALU.subtract, ALU.mult)


class Chain:

    def __init__(self, eng, sem):
        self.eng, self.sem, self.count = eng, sem, 0

    def __call__(self, instruction):
        self.count += 1
        instruction.then_inc(self.sem, 1)
        self.eng.wait_ge(self.sem, self.count)


def attention_scores(nc, t, dram):
    with ExitStack() as ctx:
        sb = lambda n, s, d=F32: ctx.enter_context(nc.sbuf_tensor(n, s, d))
        sem = semaphores(nc, ctx)
        X, H, S1, S2row, ident = t["X"], t["H"], t["S1"], t["S2row"], t["ident"]
        WT = sb("WT", [P, KD, 2 * D])
        awb = sb("awb", [P, KD, P])
        ab = sb("ab", [P, 1])
        ones = sb("ones", [P, P])
        U = sb("U", [P, 2 * D])
        norm = RowNorm(nc, ctx, sem, "ln0", t["stats"])
        h = [sb(f"h{u}", [P, D]) for u in range(2)]
        s12 = [sb(f"s12_{u}", [P, 2]) for u in range(2)]
        junk = sb("junk_a", [P, 4, D])
        diag = sb("diag", [P, T, P])
        psU = ctx.enter_context(nc.psum_tensor("psU", [P, 2 * D], F32))
        psR = ctx.enter_context(nc.psum_tensor("psR", [P, 2, 512], F32))
        XG = [(0, 7), (7, 14), (14, 20), (20, T)]
        x_in = [sem(f"x_in{n}") for n in range(len(XG))]
        w_in, h_done, stats_done = sem("aw_in"), sem("a_h"), sem("a_stats")
        u_done, u_copied, ones_set, s1_done = sem("u_done"), sem("u_copied"), sem("ones_set"), sem("a_s1")
        hi_done, lo_done, s_done, diag_done = sem("a_hi"), sem("a_lo"), sem("a_s"), sem("a_diag")
        row_done, row_copied = sem("a_row"), sem("a_rowcp")
        block = ctx.enter_context(nc.Block())
        xv = dram["x"].rearrange("(t p) d -> p t d", p=P)
        chunks = [(c, min(c + 4, T)) for c in range(0, T, 4)]

        @block.sync
        def _(sp):
            for n, (a, b) in enumerate(XG):
                sp.dma_start(X[:, a:b, :], xv[:, a:b, :]).then_inc(x_in[n], 16)
            sp.dma_start(WT[:, :, :], dram["WT"].rearrange("(k p) n -> p k n", p=P)).then_inc(w_in, 16)
            sp.dma_start(awb[:, :, :], dram["awb"]).then_inc(w_in, 16)
            sp.dma_start(ab[:, :], dram["ab"]).then_inc(w_in, 16)
            sp.dma_start(ident[:, :], dram["ident"]).then_inc(w_in, 16)
            for n in range(len(XG)):
                sp.wait_ge(x_in[n], 16)
            sp.wait_ge(w_in, 64)

        @block.tensor
        def _(pe):
            pe.wait_ge(w_in, 64)
            for k in range(KD):
                mm = nc.tensor.matmul(psU[:, :], awb[:, k, :], WT[:, k, :], start=(k == 0), stop=(k == KD - 1))
            mm.then_inc(u_done, 1)
            pe.wait_ge(ones_set, 1)
            for n, (a, b) in enumerate(chunks):
                pe.wait_ge(diag_done, b)
                wait(pe, row_copied, n - 1)
                nc.tensor.matmul(psR[:, n % 2, 0:(b - a) * P], ones[:, :],
                                 diag[:, a:b, :].rearrange("p t j -> p (t j)"),
                                 start=True, stop=True).then_inc(row_done, 1)

        @block.scalar
        def _(act):
            act.wait_ge(u_done, 1)
            nc.scalar.copy(U[:, :], psU[:, :]).then_inc(u_copied, 1)
            norm.deviation(act)

            def tile_pair(i):
                for u in range(2):
                    act.wait_ge(h_done, i + u + 1)
                    nc.scalar.activation(H[:, i + u, 0:D], h[u][:, :], ACT.Copy, scale=H_SCALE).then_inc(hi_done, 1)

            pairs(act, tile_pair)
            for n, (a, b) in enumerate(chunks):
                act.wait_ge(row_done, n + 1)
                nc.scalar.copy(S2row[:, a * P:b * P], psR[:, n % 2, 0:(b - a) * P]).then_inc(row_copied, 1)

        @block.vector
        def _(dve):
            nc.vector.memset(ones[:, :], 1.0).then_inc(ones_set, 1)
            for n, (a, b) in enumerate(XG):
                dve.wait_ge(x_in[n], 16)
                for i in range(a, b):
                    nc.vector.bn_stats(t["stats"][:, i, :], X[:, i, :]).then_inc(stats_done, 1)
            dve.wait_ge(stats_done, T)
            norm.finish(dve)
            dve.wait_ge(u_copied, 1)
            dve.wait_ge(w_in, 64)

            def tile_pair(i):
                for u in range(2):
                    wait(dve, s_done, 2 * (i + u) - 2)
                    wait(dve, lo_done, i + u - 1)
                    norm.normalise(h[u][:, :], X[:, i + u, :], i + u).then_inc(h_done, 1)
                for u in range(2):
                    dve.wait_ge(h_done, i + u + 1)
                    wait(dve, s_done, 2 * (i + u) - 2)
                    nc.vector.tensor_tensor_reduce(junk[:, 2 * u, :], h[u][:, :], U[:, 0:D], 1.0, 0.0, ALU.mult,
                                                   ALU.add, s12[u][:, 0:1]).then_inc(s_done, 1)
                    nc.vector.tensor_tensor_reduce(junk[:, 2 * u + 1, :], h[u][:, :], U[:, D:2 * D], 1.0, 0.0, ALU.mult,
                                                   ALU.add, s12[u][:, 1:2]).then_inc(s_done, 1)
                for u in range(2):
                    dve.wait_ge(hi_done, i + u + 1)
                    nc.vector.scalar_tensor_tensor(H[:, i + u, D:2 * D], h[u][:, :], H_SCALE, H[:, i + u, 0:D],
                                                   ALU.mult, ALU.subtract).then_inc(lo_done, 1)
                for u in range(2):
                    dve.wait_ge(s_done, 2 * (i + u + 1))
                    nc.vector.tensor_scalar(S1[:, ds(i + u, 1)], s12[u][:, 0:1], ab[:, 0:1], None,
                                            ALU.add).then_inc(s1_done, 1)
                    nc.vector.tensor_scalar(diag[:, i + u, :], ident[:, :], s12[u][:, 1:2], None,
                                            ALU.mult).then_inc(diag_done, 1)

            pairs(dve, tile_pair)


TG = [(0, 8), (8, 16), (16, 24), (24, T)]
NG = len(TG)


def graph_attention(nc, t, dram):
    with ExitStack() as ctx:
        sb = lambda n, s, d=F32: ctx.enter_context(nc.sbuf_tensor(n, s, d))
        sem = semaphores(nc, ctx)
        X, H, S1, S2row, ident, stats = t["X"], t["H"], t["S1"], t["S2row"], t["ident"], t["stats"]
        stats_done = sem("b_stats")
        adjf = [sb(f"adjf{u}", [P, NP]) for u in range(2)]
        bias = [sb(f"maskbias{u}", [P, NP], BF16) for u in range(2)]
        score = [sb(f"score{u}", [P, NP]) for u in range(2)]
        probs = [sb(f"probs{u}", [P, NP]) for u in range(2)]
        PThi = [sb(f"PThi{u}", [P, NP], F16) for u in range(2)]
        PTlo = [sb(f"PTlo{u}", [P, NP], F16) for u in range(2)]
        fcw = sb("fcw", [P, KD, D])
        fcb = sb("fcb", [P, D])
        big = sb("big", [P, 1])
        rowmax = [sb(f"rowmax{u}", [P, 1]) for u in range(2)]
        shifted = [sb(f"shifted{u}", [P, 1]) for u in range(2)]
        leaky = [sb(f"leaky{u}", [P, 1]) for u in range(2)]
        straight = [sb(f"straight{u}", [P, 1]) for u in range(2)]
        sloped = [sb(f"sloped{u}", [P, 1]) for u in range(2)]
        total = [sb(f"total{u}", [P, 1]) for u in range(2)]
        rtotal = sb("rtotal", [P, T])
        rscale = sb("rscale", [P, T])
        part = sb("part", [P, D])
        agg = [sb(f"agg{u}", [P, D]) for u in range(2)]
        aggT = [sb(f"aggT{u}", [P, KD, P]) for u in range(2)]
        ps = lambda n, s: ctx.enter_context(nc.psum_tensor(n, s, F32))
        psT = [ps(f"psT{u}", [P, 8 * P]) for u in range(2)]
        acc = [ps(f"acc{u}", [P, 2 * D]) for u in range(2)]
        psA = ps("psA", [P, 512])
        psF = ps("psF", [P, 512])
        adj_in = [sem(f"b_adj{u}") for u in range(2)]
        w_in, pad_set, mask_waits = sem("b_w"), sem("b_pad"), sem("b_mask_waits")
        mask_ready, masked_ready, small, shift_ready = sem("b_mask"), sem("b_masked"), sem("b_small"), sem("b_shift")
        straight_ready, sloped_ready = sem("b_straight"), sem("b_sloped")
        probs_ready, turned, hi_ready, lo_ready = (sem("b_probs"), sem("b_turned"),
                                                                sem("b_hi"), sem("b_lo"))
        acc_ready, scale_ready, agg_part, agg_ready = sem("b_acc"), sem("b_scale"), sem("b_part"), sem("b_agg")
        agg_turned, aggT_ready, fc_ready, x_part, x_ready = (sem("b_aggt"), sem("b_aggT"), sem("b_fc"), sem("b_xp"),
                                                             sem("b_x"))
        block = ctx.enter_context(nc.Block())
        adjv = dram["adj"].rearrange("(t p) j -> t p j", p=P)
        FIRST, LAST, TOTAL = 4, T - 4, T + 2

        def live(t):
            return not isinstance(t, int) or 0 <= t < T

        @block.sync
        def _(sp):
            sp.dma_start(fcw[:, :, :], dram["fcw"].rearrange("(k p) n -> p k n", p=P)).then_inc(w_in, 16)
            sp.dma_start(fcb[:, :], dram["fcb"]).then_inc(w_in, 16)

            def load(t, u):
                if live(t):
                    wait(sp, mask_ready, t - 1)
                    sp.dma_start(adjf[u][:, :], adjv[t, :, :]).then_inc(adj_in[u], 16)

            steps(sp, load, FIRST, LAST, T)
            sp.wait_ge(w_in, 32)

        @block.scalar
        def _(act):
            def hi(t, u, g):
                a, b = TG[g]
                act.wait_ge(turned, NG * t + g + 1)
                if g == 0:
                    wait(act, acc_ready, t - 1)
                nc.scalar.activation(PThi[u][:, a * P:b * P], psT[g % 2][:, 0:(b - a) * P], ACT.Copy,
                                     scale=P_SCALE).then_inc(hi_ready, 1)

            def no_edge(t, u):
                act.wait_ge(adj_in[u], 8 * (t - u) + 16)
                wait(act, masked_ready, t - 1)
                nc.scalar.activation(bias[u][:, 0:N], adjf[u][:, 0:N], ACT.Relu, bias=big[:, :],
                                     scale=-EDGE_SCALE).then_inc(mask_ready, 1)

            def straight_exp(t, u):
                act.wait_ge(shift_ready, 2 * t + 2)
                wait(act, turned, NG * (t - 1))
                nc.scalar.activation(probs[u][:, 0:N], score[u][:, 0:N], ACT.Exp,
                                     bias=straight[u][:, :]).then_inc(straight_ready, 1)

            def sloped_exp(t, u):
                act.wait_ge(straight_ready, t + 1)
                nc.scalar.activation(score[u][:, 0:N], score[u][:, 0:N], ACT.Exp, bias=sloped[u][:, :],
                                     scale=ALPHA).then_inc(sloped_ready, 1)

            def iteration(t, u):
                if live(t):
                    hi(t, u, 0)
                    hi(t, u, 1)
                if live(t + 1):
                    straight_exp(t + 1, 1 - u)
                if live(t - 2):
                    act.wait_ge(agg_turned, t - 1)
                    wait(act, fc_ready, t - 3)
                    nc.scalar.copy(aggT[u][:, :, :].rearrange("p k n -> p (k n)"), psA[:, 0:D]).then_inc(aggT_ready, 1)
                if live(t + 1):
                    sloped_exp(t + 1, 1 - u)
                if live(t):
                    hi(t, u, 2)
                    hi(t, u, 3)
                if live(t + 3):
                    no_edge(t + 3, 1 - u)

            act.wait_ge(pad_set, 3)
            no_edge(0, 0)
            no_edge(1, 1)
            straight_exp(0, 0)
            sloped_exp(0, 0)
            no_edge(2, 0)
            steps(act, iteration, FIRST, LAST, TOTAL)

        @block.vector
        def _(dve):
            nc.vector.memset(big[:, :], FAR).then_inc(pad_set, 1)
            for u in range(2):
                nc.vector.memset(probs[u][:, N:NP], 0.0).then_inc(pad_set, 1)

            def masked(t, u):
                settled(dve, mask_waits, (mask_ready, t + 1), (probs_ready, t - 1))
                nc.vector.tensor_tensor_reduce(score[u][:, 0:N], S2row[:, 0:N], bias[u][:, 0:N], 1.0, -2 * FAR,
                                               ALU.subtract, ALU.max, rowmax[u][:, :]).then_inc(masked_ready, 1)
                dve.wait_ge(masked_ready, t + 1)
                nc.vector.tensor_tensor(shifted[u][:, :], rowmax[u][:, :], S1[:, ds(t, 1)],
                                        ALU.add).then_inc(small, 1)
                dve.wait_ge(small, 2 * t + 1)
                nc.vector.scalar_tensor_tensor(leaky[u][:, :], shifted[u][:, :], ALPHA, shifted[u][:, :],
                                               ALU.mult, ALU.max).then_inc(small, 1)
                dve.wait_ge(small, 2 * t + 2)
                nc.vector.tensor_tensor(straight[u][:, :], S1[:, ds(t, 1)], leaky[u][:, :],
                                        ALU.subtract).then_inc(shift_ready, 1)
                nc.vector.scalar_tensor_tensor(sloped[u][:, :], S1[:, ds(t, 1)], ALPHA, leaky[u][:, :], ALU.mult,
                                               ALU.subtract).then_inc(shift_ready, 1)

            def combine(t, u):
                dve.wait_ge(sloped_ready, t + 1)
                nc.vector.scalar_tensor_tensor(probs[u][:, 0:N], score[u][:, 0:N], 1.0, probs[u][:, 0:N], ALU.mult,
                                               ALU.max, accum_out=total[u][:, :]).then_inc(probs_ready, 1)

            def lo(t, u, g):
                a, b = TG[g]
                dve.wait_ge(hi_ready, NG * t + g + 1)
                nc.vector.scalar_tensor_tensor(PTlo[u][:, a * P:b * P], psT[g % 2][:, 0:(b - a) * P], P_SCALE,
                                               PThi[u][:, a * P:b * P], ALU.mult, ALU.subtract).then_inc(lo_ready, 1)

            def row_scale(t, u):
                dve.wait_ge(probs_ready, t + 1)
                nc.vector.reciprocal(rtotal[:, ds(t, 1)], total[u][:, :]).then_inc(scale_ready, 1)
                dve.wait_ge(scale_ready, 2 * t + 1)
                nc.vector.tensor_scalar(rscale[:, ds(t, 1)], rtotal[:, ds(t, 1)], 1.0 / (H_SCALE * P_SCALE), None,
                                        ALU.mult).then_inc(scale_ready, 1)

            def aggregate(t, u):
                dve.wait_ge(scale_ready, 2 * t + 2)
                dve.wait_ge(acc_ready, t + 1)
                wait(dve, agg_turned, t - 1)
                nc.vector.tensor_scalar(part[:, :], acc[u][:, 0:D], rscale[:, ds(t, 1)], None,
                                        ALU.mult).then_inc(agg_part, 1)
                dve.wait_ge(agg_part, t + 1)
                nc.vector.scalar_tensor_tensor(agg[u][:, :], acc[u][:, D:2 * D], rscale[:, ds(t, 1)], part[:, :],
                                               ALU.mult, ALU.add).then_inc(agg_ready, 1)

            def residual(t, u):
                dve.wait_ge(fc_ready, t + 1)
                nc.vector.tensor_tensor(X[:, t, :], psF[:, 0:D], X[:, t, :], ALU.add).then_inc(x_part, 1)
                dve.wait_ge(x_part, t + 1)
                nc.vector.tensor_tensor(X[:, t, :], X[:, t, :], fcb[:, :], ALU.add).then_inc(x_ready, 1)
                dve.wait_ge(x_ready, t + 1)
                nc.vector.bn_stats(stats[:, t, :], X[:, t, :]).then_inc(stats_done, 1)

            def iteration(t, u):
                if live(t - 2):
                    aggregate(t - 2, u)
                if live(t):
                    lo(t, u, 0)
                    lo(t, u, 1)
                if live(t + 2):
                    masked(t + 2, u)
                if live(t + 1):
                    combine(t + 1, 1 - u)
                    row_scale(t + 1, 1 - u)
                if live(t):
                    lo(t, u, 2)
                    lo(t, u, 3)
                if live(t - 2):
                    residual(t - 2, u)

            masked(0, 0)
            masked(1, 1)
            combine(0, 0)
            row_scale(0, 0)
            dve.wait_ge(w_in, 32)
            steps(dve, iteration, FIRST, LAST, TOTAL)

        @block.tensor
        def _(pe):
            def turn(t, u, g):
                a, b = TG[g]
                if g == 0:
                    pe.wait_ge(probs_ready, t + 1)
                wait(pe, hi_ready, NG * t + g - 1)
                wait(pe, lo_ready, NG * t + g - 1)
                for j in range(a, b):
                    mm = nc.tensor.transpose(psT[g % 2][:, (j - a) * P:(j - a + 1) * P],
                                             probs[u][:, j * P:(j + 1) * P], ident[:, :])
                mm.then_inc(turned, 1)

            def products(t, u, g):
                a, b = TG[g]
                pe.wait_ge(lo_ready, NG * t + g + 1)
                if g == 0:
                    wait(pe, agg_ready, t - 1)
                for j in range(a, b):
                    high = (acc[u][:, :], PThi[u][:, j * P:(j + 1) * P], H[:, j, 0:2 * D])
                    low = (acc[u][:, 0:D], PTlo[u][:, j * P:(j + 1) * P], H[:, j, 0:D])
                    for n, (to, left, right) in enumerate((low, high) if j == T - 1 else (high, low)):
                        mm = nc.tensor.matmul(to, left, right, start=(j == 0 and n == 0), stop=(j == T - 1 and n == 1),
                                              skip_group_check=True)
                if g == NG - 1:
                    mm.then_inc(acc_ready, 1)

            def iteration(t, u):
                if live(t):
                    turn(t, u, 0)
                    turn(t, u, 1)
                if live(t - 1):
                    products(t - 1, 1 - u, 0)
                if live(t - 2):
                    pe.wait_ge(agg_ready, t - 1)
                    wait(pe, aggT_ready, t - 2)
                    for k in range(KD):
                        mm = nc.tensor.transpose(psA[:, k * P:(k + 1) * P], agg[u][:, k * P:(k + 1) * P], ident[:, :])
                    mm.then_inc(agg_turned, 1)
                if live(t):
                    turn(t, u, 2)
                if live(t - 1):
                    products(t - 1, 1 - u, 1)
                if live(t):
                    turn(t, u, 3)
                if live(t - 2):
                    pe.wait_ge(aggT_ready, t - 1)
                    wait(pe, x_part, t - 2)
                    for k in range(KD):
                        mm = nc.tensor.matmul(psF[:, 0:D], aggT[u][:, k, :], fcw[:, k, :], start=(k == 0),
                                              stop=(k == KD - 1))
                    mm.then_inc(fc_ready, 1)
                if live(t - 1):
                    products(t - 1, 1 - u, 2)
                    products(t - 1, 1 - u, 3)

            pe.wait_ge(w_in, 32)
            pe.wait_ge(pad_set, 3)
            steps(pe, iteration, FIRST, LAST, TOTAL)


def normalised_projection(nc, t, name, w_dram, width, out, bias=None, HT=None, H=None, rows=None, preload=None):
    with ExitStack() as ctx:
        make = semaphores(nc, ctx)
        sem = lambda n: make(f"{name}_{n}")
        X, ident = t["X"], t["ident"]
        norm = RowNorm(nc, ctx, make, name + "_ln", t["stats"])
        h = [ctx.enter_context(nc.sbuf_tensor(f"{name}_h{u}", [P, D], F32)) for u in range(2)]
        h_done = sem("h_done")
        W = ctx.enter_context(nc.sbuf_tensor(name + "_W", [P, KD, width], F32))
        hT = [ctx.enter_context(nc.sbuf_tensor(f"{name}_hT{u}", [P, KD, P], F32)) for u in range(2)]
        psT = [ctx.enter_context(nc.psum_tensor(f"{name}_psT{u}", [P, 512], F32)) for u in range(2)]
        psO = [ctx.enter_context(nc.psum_tensor(f"{name}_psO{u}", [P, 512], F32)) for u in range(2)]
        w_in, turned, hT_ready, copied, projected, out_ready = (sem("w"), sem("turned"), sem("hT"), sem("copied"),
                                                                sem("projected"), sem("out"))
        hi_ready, lo_ready, rows_ready, bias_ready = sem("hi"), sem("lo"), sem("rows"), sem("bias")
        if bias is not None:
            bias_sb = ctx.enter_context(nc.sbuf_tensor(name + "_bias", [P, 2, width], F32))
        block = ctx.enter_context(nc.Block())
        loads = 1 + len(bias or ())

        @block.sync
        def _(sp):
            sp.dma_start(W[:, :, :], w_dram.rearrange("(k p) n -> p k n", p=P)).then_inc(w_in, 16)
            if preload is not None:
                preload(sp)
            if bias is not None:
                for n, b in enumerate(bias):
                    sp.dma_start(bias_sb[:, n, :], b).then_inc(w_in, 16)
            sp.wait_ge(w_in, 16 * loads)

        @block.scalar
        def _(act):
            def tile_pair(i):
                for u in range(2):
                    if H is not None:
                        act.wait_ge(h_done, i + u + 1)
                        nc.scalar.activation(H[:, i + u, 0:D], h[u][:, :], ACT.Copy,
                                             scale=H_SCALE).then_inc(hi_ready, 1)
                for u in range(2):
                    act.wait_ge(turned, i + u + 1)
                    wait(act, projected, i + u - 1)
                    nc.scalar.copy(hT[u][:, :, :].rearrange("p k n -> p (k n)"), psT[u][:, 0:D]).then_inc(hT_ready, 1)
                    if HT is not None:
                        nc.scalar.copy(HT[:, :, ds((i + u) * P, P)],
                                       psT[u][:, 0:D].rearrange("p (k n) -> p k n", k=KD)).then_inc(copied, 1)

            norm.deviation(act)
            pairs(act, tile_pair)

        @block.tensor
        def _(pe):
            def tile_pair(i):
                for u in range(2):
                    pe.wait_ge(h_done, i + u + 1)
                    wait(pe, copied if HT is not None else hT_ready, i + u - 1)
                    for k in range(KD):
                        mm = nc.tensor.transpose(psT[u][:, k * P:(k + 1) * P], h[u][:, k * P:(k + 1) * P],
                                                 ident[:, :])
                    mm.then_inc(turned, 1)
                for u in range(2):
                    pe.wait_ge(hT_ready, i + u + 1)
                    wait(pe, out_ready, i + u - 1)
                    for k in range(KD):
                        mm = nc.tensor.matmul(psO[u][:, 0:width], hT[u][:, k, :], W[:, k, :], start=(k == 0),
                                              stop=(k == KD - 1))
                    mm.then_inc(projected, 1)

            pe.wait_ge(w_in, 16 * loads)
            pairs(pe, tile_pair)

        @block.vector
        def _(dve):
            def produce(i):
                for u in range(2):
                    wait(dve, turned, i + u - 1)
                    if H is not None:
                        wait(dve, lo_ready, i + u - 1)
                    if rows is not None:
                        wait(dve, rows_ready, i + u - 1)
                    norm.normalise(h[u][:, :], X[:, i + u, :], i + u).then_inc(h_done, 1)
                for u in range(2):
                    if H is not None:
                        dve.wait_ge(hi_ready, i + u + 1)
                        nc.vector.scalar_tensor_tensor(H[:, i + u, D + 2:2 * D + 2], h[u][:, :], H_SCALE,
                                                       H[:, i + u, 0:D], ALU.mult, ALU.subtract).then_inc(lo_ready, 1)
                    if rows is not None:
                        dve.wait_ge(h_done, i + u + 1)
                        nc.vector.tensor_copy(rows[:, i + u, :], h[u][:, :]).then_inc(rows_ready, 1)

            def collect(i):
                for u in range(2):
                    dve.wait_ge(projected, i + u + 1)
                    if bias is not None:
                        nc.vector.tensor_tensor(out[:, i + u, :], psO[u][:, 0:width], bias_sb[:, 0, :],
                                                ALU.add).then_inc(out_ready, 1)
                    else:
                        nc.vector.tensor_copy(out[:, i + u, :], psO[u][:, 0:width]).then_inc(out_ready, 1)

            norm.finish(dve)
            if bias is not None:
                dve.wait_ge(w_in, 16 * loads)
                if len(bias) == 2:
                    nc.vector.tensor_tensor(bias_sb[:, 0, :], bias_sb[:, 0, :], bias_sb[:, 1, :],
                                            ALU.add).then_inc(bias_ready, 1)
                    dve.wait_ge(bias_ready, 1)
            produce(0)
            with dve.Fori(2, T - 1, 2) as i:
                produce(i)
                collect(i - 2)
            collect(T - 2)


def wide(ap, shape):
    return ap.unsqueeze(2).to_broadcast(shape)


class TopTwo:

    def __init__(self, nc, ctx, name, E):
        sb = lambda n, s, d=F32: ctx.enter_context(nc.sbuf_tensor(f"{name}_{n}", s, d))
        self.nc, self.E = nc, E
        self.descending = sb("descending", [P, T, E])
        self.score = sb("score", [P, T, E])
        self.rest = sb("rest", [P, T, E])
        self.rank = sb("rank", [P, T])
        self.best = [sb(f"best{k}", [P, T]) for k in range(2)]
        self.one_hot = [sb(f"one_hot{k}", [P, T, E]) for k in range(2)]

    def steps(self, step, logits):
        nc, E, v = self.nc, self.E, self.nc.vector
        full = [P, T, E]
        for k in range(2):
            src = logits if k == 0 else self.rest
            step(v.tensor_reduce(self.best[k][:, :], src[:, :, :], AX_X, ALU.max))
            step(v.tensor_tensor(self.score[:, :, :], src[:, :, :], wide(self.best[k][:, :], full), ALU.is_equal))
            step(v.tensor_tensor(self.score[:, :, :], self.score[:, :, :], self.descending[:, :, :], ALU.mult))
            step(v.tensor_reduce(self.rank[:, :], self.score[:, :, :], AX_X, ALU.max))
            step(v.tensor_tensor(self.one_hot[k][:, :, :], self.score[:, :, :], wide(self.rank[:, :], full),
                                 ALU.is_equal))
            if k == 0:
                step(v.scalar_tensor_tensor(self.rest[:, :, :], self.one_hot[0][:, :, :], -FAR * FAR,
                                            logits[:, :, :], ALU.mult, ALU.add))


E0 = 64
CAP = 256
F0 = 1024
MF = F0 // P
CH = 256
NCH = NP // CH
RC = 4
assert NP % CH == 0 and T * E0 % RC == 0 and T * E0 // RC <= 512


def capacity_ffn(nc, t, dram):
    with ExitStack() as ctx:
        sb = lambda n, s, d=F32: ctx.enter_context(nc.sbuf_tensor(n, s, d))
        sem = semaphores(nc, ctx)
        X, HT, L = t["X"], t["HT"], t["L0"]
        w1 = sb("w1", [P, KD, F0])
        w2 = sb("w2", [P, MF, D])
        b1 = sb("b1", [P, MF])
        b2 = sb("b2", [P, D])
        G = [sb(f"G{u}", [P, MF, CH]) for u in range(2)]
        Y = sb("Y", [P, T, D])
        top = TopTwo(nc, ctx, "r0", E0)
        chosen = sb("chosen", [P, T, E0], F16)
        before = sb("before", [P, T, E0])
        sums = [sb(f"sums{k}", [P, T, E0]) for k in range(2)]
        tri = sb("tri", [P, P], F16)
        ones = sb("ones16", [P, P], F16)
        z, rz, e2, gate, held = (sb(n, [P, T]) for n in ("z", "rz", "e2", "gate", "held"))
        share = [sb(f"share{k}", [P, T]) for k in range(2)]
        ps = lambda n, s: ctx.enter_context(nc.psum_tensor(n, s, F32))
        psH = [ps(f"psH{u}", [P, 512]) for u in range(2)]
        psY = [ps(f"psY{u}", [P, 512]) for u in range(2)]
        psC = ps("psC", [P, RC, 512])
        w_in, r_in = sem("c_w"), sem("c_r")
        hidden, active, y_done, y_copied = sem("c_hidden"), sem("c_active"), sem("c_y"), sem("c_ycp")
        chain, chosen_ready, counted, before_ready, exp_in, exp_out = (sem("c_chain"), sem("c_chosen"), sem("c_counted"),
                                                               sem("c_before"), sem("c_expin"), sem("c_expout"))
        stats_done = sem("c_stats")
        biased, x_ready, zero_set, zeroed = sem("c_biased"), sem("c_x"), sem("c_zero"), sem("c_zeroed")
        zero = sb("zero", [P, D])
        block = ctx.enter_context(nc.Block())
        W = T * E0 // RC

        @block.sync
        def _(sp):
            sp.dma_start(top.descending[:, :, :], dram["desc0"]).then_inc(r_in, 16)
            sp.dma_start(tri[:, :], dram["tri"]).then_inc(r_in, 16)
            sp.dma_start(ones[:, :], dram["ones"]).then_inc(r_in, 16)
            sp.dma_start(w1[:, :, :], dram["w1T"].rearrange("(k p) n -> p k n", p=P)).then_inc(w_in, 16)
            sp.dma_start(w2[:, :, :], dram["w2T"].rearrange("(k p) n -> p k n", p=P)).then_inc(w_in, 16)
            sp.dma_start(b1[:, :], dram["b1c"]).then_inc(w_in, 16)
            sp.dma_start(b2[:, :], dram["b2"]).then_inc(w_in, 16)
            sp.wait_ge(zero_set, 1)
            sp.dma_start(dram["slot_rows"].rearrange("(s p) d -> p s d", p=P),
                         zero[:, :].unsqueeze(1).to_broadcast([P, NS, D])).then_inc(zeroed, 16)
            sp.wait_ge(zeroed, 16)
            sp.wait_ge(r_in, 48)
            sp.wait_ge(w_in, 64)

        @block.tensor
        def _(pe):
            def hidden_part(c, u, m):
                b = m // 2
                if m % 2 == 0:
                    wait(pe, active, MF * c + m - 2)
                for k in range(KD):
                    mm = nc.tensor.matmul(psH[b % 2][:, (m % 2) * CH:(m % 2 + 1) * CH], w1[:, k, m * P:(m + 1) * P],
                                          HT[:, k, ds(c * CH, CH)], start=(k == 0), stop=(k == KD - 1))
                mm.then_inc(hidden, 1)

            def output_part(c, u, s):
                pe.wait_ge(active, MF * (c + 1))
                wait(pe, y_copied, 2 * c + s - 1)
                for m in range(MF):
                    mm = nc.tensor.matmul(psY[s][:, 0:D], G[u][:, m, s * P:(s + 1) * P], w2[:, m, :],
                                          start=(m == 0), stop=(m == MF - 1))
                mm.then_inc(y_done, 1)

            def iteration(c, u):
                if not isinstance(c, int) or c < NCH:
                    for m in range(MF):
                        hidden_part(c, u, m)
                if not isinstance(c, int) or c > 0:
                    for s in range(2):
                        output_part(c - 1, 1 - u, s)

            pe.wait_ge(w_in, 64)
            iteration(0, 0)
            iteration(1, 1)
            iteration(2, 0)
            iteration(3, 1)
            pe.wait_ge(r_in, 48)
            pe.wait_ge(chosen_ready, 1)
            for stationary in (tri, ones):
                if stationary is ones:
                    pe.wait_ge(before_ready, 1)
                for c in range(RC):
                    flat = chosen[:, :, :].rearrange("p t e -> p (t e)")
                    mm = nc.tensor.matmul(psC[:, c, 0:W], stationary[:, :], flat[:, c * W:(c + 1) * W],
                                          start=True, stop=True)
                mm.then_inc(counted, 1)
            with pe.Fori(4, NCH - 2, 2) as c:
                for u in range(2):
                    iteration(c + u, u)
            for c in range(NCH - 1, NCH + 1):
                iteration(c, c % 2)

        @block.scalar
        def _(act):
            def iteration(c, u):
                for m in range(MF):
                    act.wait_ge(hidden, MF * c + (m // 2 + 1) * 2)
                    if m == 0:
                        wait(act, y_done, 2 * (c - 1))
                    nc.scalar.activation(G[u][:, m, :], psH[m // 2 % 2][:, (m % 2) * CH:(m % 2 + 1) * CH], ACT.Gelu,
                                         bias=b1[:, m:m + 1]).then_inc(active, 1)

            def take(c):
                for s in range(2):
                    act.wait_ge(y_done, 2 * c + s + 1)
                    nc.scalar.copy(Y[:, c * 2 + s, :], psY[s][:, 0:D]).then_inc(y_copied, 1)

            act.wait_ge(exp_in, 1)
            nc.scalar.activation(top.rest[:, :, :], top.rest[:, :, :], ACT.Exp).then_inc(exp_out, 1)
            act.wait_ge(exp_in, 2)
            nc.scalar.activation(e2[:, :], held[:, :], ACT.Exp).then_inc(exp_out, 1)
            act.wait_ge(w_in, 64)
            iteration(0, 0)
            iteration(1, 1)
            take(0)
            with act.Fori(2, NCH - 2, 2) as c:
                for u in range(2):
                    iteration(c + u, u)
                    take(c + u - 1)
            iteration(NCH - 1, (NCH - 1) % 2)
            take(NCH - 2)
            take(NCH - 1)

        @block.vector
        def _(dve):
            v = nc.vector
            step = Chain(dve, chain)
            full = [P, T, E0]
            v.memset(zero[:, :], 0.0).then_inc(zero_set, 1)
            dve.wait_ge(r_in, 48)
            top.steps(step, L)
            step(v.tensor_tensor(top.score[:, :, :], top.one_hot[0][:, :, :], top.one_hot[1][:, :, :], ALU.add))
            v.tensor_copy(chosen[:, :, :], top.score[:, :, :]).then_inc(chosen_ready, 1)
            v.tensor_tensor(top.rest[:, :, :], L[:, :, :], wide(top.best[0][:, :], full),
                            ALU.subtract).then_inc(exp_in, 1)
            v.tensor_tensor(held[:, :], top.best[1][:, :], top.best[0][:, :], ALU.subtract).then_inc(exp_in, 1)
            dve.wait_ge(exp_out, 2)
            step(v.tensor_reduce(z[:, :], top.rest[:, :, :], AX_X, ALU.add))
            step(v.reciprocal(share[0][:, :], z[:, :]))
            step(v.tensor_tensor(share[1][:, :], e2[:, :], share[0][:, :], ALU.mult))
            dve.wait_ge(counted, 1)
            flat = lambda x: x[:, :, :].rearrange("p t e -> p (t e)").rearrange("p (c w) -> p c w", c=RC)
            v.tensor_copy(flat(before), psC[:, :, 0:W]).then_inc(before_ready, 1)
            dve.wait_ge(counted, 2)
            step(v.tensor_copy(flat(sums[0]), psC[:, :, 0:W]))
            a, b, reach = sums[0], sums[1], 1
            while reach < T:
                step(v.tensor_copy(b[:, 0:reach, :], a[:, 0:reach, :]))
                step(v.tensor_tensor(b[:, reach:T, :], a[:, reach:T, :], a[:, 0:T - reach, :], ALU.add))
                a, b, reach = b, a, 2 * reach
            step(v.tensor_tensor(before[:, 1:T, :], before[:, 1:T, :], a[:, 0:T - 1, :], ALU.add))
            for k in range(2):
                step(v.tensor_tensor(top.score[:, :, :], before[:, :, :], top.one_hot[k][:, :, :], ALU.mult))
                step(v.tensor_reduce(held[:, :], top.score[:, :, :], AX_X, ALU.add))
                step(v.scalar_tensor_tensor(share[k][:, :], held[:, :], float(CAP), share[k][:, :], ALU.is_lt,
                                            ALU.mult))
            step(v.tensor_tensor(gate[:, :], share[0][:, :], share[1][:, :], ALU.add))
            dve.wait_ge(w_in, 64)
            with dve.Fori(0, T) as i:
                dve.wait_ge(y_copied, i + 1)
                v.tensor_tensor(Y[:, i, :], Y[:, i, :], b2[:, :], ALU.add).then_inc(biased, 1)
                dve.wait_ge(biased, i + 1)
                v.scalar_tensor_tensor(X[:, i, :], Y[:, i, :], gate[:, ds(i, 1)], X[:, i, :], ALU.mult,
                                       ALU.add).then_inc(x_ready, 1)
                dve.wait_ge(x_ready, i + 1)
                v.bn_stats(t["stats"][:, i, :], X[:, i, :]).then_inc(stats_done, 1)


def mean_aggregation(nc, t, dram):
    with ExitStack() as ctx:
        sb = lambda n, s, d=F32: ctx.enter_context(nc.sbuf_tensor(n, s, d))
        sem = semaphores(nc, ctx)
        X, H, own, ident, stats = t["X"], t["H"], t["own"], t["ident"], t["stats"]
        stats_done = sem("d_stats")
        adjf = [sb(f"adjTf{u}", [P, NP]) for u in range(2)]
        adjh = [sb(f"adjTh{u}", [P, NP], F16) for u in range(2)]
        Wn = sb("Wn", [P, KD, D])
        degree = [sb(f"degree{u}", [P, 1]) for u in range(2)]
        rdegree = [sb(f"rdegree{u}", [P, 1]) for u in range(2)]
        agg = [sb(f"mean{u}", [P, D]) for u in range(2)]
        aggT = [sb(f"meanT{u}", [P, KD, P]) for u in range(2)]
        out = [sb(f"summed{u}", [P, D]) for u in range(2)]
        ps = lambda n: ctx.enter_context(nc.psum_tensor(n, [P, 512], F32))
        acc = [ps(f"sum{u}") for u in range(2)]
        psA = [ps(f"psM{u}") for u in range(2)]
        psF = [ps(f"psN{u}") for u in range(2)]
        adj_in = [sem(f"d_adj{u}") for u in range(2)]
        w_in, half_ready, ones_set = sem("d_w"), sem("d_half"), sem("d_ones")
        acc_ready, deg_ready, rdeg_ready, agg_ready = sem("d_acc"), sem("d_deg"), sem("d_rdeg"), sem("d_agg")
        turned, aggT_ready, proj_ready, out_ready, x_ready = (sem("d_turned"), sem("d_aggT"), sem("d_proj"),
                                                              sem("d_out"), sem("d_x"))
        block = ctx.enter_context(nc.Block())
        adjv = dram["adjT"]
        FIRST, LAST, TOTAL = 4, T - 2, T + 2

        def live(t):
            return not isinstance(t, int) or 0 <= t < T

        @block.sync
        def _(sp):
            sp.dma_start(Wn[:, :, :], dram["WnT"].rearrange("(k p) n -> p k n", p=P)).then_inc(w_in, 16)

            def load(t, u):
                wait(sp, half_ready, t - 1)
                sp.dma_start(adjf[u][:, :], adjv[t, :, :]).then_inc(adj_in[u], 16)

            steps(sp, load, FIRST, LAST, T)
            sp.wait_ge(w_in, 16)

        @block.scalar
        def _(act):
            def iteration(t, u):
                if live(t):
                    act.wait_ge(adj_in[u], 8 * (t - u) + 16)
                    wait(act, acc_ready, t - 1)
                    nc.scalar.copy(adjh[u][:, :], adjf[u][:, :]).then_inc(half_ready, 1)
                if live(t - 2):
                    act.wait_ge(turned, t - 1)
                    wait(act, proj_ready, t - 3)
                    nc.scalar.copy(aggT[u][:, :, :].rearrange("p k n -> p (k n)"),
                                   psA[u][:, 0:D]).then_inc(aggT_ready, 1)

            steps(act, iteration, FIRST, LAST, TOTAL)

        @block.tensor
        def _(pe):
            def products(t, u):
                pe.wait_ge(half_ready, t + 1)
                wait(pe, agg_ready, t - 1)
                for j in range(T):
                    left = adjh[u][:, j * P:(j + 1) * P]
                    nc.tensor.matmul(acc[u][:, 0:D + 1], left, H[:, j, 0:D + 1], start=(j == 0), stop=False,
                                     skip_group_check=True)
                    mm = nc.tensor.matmul(acc[u][:, 0:D], left, H[:, j, D + 2:2 * D + 2], start=False, stop=(j == T - 1),
                                          skip_group_check=True)
                mm.then_inc(acc_ready, 1)

            def iteration(t, u):
                if live(t - 1):
                    pe.wait_ge(agg_ready, t)
                    wait(pe, aggT_ready, t - 2)
                    for k in range(KD):
                        mm = nc.tensor.transpose(psA[1 - u][:, k * P:(k + 1) * P], agg[1 - u][:, k * P:(k + 1) * P],
                                                 ident[:, :])
                    mm.then_inc(turned, 1)
                if live(t - 2):
                    pe.wait_ge(aggT_ready, t - 1)
                    wait(pe, out_ready, t - 3)
                    for k in range(KD):
                        mm = nc.tensor.matmul(psF[u][:, 0:D], aggT[u][:, k, :], Wn[:, k, :], start=(k == 0),
                                              stop=(k == KD - 1))
                    mm.then_inc(proj_ready, 1)

            pe.wait_ge(w_in, 16)
            pe.wait_ge(ones_set, 1)

            def whole(t, u):
                if live(t):
                    products(t, u)
                iteration(t, u)

            steps(pe, whole, FIRST, LAST, TOTAL)

        @block.vector
        def _(dve):
            v = nc.vector
            v.memset(H[:, :, D:D + 1], 1.0).then_inc(ones_set, 1)

            def aggregate(t, u):
                dve.wait_ge(acc_ready, t + 1)
                v.tensor_scalar(degree[u][:, :], acc[u][:, D:D + 1], EPS, None, ALU.add).then_inc(deg_ready, 1)
                dve.wait_ge(deg_ready, t + 1)
                v.reciprocal(rdegree[u][:, :], degree[u][:, :]).then_inc(rdeg_ready, 1)
                dve.wait_ge(rdeg_ready, t + 1)
                wait(dve, turned, t - 1)
                v.tensor_scalar(agg[u][:, :], acc[u][:, 0:D], rdegree[u][:, :], 1.0 / H_SCALE, ALU.mult,
                                ALU.mult).then_inc(agg_ready, 1)

            def residual(t, u):
                dve.wait_ge(proj_ready, t + 1)
                wait(dve, x_ready, t - 1)
                v.tensor_tensor(out[u][:, :], psF[u][:, 0:D], own[:, t, :], ALU.add).then_inc(out_ready, 1)
                dve.wait_ge(out_ready, t + 1)
                v.scalar_tensor_tensor(X[:, t, :], out[u][:, :], 0.0, X[:, t, :], ALU.max, ALU.add).then_inc(x_ready, 1)
                dve.wait_ge(x_ready, t + 1)
                v.bn_stats(stats[:, t, :], X[:, t, :]).then_inc(stats_done, 1)

            def iteration(t, u):
                if live(t):
                    aggregate(t, u)
                if live(t - 2):
                    residual(t - 2, u)

            steps(dve, iteration, FIRST, LAST, TOTAL)


E1 = 8
F1 = 512
KF = F1 // P
NS = (2 * NP - E1) // P + E1
assert NS * P >= 2 * NP


def dispatch(nc, t, dram):
    with ExitStack() as ctx:
        sb = lambda n, s, d=F32: ctx.enter_context(nc.sbuf_tensor(n, s, d))
        sem = semaphores(nc, ctx)
        L, rows, slots, share, expert = t["L1"], t["rows"], t["slots"], t["share"], t["expert"]
        top = TopTwo(nc, ctx, "r1", E1)
        full = [P, T, E1]
        chosen = sb("chosen1", full, F16)
        before = sb("before1", full)
        sums = [sb(f"sums1_{k}", full) for k in range(2)]
        tri = sb("tri1", [P, P], F16)
        ones = sb("ones1", [P, P], F16)
        limits = sb("limits", [P, E1, T])
        tile_no = sb("tile_no", [P, NS, E1])
        over = sb("over", [P, E1, T])
        passed = sb("passed", [P, NS, E1])
        tiles = sb("tiles", [P, E1])
        ends = [sb(f"ends{k}", [P, E1]) for k in range(2)]
        base = sb("base", [P, E1])
        slot = sb("slot", [P, T])
        expert_f = sb("expert_f", [P, NS])
        gap, grown, denominator = sb("gap", [P, T]), sb("odds", [P, T]), sb("denominator", [P, T])
        psC = ctx.enter_context(nc.psum_tensor("psC1", [P, 2, 512], F32))
        c_in, chain, chosen_ready, counted, gap_ready, grown_ready = (sem("e_in"), sem("e_chain"), sem("e_chosen"),
                                                                      sem("e_counted"), sem("e_gap"), sem("e_grown"))
        slots_ready, scattered = sem("e_slots"), sem("e_scattered")
        block = ctx.enter_context(nc.Block())

        @block.sync
        def _(sp):
            for to, name in ((top.descending, "desc1"), (tri, "tri"), (ones, "ones"), (limits, "limits"),
                             (tile_no, "tile_no")):
                sp.dma_start(to[...], dram[name]).then_inc(c_in, 16)
            sp.wait_ge(c_in, 80)

        @block.tensor
        def _(pe):
            pe.wait_ge(c_in, 80)
            pe.wait_ge(chosen_ready, 1)
            for n, stationary in enumerate((tri, ones)):
                nc.tensor.matmul(psC[:, n, 0:T * E1], stationary[:, :],
                                 chosen[:, :, :].rearrange("p t e -> p (t e)"), start=True,
                                 stop=True).then_inc(counted, 1)

        @block.scalar
        def _(act):
            act.wait_ge(gap_ready, 1)
            nc.scalar.activation(grown[:, :], gap[:, :], ACT.Exp).then_inc(grown_ready, 1)

        @block.vector
        def _(dve):
            v = nc.vector
            step = Chain(dve, chain)
            dve.wait_ge(c_in, 80)
            top.steps(step, L)
            step(v.tensor_tensor(top.score[:, :, :], top.one_hot[0][:, :, :], top.one_hot[1][:, :, :], ALU.add))
            v.tensor_copy(chosen[:, :, :], top.score[:, :, :]).then_inc(chosen_ready, 1)
            v.tensor_tensor(gap[:, :], top.best[1][:, :], top.best[0][:, :], ALU.subtract).then_inc(gap_ready, 1)
            dve.wait_ge(grown_ready, 1)
            step(v.tensor_scalar(denominator[:, :], grown[:, :], 1.0, None, ALU.add))
            step(v.reciprocal(share[0][:, :], denominator[:, :]))
            step(v.tensor_tensor(share[1][:, :], grown[:, :], share[0][:, :], ALU.mult))
            flat = lambda x: x[:, :, :].rearrange("p t e -> p (t e)")
            dve.wait_ge(counted, 2)
            step(v.tensor_copy(flat(before), psC[:, 0, 0:T * E1]))
            step(v.tensor_copy(flat(sums[0]), psC[:, 1, 0:T * E1]))
            a, b, reach = sums[0], sums[1], 1
            while reach < T:
                step(v.tensor_copy(b[:, 0:reach, :], a[:, 0:reach, :]))
                step(v.tensor_tensor(b[:, reach:T, :], a[:, reach:T, :], a[:, 0:T - reach, :], ALU.add))
                a, b, reach = b, a, 2 * reach
            step(v.tensor_tensor(before[:, 1:T, :], before[:, 1:T, :], a[:, 0:T - 1, :], ALU.add))
            step(v.tensor_tensor(over[:, :, :], wide(a[:, T - 1, :], [P, E1, T]), limits[:, :, :], ALU.is_gt))
            step(v.tensor_reduce(tiles[:, :], over[:, :, :], AX_X, ALU.add))
            step(v.tensor_copy(ends[0][:, :], tiles[:, :]))
            a, b, reach = ends[0], ends[1], 1
            while reach < E1:
                step(v.tensor_copy(b[:, 0:reach], a[:, 0:reach]))
                step(v.tensor_tensor(b[:, reach:E1], a[:, reach:E1], a[:, 0:E1 - reach], ALU.add))
                a, b, reach = b, a, 2 * reach
            step(v.tensor_tensor(base[:, :], a[:, :], tiles[:, :], ALU.subtract))
            step(v.tensor_scalar(base[:, :], base[:, :], float(P), None, ALU.mult))
            step(v.tensor_tensor(before[:, :, :], before[:, :, :],
                                 base[:, :].unsqueeze(1).to_broadcast(full), ALU.add))
            for k in range(2):
                step(v.tensor_tensor(top.score[:, :, :], before[:, :, :], top.one_hot[k][:, :, :], ALU.mult))
                step(v.tensor_reduce(slot[:, :], top.score[:, :, :], AX_X, ALU.add))
                v.tensor_copy(slots[k][:, :], slot[:, :]).then_inc(slots_ready, 1)
                dve.wait_ge(slots_ready, k + 1)
            step(v.tensor_tensor(passed[:, :, :], tile_no[:, :, :],
                                 a[:, :].unsqueeze(1).to_broadcast([P, NS, E1]), ALU.is_ge))
            step(v.tensor_reduce(expert_f[:, :], passed[:, :, :], AX_X, ALU.add))
            step(v.tensor_scalar(expert_f[:, :], expert_f[:, :], float(E1 - 1), None, ALU.min))
            step(v.tensor_copy(expert[:, :], expert_f[:, :]))

        @block.gpsimd
        def _(pool):
            for k in range(2):
                pool.wait_ge(slots_ready, k + 1)
                for n in range(T):
                    pool.indirect_dma_start(out=dram["slot_rows"], in_=rows[:, n, :], in_offset=None,
                                            out_offset=bass.IndirectOffsetOnAxis(ap=slots[k][:, n:n + 1], axis=0)
                                            ).then_inc(scattered, 16)
            pool.wait_ge(scattered, 16 * 2 * T)


def expert_ffn(nc, t, dram):
    with ExitStack() as ctx:
        sb = lambda n, s, d=F32: ctx.enter_context(nc.sbuf_tensor(n, s, d))
        sem = semaphores(nc, ctx)
        W1, W2, expert, ident = t["W1"], t["W2"], t["expert"], t["ident"]
        b1 = sb("eb1", [P, E1, 2 * F1])
        b2 = sb("eb2", [P, E1, D])
        xs = [sb(f"xs{u}", [P, D]) for u in range(2)]
        xT = [sb(f"xT{u}", [P, KD, P]) for u in range(2)]
        hb = [sb(f"hb{u}", [P, 2 * F1]) for u in range(2)]
        silu = [sb(f"silu{u}", [P, F1]) for u in range(2)]
        act_sb = [sb(f"act{u}", [P, F1]) for u in range(2)]
        actT = [sb(f"actT{u}", [P, KF, P]) for u in range(2)]
        ys = [sb(f"ys{u}", [P, D]) for u in range(2)]
        ps = lambda n, w: ctx.enter_context(nc.psum_tensor(n, [P, w], F32))
        psH = [ps(f"ePsH{u}", 2 * F1) for u in range(2)]
        psX, psA = ps("ePsX", 512), ps("ePsA", 512)
        psY = [ps(f"ePsY{u}", 512) for u in range(2)]
        b_in = sem("f_b")
        x_in = [sem(f"f_x{u}") for u in range(2)]
        stored = [sem(f"f_stored{u}") for u in range(2)]
        x_turned, xT_ready, h_ready, hb_ready, silu_ready, act_ready = (sem("f_xt"), sem("f_xT"), sem("f_h"), sem("f_hb"),
                                                                        sem("f_silu"), sem("f_act"))
        a_turned, actT_ready, y_ready, ys_ready = sem("f_at"), sem("f_aT"), sem("f_y"), sem("f_ys")
        block = ctx.enter_context(nc.Block())
        src = dram["slot_rows"].rearrange("(s p) d -> s p d", p=P)
        dst = dram["slot_out"].rearrange("(s p) d -> s p d", p=P)
        FIRST, LAST, TOTAL = 4, NS - 3 + (NS - 1) % 2, NS + 3

        def live(s):
            return not isinstance(s, int) or 0 <= s < NS

        def tile_expert(eng, s):
            return eng.value_load(expert[0:1, ds(s, 1)], min_val=0, max_val=E1 - 1)

        @block.sync
        def _(sp):
            sp.dma_start(b1[:, :, :], dram["eb1"]).then_inc(b_in, 16)
            sp.dma_start(b2[:, :, :], dram["eb2"]).then_inc(b_in, 16)

            def iteration(s, u):
                if live(s):
                    wait(sp, x_turned, s - 1)
                    sp.dma_start(xs[u][:, :], src[s, :, :]).then_inc(x_in[u], 16)
                if live(s - 3):
                    sp.wait_ge(ys_ready, s - 2)
                    sp.dma_start(dst[s - 3, :, :], ys[1 - u][:, :]).then_inc(stored[1 - u], 16)

            steps(sp, iteration, FIRST, LAST, TOTAL)
            sp.wait_ge(b_in, 32)
            for u in range(2):
                sp.wait_ge(stored[u], 16 * ((NS + 1 - u) // 2))

        @block.tensor
        def _(pe):
            def turn_rows(s, u):
                pe.wait_ge(x_in[u], 8 * (s - u) + 16)
                wait(pe, xT_ready, s)
                for k in range(KD):
                    mm = nc.tensor.transpose(psX[:, k * P:(k + 1) * P], xs[u][:, k * P:(k + 1) * P], ident[:, :])
                mm.then_inc(x_turned, 1)

            def iteration(s, u):
                if live(s):
                    e = tile_expert(pe, s)
                    pe.wait_ge(xT_ready, s + 1)
                    wait(pe, hb_ready, s - 1)
                    for n in range(2):
                        for k in range(KD):
                            mm = nc.tensor.matmul(psH[u][:, n * F1:(n + 1) * F1], xT[u][:, k, :],
                                                  W1[:, e, k, n * F1:(n + 1) * F1], start=(k == 0), stop=(k == KD - 1))
                    mm.then_inc(h_ready, 1)
                if live(s - 1):
                    pe.wait_ge(act_ready, s)
                    wait(pe, actT_ready, s - 1)
                    for k in range(KF):
                        mm = nc.tensor.transpose(psA[:, k * P:(k + 1) * P], act_sb[1 - u][:, k * P:(k + 1) * P],
                                                 ident[:, :])
                    mm.then_inc(a_turned, 1)
                if live(s + 1):
                    turn_rows(s + 1, 1 - u)
                if live(s - 2):
                    e = tile_expert(pe, s - 2)
                    pe.wait_ge(actT_ready, s - 1)
                    wait(pe, ys_ready, s - 3)
                    for k in range(KF):
                        mm = nc.tensor.matmul(psY[u][:, 0:D], actT[u][:, k, :], W2[:, e, k, :], start=(k == 0),
                                              stop=(k == KF - 1))
                    mm.then_inc(y_ready, 1)

            pe.wait_ge(t["W1_in"], 16)
            pe.wait_ge(t["W2_in"], 16)
            turn_rows(0, 0)
            steps(pe, iteration, FIRST, LAST, TOTAL)

        @block.scalar
        def _(act):
            def rows_back(s, u):
                act.wait_ge(x_turned, s + 1)
                wait(act, h_ready, s - 1)
                nc.scalar.copy(xT[u][:, :, :].rearrange("p k n -> p (k n)"), psX[:, 0:D]).then_inc(xT_ready, 1)

            def iteration(s, u):
                if live(s - 1):
                    act.wait_ge(a_turned, s)
                    wait(act, y_ready, s - 3)
                    nc.scalar.copy(actT[1 - u][:, :, :].rearrange("p k n -> p (k n)"), psA[:, :]).then_inc(actT_ready, 1)
                if live(s + 1):
                    rows_back(s + 1, 1 - u)
                if live(s):
                    act.wait_ge(hb_ready, s + 1)
                    wait(act, act_ready, s - 1)
                    nc.scalar.activation(silu[u][:, :], hb[u][:, 0:F1], ACT.Silu).then_inc(silu_ready, 1)

            rows_back(0, 0)
            steps(act, iteration, FIRST, LAST, TOTAL)

        @block.vector
        def _(dve):
            v = nc.vector

            def iteration(s, u):
                if live(s):
                    e = tile_expert(dve, s)
                    dve.wait_ge(h_ready, s + 1)
                    wait(dve, act_ready, s - 1)
                    v.tensor_tensor(hb[u][:, :], psH[u][:, :], b1[:, e, :], ALU.add).then_inc(hb_ready, 1)
                    dve.wait_ge(silu_ready, s + 1)
                    wait(dve, a_turned, s - 1)
                    v.tensor_tensor(act_sb[u][:, :], silu[u][:, :], hb[u][:, F1:2 * F1], ALU.mult).then_inc(act_ready, 1)
                if live(s - 2):
                    e = tile_expert(dve, s - 2)
                    dve.wait_ge(y_ready, s - 1)
                    if live(s - 4):
                        dve.wait_ge(stored[u], 8 * (s - 4 - u) + 16)
                    v.tensor_tensor(ys[u][:, :], psY[u][:, 0:D], b2[:, e, :], ALU.add).then_inc(ys_ready, 1)

            dve.wait_ge(b_in, 32)
            steps(dve, iteration, FIRST, LAST, TOTAL)


def combine_and_store(nc, t, dram, out):
    with ExitStack() as ctx:
        sem = semaphores(nc, ctx)
        X, slots, share = t["X"], t["slots"], t["share"]
        results = ctx.enter_context(nc.sbuf_tensor("results", [P, T, 2, D], F32))
        groups = [(n, min(n + 4, T)) for n in range(0, T, 4)]
        fetched = [sem(f"g_fetched{n}") for n in range(len(groups))]
        added, done, stored = sem("g_added"), sem("g_done"), sem("g_stored")
        block = ctx.enter_context(nc.Block())

        @block.gpsimd
        def _(pool):
            for n in range(T):
                for k in range(2):
                    pool.indirect_dma_start(out=results[:, n, k, :], in_=dram["slot_out"], out_offset=None,
                                            in_offset=bass.IndirectOffsetOnAxis(ap=slots[k][:, n:n + 1], axis=0)
                                            ).then_inc(fetched[n // 4], 16)

        @block.vector
        def _(dve):
            for n in range(T):
                if n % 4 == 0:
                    a, b = groups[n // 4]
                    dve.wait_ge(fetched[n // 4], 32 * (b - a))
                for k in range(2):
                    nc.vector.scalar_tensor_tensor(X[:, n, :], results[:, n, k, :], share[k][:, n:n + 1], X[:, n, :],
                                                   ALU.mult, ALU.add).then_inc(added if k == 0 else done, 1)
                    if k == 0:
                        dve.wait_ge(added, n + 1)

        @block.sync
        def _(sp):
            for n in range(T):
                sp.wait_ge(done, n + 1)
                rows = min(P, N - n * P)
                sp.dma_start(out[n * P:n * P + rows, :], X[0:rows, n, :]).then_inc(stored, 16)
            sp.wait_ge(stored, 16 * T)


def gnn_program(nc, dram, out):
    with ExitStack() as ctx:
        sb = lambda n, s, d=F32: ctx.enter_context(nc.sbuf_tensor(n, s, d))
        t = {"X": sb("X", [P, T, D]), "ident": sb("ident", [P, P]), "stats": sb("stats", [P, T, 6])}
        H_scope = ctx.enter_context(ExitStack())
        t["H"] = H_scope.enter_context(nc.sbuf_tensor("H", [P, T, 2 * D + 2], F16))
        with ExitStack() as att:
            sa = lambda n, s, d=F32: att.enter_context(nc.sbuf_tensor(n, s, d))
            t["S1"] = sa("S1", [P, T])
            t["S2row"] = sa("S2row", [P, NP])
            attention_scores(nc, t, dram)
            graph_attention(nc, t, dram)
        with ExitStack() as ffn:
            t["HT"] = ffn.enter_context(nc.sbuf_tensor("HT", [P, KD, NP], F32))
            t["L0"] = ffn.enter_context(nc.sbuf_tensor("L0", [P, T, E0], F32))
            normalised_projection(nc, t, "r0p", dram["rwT"], E0, t["L0"], HT=t["HT"])
            capacity_ffn(nc, t, dram)
        with ExitStack() as agg:
            t["own"] = agg.enter_context(nc.sbuf_tensor("own", [P, T, D], F32))
            normalised_projection(nc, t, "self", dram["WsT"], D, t["own"], bias=(dram["b_self"], dram["b_neigh"]), H=t["H"])
            mean_aggregation(nc, t, dram)
        H_scope.close()
        t["W1_in"] = ctx.enter_context(nc.semaphore("W1_in"))
        t["W2_in"] = ctx.enter_context(nc.semaphore("W2_in"))
        t["slots"] = [sb(f"slots{k}", [P, T], I32) for k in range(2)]
        t["share"] = [sb(f"part{k}", [P, T]) for k in range(2)]
        t["expert"] = sb("expert", [P, NS], I32)
        with ExitStack() as experts:
            t["W1"] = experts.enter_context(nc.sbuf_tensor("W1", [P, E1, KD, 2 * F1], F32))
            t["W2"] = experts.enter_context(nc.sbuf_tensor("W2", [P, E1, KF, D], F32))
            with ExitStack() as route:
                t["rows"] = route.enter_context(nc.sbuf_tensor("rows", [P, T, D], F32))
                t["L1"] = route.enter_context(nc.sbuf_tensor("L1", [P, T, E1], F32))

                def load_experts(sp):
                    sp.dma_start(t["W1"][:, :, :, :], dram["eW1"]).then_inc(t["W1_in"], 16)
                    sp.dma_start(t["W2"][:, :, :, :], dram["eW2"]).then_inc(t["W2_in"], 16)

                normalised_projection(nc, t, "r1p", dram["Wg"], E1, t["L1"], bias=(dram["bg"],), rows=t["rows"],
                                      preload=load_experts)
                dispatch(nc, t, dram)
            expert_ffn(nc, t, dram)
        combine_and_store(nc, t, dram, out)


def kernel(**inputs):
    import numpy as np
    import concourse.bacc as bacc
    from concourse.bass_utils import run_bass_kernel_spmd

    a = {k: np.asarray(v) for k, v in inputs.items()}
    full = lambda v, shape: np.ascontiguousarray(np.broadcast_to(v, shape))
    flip = lambda v: np.ascontiguousarray(v.T)
    adj = np.pad(a["adj"], ((0, NP - N), (0, NP - N)))
    adj_tiles = np.ascontiguousarray(adj.reshape(T, P, T, P).transpose(0, 3, 2, 1)).reshape(T, P, NP)
    arrays = {
        "x": np.pad(a["x"], ((0, NP - N), (0, 0))),
        "adj": adj,
        "WT": flip(a["L0_gnn_W"]),
        "awb": full(a["L0_gnn_a_w"].reshape(KD, P).T[:, :, None], (P, KD, P)),
        "ab": full(a["L0_gnn_a_b"].reshape(1, 1), (P, 1)),
        "ident": np.eye(P, dtype=np.float32),
        "fcw": np.ascontiguousarray(a["L0_gnn_fc_w"]),
        "fcb": full(a["L0_gnn_fc_b"], (P, D)),
        "rwT": flip(a["L0_ffn_router_w"]),
        "desc0": full(np.arange(E0, 0, -1, dtype=np.float32), (P, T, E0)),
        "tri": np.triu(np.ones((P, P), np.float16), 1),
        "ones": np.ones((P, P), np.float16),
        "w1T": flip(a["L0_ffn_w1"]),
        "w2T": flip(a["L0_ffn_w2"]),
        "b1c": flip(a["L0_ffn_b1"].reshape(MF, P)),
        "b2": full(a["L0_ffn_b2"], (P, D)),
        "WsT": flip(a["L1_gnn_W_self"]),
        "WnT": flip(a["L1_gnn_W_neigh"]),
        "adjT": adj_tiles,
        "Wg": a["L1_ffn_Wg"],
        "bg": full(a["L1_ffn_bg"], (P, E1)),
        "desc1": full(np.arange(E1, 0, -1, dtype=np.float32), (P, T, E1)),
        "limits": full(P * np.arange(T, dtype=np.float32), (P, E1, T)),
        "tile_no": full(np.arange(NS, dtype=np.float32)[:, None], (P, NS, E1)),
        "eW1": np.ascontiguousarray(a["L1_ffn_W1"].reshape(E1, KD, P, 2 * F1).transpose(2, 0, 1, 3)),
        "eW2": np.ascontiguousarray(a["L1_ffn_W2"].reshape(E1, KF, P, D).transpose(2, 0, 1, 3)),
        "eb1": full(a["L1_ffn_b1"], (P, E1, 2 * F1)),
        "eb2": full(a["L1_ffn_b2"], (P, E1, D)),
        "b_self": full(a["L1_gnn_b_self"], (P, D)),
        "b_neigh": full(a["L1_gnn_b_neigh"], (P, D)),
    }
    nc = bacc.Bacc("TRN2", target_bir_lowering=False, num_devices=1)
    dram = {k: nc.dram_tensor(k + "_dram", v.shape, mybir.dt.from_np(v.dtype), kind="ExternalInput").ap()
            for k, v in arrays.items()}
    for name in ("slot_rows", "slot_out"):
        dram[name] = nc.dram_tensor(name, (NS * P, D), F32, kind="Internal").ap()
    out = nc.dram_tensor("out_dram", (N, D), F32, kind="ExternalOutput").ap()
    gnn_program(nc, dram, out)
    r = run_bass_kernel_spmd(nc, [{k + "_dram": v for k, v in arrays.items()}], core_ids=[0])
    return r.results[0]["out_dram"]
```

```python
from contextlib import ExitStack

import concourse.bass as bass
from concourse import mybir

ALU = mybir.AluOpType
ACT = mybir.ActivationFunctionType
AX_X = mybir.AxisListType.X
F32 = mybir.dt.float32
F16 = mybir.dt.float16
BF16 = mybir.dt.bfloat16
F8 = mybir.dt.float8e4
I32 = mybir.dt.int32
ds = bass.ds

P = 128
N = 3327
T = -(-N // P)
NP = T * P
D = 256
KD = D // P
EPS = 1e-5
ALPHA = 0.2
FAR = float(2 ** 53)
EDGE_SCALE = float(2 ** 126)
H_SCALE = float(2 ** 11)
P_SCALE = float(2 ** 15)
assert T % 2 == 0 and NP - N < P


def wait(eng, sem, value):
    if not (isinstance(value, int) and value <= 0):
        eng.wait_ge(sem, value)


def steps(eng, body, first, last, total):
    for t in range(first):
        body(t, t % 2)
    with eng.Fori(first, last - 1, 2) as i:
        for u in range(2):
            body(i + u, (first + u) % 2)
    for t in range(last, total):
        body(t, t % 2)


def pairs(eng, body):
    body(0)
    with eng.Fori(2, T - 1, 2) as t:
        body(t)


def semaphores(nc, ctx):
    made = []

    def make(name):
        made.append(nc.alloc_semaphore(name))
        return made[-1]

    def give_back():
        nc.clear_and_free_semaphores(made)
        nc.all_engine_barrier()

    ctx.callback(give_back)
    return make


def settled(eng, passed, *waits):
    for sem, count in waits:
        wait(eng, sem, count)
    eng.sem_inc(passed, 1)


class RowNorm:

    def __init__(self, nc, ctx, make, name, stats):
        sb = lambda n: ctx.enter_context(nc.sbuf_tensor(f"{name}_{n}", [P, T], F32))
        self.nc, self.stats = nc, stats
        self.sum, self.mean, self.gap, self.gap2, self.m2, self.var_in, self.var, self.std, self.rstd = (
            sb(n) for n in ("sum", "mean", "gap", "gap2", "m2", "var_in", "var", "std", "rstd"))
        self.chain, self.var_done, self.std_done = (make(f"{name}_{n}") for n in ("chain", "var_done", "std_done"))

    def deviation(self, act):
        act.wait_ge(self.var_done, 1)
        self.nc.scalar.activation(self.std[:, :], self.var[:, :], ACT.Sqrt).then_inc(self.std_done, 1)

    def finish(self, dve):
        v = self.nc.vector
        step = Chain(dve, self.chain)
        even, odd = (lambda n: self.stats[:, :, n]), (lambda n: self.stats[:, :, 3 + n])
        v.tensor_tensor(self.sum[:, :], even(1), odd(1), ALU.add).then_inc(self.chain, 1)
        v.tensor_tensor(self.gap[:, :], even(1), odd(1), ALU.subtract).then_inc(self.chain, 1)
        v.tensor_tensor(self.m2[:, :], even(2), odd(2), ALU.add).then_inc(self.chain, 1)
        step.count = 3
        dve.wait_ge(self.chain, 3)
        v.tensor_scalar(self.mean[:, :], self.sum[:, :], 0.5, None, ALU.mult).then_inc(self.chain, 1)
        v.tensor_tensor(self.gap2[:, :], self.gap[:, :], self.gap[:, :], ALU.mult).then_inc(self.chain, 1)
        v.tensor_scalar(self.var_in[:, :], self.m2[:, :], 1.0 / D, EPS, ALU.mult, ALU.add).then_inc(self.chain, 1)
        step.count = 6
        dve.wait_ge(self.chain, 6)
        v.scalar_tensor_tensor(self.var[:, :], self.gap2[:, :], 0.25, self.var_in[:, :], ALU.mult,
                               ALU.add).then_inc(self.var_done, 1)
        dve.wait_ge(self.std_done, 1)
        step(v.reciprocal(self.rstd[:, :], self.std[:, :]))

    def normalise(self, h, rows, t):
        return self.nc.vector.tensor_scalar(h, rows, self.mean[:, ds(t, 1)], self.rstd[:, ds(t, 1)],
                                            ALU.subtract, ALU.mult)


class Chain:

    def __init__(self, eng, sem):
        self.eng, self.sem, self.count = eng, sem, 0

    def __call__(self, instruction):
        self.count += 1
        instruction.then_inc(self.sem, 1)
        self.eng.wait_ge(self.sem, self.count)


def attention_scores(nc, t, dram):
    with ExitStack() as ctx:
        sb = lambda n, s, d=F32: ctx.enter_context(nc.sbuf_tensor(n, s, d))
        sem = semaphores(nc, ctx)
        X, H, S1, S2row, ident = t["X"], t["H"], t["S1"], t["S2row"], t["ident"]
        WT = sb("WT", [P, KD, 2 * D])
        awb = sb("awb", [P, KD, P])
        ab = sb("ab", [P, 1])
        ones = sb("ones", [P, P])
        U = sb("U", [P, 2 * D])
        norm = RowNorm(nc, ctx, sem, "ln0", t["stats"])
        h = [sb(f"h{u}", [P, D]) for u in range(2)]
        s12 = [sb(f"s12_{u}", [P, 2]) for u in range(2)]
        junk = sb("junk_a", [P, 4, D])
        diag = sb("diag", [P, T, P])
        psU = ctx.enter_context(nc.psum_tensor("psU", [P, 2 * D], F32))
        psR = ctx.enter_context(nc.psum_tensor("psR", [P, 2, 512], F32))
        XG = [(0, 7), (7, 14), (14, 20), (20, T)]
        x_in = [sem(f"x_in{n}") for n in range(len(XG))]
        w_in, h_done, stats_done = sem("aw_in"), sem("a_h"), sem("a_stats")
        u_done, u_copied, ones_set, s1_done = sem("u_done"), sem("u_copied"), sem("ones_set"), sem("a_s1")
        hi_done, lo_done, s_done, diag_done = sem("a_hi"), sem("a_lo"), sem("a_s"), sem("a_diag")
        row_done, row_copied = sem("a_row"), sem("a_rowcp")
        block = ctx.enter_context(nc.Block())
        xv = dram["x"].rearrange("(t p) d -> p t d", p=P)
        chunks = [(c, min(c + 4, T)) for c in range(0, T, 4)]

        @block.sync
        def _(sp):
            for n, (a, b) in enumerate(XG):
                sp.dma_start(X[:, a:b, :], xv[:, a:b, :]).then_inc(x_in[n], 16)
            sp.dma_start(WT[:, :, :], dram["WT"].rearrange("(k p) n -> p k n", p=P)).then_inc(w_in, 16)
            sp.dma_start(awb[:, :, :], dram["awb"]).then_inc(w_in, 16)
            sp.dma_start(ab[:, :], dram["ab"]).then_inc(w_in, 16)
            sp.dma_start(ident[:, :], dram["ident"]).then_inc(w_in, 16)
            for n in range(len(XG)):
                sp.wait_ge(x_in[n], 16)
            sp.wait_ge(w_in, 64)

        @block.tensor
        def _(pe):
            pe.wait_ge(w_in, 64)
            for k in range(KD):
                mm = nc.tensor.matmul(psU[:, :], awb[:, k, :], WT[:, k, :], start=(k == 0), stop=(k == KD - 1))
            mm.then_inc(u_done, 1)
            pe.wait_ge(ones_set, 1)
            for n, (a, b) in enumerate(chunks):
                pe.wait_ge(diag_done, b)
                wait(pe, row_copied, n - 1)
                nc.tensor.matmul(psR[:, n % 2, 0:(b - a) * P], ones[:, :],
                                 diag[:, a:b, :].rearrange("p t j -> p (t j)"),
                                 start=True, stop=True).then_inc(row_done, 1)

        @block.scalar
        def _(act):
            act.wait_ge(u_done, 1)
            nc.scalar.copy(U[:, :], psU[:, :]).then_inc(u_copied, 1)
            norm.deviation(act)

            def tile_pair(i):
                for u in range(2):
                    act.wait_ge(h_done, i + u + 1)
                    nc.scalar.activation(H[:, i + u, 0:D], h[u][:, :], ACT.Copy, scale=H_SCALE).then_inc(hi_done, 1)

            pairs(act, tile_pair)
            for n, (a, b) in enumerate(chunks):
                act.wait_ge(row_done, n + 1)
                nc.scalar.copy(S2row[:, a * P:b * P], psR[:, n % 2, 0:(b - a) * P]).then_inc(row_copied, 1)

        @block.vector
        def _(dve):
            nc.vector.memset(ones[:, :], 1.0).then_inc(ones_set, 1)
            for n, (a, b) in enumerate(XG):
                dve.wait_ge(x_in[n], 16)
                for i in range(a, b):
                    nc.vector.bn_stats(t["stats"][:, i, :], X[:, i, :]).then_inc(stats_done, 1)
            dve.wait_ge(stats_done, T)
            norm.finish(dve)
            dve.wait_ge(u_copied, 1)
            dve.wait_ge(w_in, 64)

            def tile_pair(i):
                for u in range(2):
                    wait(dve, s_done, 2 * (i + u) - 2)
                    wait(dve, lo_done, i + u - 1)
                    norm.normalise(h[u][:, :], X[:, i + u, :], i + u).then_inc(h_done, 1)
                for u in range(2):
                    dve.wait_ge(h_done, i + u + 1)
                    wait(dve, s_done, 2 * (i + u) - 2)
                    nc.vector.tensor_tensor_reduce(junk[:, 2 * u, :], h[u][:, :], U[:, 0:D], 1.0, 0.0, ALU.mult,
                                                   ALU.add, s12[u][:, 0:1]).then_inc(s_done, 1)
                    nc.vector.tensor_tensor_reduce(junk[:, 2 * u + 1, :], h[u][:, :], U[:, D:2 * D], 1.0, 0.0, ALU.mult,
                                                   ALU.add, s12[u][:, 1:2]).then_inc(s_done, 1)
                for u in range(2):
                    dve.wait_ge(hi_done, i + u + 1)
                    nc.vector.scalar_tensor_tensor(H[:, i + u, D:2 * D], h[u][:, :], H_SCALE, H[:, i + u, 0:D],
                                                   ALU.mult, ALU.subtract).then_inc(lo_done, 1)
                for u in range(2):
                    dve.wait_ge(s_done, 2 * (i + u + 1))
                    nc.vector.tensor_scalar(S1[:, ds(i + u, 1)], s12[u][:, 0:1], ab[:, 0:1], None,
                                            ALU.add).then_inc(s1_done, 1)
                    nc.vector.tensor_scalar(diag[:, i + u, :], ident[:, :], s12[u][:, 1:2], None,
                                            ALU.mult).then_inc(diag_done, 1)

            pairs(dve, tile_pair)


TG = [(0, 8), (8, 16), (16, 24), (24, T)]
NG = len(TG)


def graph_attention(nc, t, dram):
    with ExitStack() as ctx:
        sb = lambda n, s, d=F32: ctx.enter_context(nc.sbuf_tensor(n, s, d))
        sem = semaphores(nc, ctx)
        X, H, S1, S2row, ident, stats = t["X"], t["H"], t["S1"], t["S2row"], t["ident"], t["stats"]
        stats_done = sem("b_stats")
        adjf = [sb(f"adjf{u}", [P, NP]) for u in range(2)]
        bias = [sb(f"maskbias{u}", [P, NP], BF16) for u in range(2)]
        score = [sb(f"score{u}", [P, NP]) for u in range(2)]
        probs = [sb(f"probs{u}", [P, NP]) for u in range(2)]
        PThi = [sb(f"PThi{u}", [P, NP], F16) for u in range(2)]
        PTlo = [sb(f"PTlo{u}", [P, NP], F16) for u in range(2)]
        fcw = sb("fcw", [P, KD, D])
        fcb = sb("fcb", [P, D])
        big = sb("big", [P, 1])
        rowmax = [sb(f"rowmax{u}", [P, 1]) for u in range(2)]
        shifted = [sb(f"shifted{u}", [P, 1]) for u in range(2)]
        leaky = [sb(f"leaky{u}", [P, 1]) for u in range(2)]
        straight = [sb(f"straight{u}", [P, 1]) for u in range(2)]
        sloped = [sb(f"sloped{u}", [P, 1]) for u in range(2)]
        total = [sb(f"total{u}", [P, 1]) for u in range(2)]
        rtotal = sb("rtotal", [P, T])
        rscale = sb("rscale", [P, T])
        part = sb("part", [P, D])
        agg = [sb(f"agg{u}", [P, D]) for u in range(2)]
        aggT = [sb(f"aggT{u}", [P, KD, P]) for u in range(2)]
        ps = lambda n, s: ctx.enter_context(nc.psum_tensor(n, s, F32))
        psT = [ps(f"psT{u}", [P, 8 * P]) for u in range(2)]
        acc = [ps(f"acc{u}", [P, 2 * D]) for u in range(2)]
        psA = ps("psA", [P, 512])
        psF = ps("psF", [P, 512])
        zero = sb("zero", [P, D])
        zeroed = sem("b_zeroed")
        adj_in = [sem(f"b_adj{u}") for u in range(2)]
        w_in, pad_set, mask_waits = sem("b_w"), sem("b_pad"), sem("b_mask_waits")
        mask_ready, masked_ready, small, shift_ready = sem("b_mask"), sem("b_masked"), sem("b_small"), sem("b_shift")
        straight_ready, sloped_ready = sem("b_straight"), sem("b_sloped")
        probs_ready, turned, hi_ready, lo_ready = (sem("b_probs"), sem("b_turned"),
                                                                sem("b_hi"), sem("b_lo"))
        acc_ready, scale_ready, agg_part, agg_ready = sem("b_acc"), sem("b_scale"), sem("b_part"), sem("b_agg")
        agg_turned, aggT_ready, fc_ready, x_part, x_ready = (sem("b_aggt"), sem("b_aggT"), sem("b_fc"), sem("b_xp"),
                                                             sem("b_x"))
        block = ctx.enter_context(nc.Block())
        adjv = dram["adj"].rearrange("(t p) j -> t p j", p=P)
        slots = dram["slot_rows"].rearrange("(t s p) d -> t p s d", p=P, s=E1)
        FIRST, LAST, TOTAL = 4, T - 4, T + 2

        def live(t):
            return not isinstance(t, int) or 0 <= t < T

        @block.sync
        def _(sp):
            sp.dma_start(fcw[:, :, :], dram["fcw"].rearrange("(k p) n -> p k n", p=P)).then_inc(w_in, 16)
            sp.dma_start(fcb[:, :], dram["fcb"]).then_inc(w_in, 16)

            def load(t, u):
                if live(t):
                    wait(sp, mask_ready, t - 1)
                    sp.dma_start(adjf[u][:, :], adjv[t, :, :]).then_inc(adj_in[u], 16)
                    sp.dma_start(slots[t, :, :, :], zero[:, :].unsqueeze(1).to_broadcast([P, E1, D])
                                 ).then_inc(zeroed, 16)

            sp.wait_ge(pad_set, 4)
            steps(sp, load, FIRST, LAST, T)
            sp.wait_ge(w_in, 32)
            sp.wait_ge(zeroed, 16 * T)

        @block.scalar
        def _(act):
            def hi(t, u, g):
                a, b = TG[g]
                act.wait_ge(turned, NG * t + g + 1)
                if g == 0:
                    wait(act, acc_ready, t - 1)
                nc.scalar.activation(PThi[u][:, a * P:b * P], psT[g % 2][:, 0:(b - a) * P], ACT.Copy,
                                     scale=P_SCALE).then_inc(hi_ready, 1)

            def no_edge(t, u):
                act.wait_ge(adj_in[u], 8 * (t - u) + 16)
                wait(act, masked_ready, t - 1)
                nc.scalar.activation(bias[u][:, 0:N], adjf[u][:, 0:N], ACT.Relu, bias=big[:, :],
                                     scale=-EDGE_SCALE).then_inc(mask_ready, 1)

            def straight_exp(t, u):
                act.wait_ge(shift_ready, 2 * t + 2)
                wait(act, turned, NG * (t - 1))
                nc.scalar.activation(probs[u][:, 0:N], score[u][:, 0:N], ACT.Exp,
                                     bias=straight[u][:, :]).then_inc(straight_ready, 1)

            def sloped_exp(t, u):
                act.wait_ge(straight_ready, t + 1)
                nc.scalar.activation(score[u][:, 0:N], score[u][:, 0:N], ACT.Exp, bias=sloped[u][:, :],
                                     scale=ALPHA).then_inc(sloped_ready, 1)

            def iteration(t, u):
                if live(t):
                    hi(t, u, 0)
                    hi(t, u, 1)
                if live(t + 1):
                    straight_exp(t + 1, 1 - u)
                if live(t - 2):
                    act.wait_ge(agg_turned, t - 1)
                    wait(act, fc_ready, t - 3)
                    nc.scalar.copy(aggT[u][:, :, :].rearrange("p k n -> p (k n)"), psA[:, 0:D]).then_inc(aggT_ready, 1)
                if live(t + 1):
                    sloped_exp(t + 1, 1 - u)
                if live(t):
                    hi(t, u, 2)
                    hi(t, u, 3)
                if live(t + 3):
                    no_edge(t + 3, 1 - u)

            act.wait_ge(pad_set, 4)
            no_edge(0, 0)
            no_edge(1, 1)
            straight_exp(0, 0)
            sloped_exp(0, 0)
            no_edge(2, 0)
            steps(act, iteration, FIRST, LAST, TOTAL)

        @block.vector
        def _(dve):
            nc.vector.memset(big[:, :], FAR).then_inc(pad_set, 1)
            nc.vector.memset(zero[:, :], 0.0).then_inc(pad_set, 1)
            for u in range(2):
                nc.vector.memset(probs[u][:, N:NP], 0.0).then_inc(pad_set, 1)

            def masked(t, u):
                settled(dve, mask_waits, (mask_ready, t + 1), (probs_ready, t - 1))
                nc.vector.tensor_tensor_reduce(score[u][:, 0:N], S2row[:, 0:N], bias[u][:, 0:N], 1.0, -2 * FAR,
                                               ALU.subtract, ALU.max, rowmax[u][:, :]).then_inc(masked_ready, 1)
                dve.wait_ge(masked_ready, t + 1)
                nc.vector.tensor_tensor(shifted[u][:, :], rowmax[u][:, :], S1[:, ds(t, 1)],
                                        ALU.add).then_inc(small, 1)
                dve.wait_ge(small, 2 * t + 1)
                nc.vector.scalar_tensor_tensor(leaky[u][:, :], shifted[u][:, :], ALPHA, shifted[u][:, :],
                                               ALU.mult, ALU.max).then_inc(small, 1)
                dve.wait_ge(small, 2 * t + 2)
                nc.vector.tensor_tensor(straight[u][:, :], S1[:, ds(t, 1)], leaky[u][:, :],
                                        ALU.subtract).then_inc(shift_ready, 1)
                nc.vector.scalar_tensor_tensor(sloped[u][:, :], S1[:, ds(t, 1)], ALPHA, leaky[u][:, :], ALU.mult,
                                               ALU.subtract).then_inc(shift_ready, 1)

            def combine(t, u):
                dve.wait_ge(sloped_ready, t + 1)
                nc.vector.scalar_tensor_tensor(probs[u][:, 0:N], score[u][:, 0:N], 1.0, probs[u][:, 0:N], ALU.mult,
                                               ALU.max, accum_out=total[u][:, :]).then_inc(probs_ready, 1)

            def lo(t, u, g):
                a, b = TG[g]
                dve.wait_ge(hi_ready, NG * t + g + 1)
                nc.vector.scalar_tensor_tensor(PTlo[u][:, a * P:b * P], psT[g % 2][:, 0:(b - a) * P], P_SCALE,
                                               PThi[u][:, a * P:b * P], ALU.mult, ALU.subtract).then_inc(lo_ready, 1)

            def row_scale(t, u):
                dve.wait_ge(probs_ready, t + 1)
                nc.vector.reciprocal(rtotal[:, ds(t, 1)], total[u][:, :]).then_inc(scale_ready, 1)
                dve.wait_ge(scale_ready, 2 * t + 1)
                nc.vector.tensor_scalar(rscale[:, ds(t, 1)], rtotal[:, ds(t, 1)], 1.0 / (H_SCALE * P_SCALE), None,
                                        ALU.mult).then_inc(scale_ready, 1)

            def aggregate(t, u):
                dve.wait_ge(scale_ready, 2 * t + 2)
                dve.wait_ge(acc_ready, t + 1)
                wait(dve, agg_turned, t - 1)
                nc.vector.tensor_scalar(part[:, :], acc[u][:, 0:D], rscale[:, ds(t, 1)], None,
                                        ALU.mult).then_inc(agg_part, 1)
                dve.wait_ge(agg_part, t + 1)
                nc.vector.scalar_tensor_tensor(agg[u][:, :], acc[u][:, D:2 * D], rscale[:, ds(t, 1)], part[:, :],
                                               ALU.mult, ALU.add).then_inc(agg_ready, 1)

            def residual(t, u):
                dve.wait_ge(fc_ready, t + 1)
                nc.vector.tensor_tensor(X[:, t, :], psF[:, 0:D], X[:, t, :], ALU.add).then_inc(x_part, 1)
                dve.wait_ge(x_part, t + 1)
                nc.vector.tensor_tensor(X[:, t, :], X[:, t, :], fcb[:, :], ALU.add).then_inc(x_ready, 1)
                dve.wait_ge(x_ready, t + 1)
                nc.vector.bn_stats(stats[:, t, :], X[:, t, :]).then_inc(stats_done, 1)

            def iteration(t, u):
                if live(t - 2):
                    aggregate(t - 2, u)
                if live(t):
                    lo(t, u, 0)
                    lo(t, u, 1)
                if live(t + 2):
                    masked(t + 2, u)
                if live(t + 1):
                    combine(t + 1, 1 - u)
                    row_scale(t + 1, 1 - u)
                if live(t):
                    lo(t, u, 2)
                    lo(t, u, 3)
                if live(t - 2):
                    residual(t - 2, u)

            masked(0, 0)
            masked(1, 1)
            combine(0, 0)
            row_scale(0, 0)
            dve.wait_ge(w_in, 32)
            steps(dve, iteration, FIRST, LAST, TOTAL)

        @block.tensor
        def _(pe):
            def turn(t, u, g):
                a, b = TG[g]
                if g == 0:
                    pe.wait_ge(probs_ready, t + 1)
                wait(pe, hi_ready, NG * t + g - 1)
                wait(pe, lo_ready, NG * t + g - 1)
                for j in range(a, b):
                    mm = nc.tensor.transpose(psT[g % 2][:, (j - a) * P:(j - a + 1) * P],
                                             probs[u][:, j * P:(j + 1) * P], ident[:, :])
                mm.then_inc(turned, 1)

            def products(t, u, g):
                a, b = TG[g]
                pe.wait_ge(lo_ready, NG * t + g + 1)
                if g == 0:
                    wait(pe, agg_ready, t - 1)
                for j in range(a, b):
                    high = (acc[u][:, :], PThi[u][:, j * P:(j + 1) * P], H[:, j, 0:2 * D])
                    low = (acc[u][:, 0:D], PTlo[u][:, j * P:(j + 1) * P], H[:, j, 0:D])
                    for n, (to, left, right) in enumerate((low, high) if j == T - 1 else (high, low)):
                        mm = nc.tensor.matmul(to, left, right, start=(j == 0 and n == 0), stop=(j == T - 1 and n == 1),
                                              skip_group_check=True)
                if g == NG - 1:
                    mm.then_inc(acc_ready, 1)

            def iteration(t, u):
                if live(t):
                    turn(t, u, 0)
                    turn(t, u, 1)
                if live(t - 1):
                    products(t - 1, 1 - u, 0)
                if live(t - 2):
                    pe.wait_ge(agg_ready, t - 1)
                    wait(pe, aggT_ready, t - 2)
                    for k in range(KD):
                        mm = nc.tensor.transpose(psA[:, k * P:(k + 1) * P], agg[u][:, k * P:(k + 1) * P], ident[:, :])
                    mm.then_inc(agg_turned, 1)
                if live(t):
                    turn(t, u, 2)
                if live(t - 1):
                    products(t - 1, 1 - u, 1)
                if live(t):
                    turn(t, u, 3)
                if live(t - 2):
                    pe.wait_ge(aggT_ready, t - 1)
                    wait(pe, x_part, t - 2)
                    for k in range(KD):
                        mm = nc.tensor.matmul(psF[:, 0:D], aggT[u][:, k, :], fcw[:, k, :], start=(k == 0),
                                              stop=(k == KD - 1))
                    mm.then_inc(fc_ready, 1)
                if live(t - 1):
                    products(t - 1, 1 - u, 2)
                    products(t - 1, 1 - u, 3)

            pe.wait_ge(w_in, 32)
            pe.wait_ge(pad_set, 4)
            steps(pe, iteration, FIRST, LAST, TOTAL)


def normalised_projection(nc, t, name, w_dram, width, out, bias=None, HT=None, H=None, after=None):
    with ExitStack() as ctx:
        make = semaphores(nc, ctx)
        sem = lambda n: make(f"{name}_{n}")
        X, ident = t["X"], t["ident"]
        norm = RowNorm(nc, ctx, make, name + "_ln", t["stats"])
        h = [ctx.enter_context(nc.sbuf_tensor(f"{name}_h{u}", [P, D], F32)) for u in range(2)]
        h_done = sem("h_done")
        W = ctx.enter_context(nc.sbuf_tensor(name + "_W", [P, KD, width], F32))
        hT = [ctx.enter_context(nc.sbuf_tensor(f"{name}_hT{u}", [P, KD, P], F32)) for u in range(2)]
        psT = [ctx.enter_context(nc.psum_tensor(f"{name}_psT{u}", [P, 512], F32)) for u in range(2)]
        psO = [ctx.enter_context(nc.psum_tensor(f"{name}_psO{u}", [P, 512], F32)) for u in range(2)]
        w_in, turned, hT_ready, copied, projected, out_ready = (sem("w"), sem("turned"), sem("hT"), sem("copied"),
                                                                sem("projected"), sem("out"))
        hi_ready, lo_ready, bias_ready = sem("hi"), sem("lo"), sem("bias")
        if bias is not None:
            bias_sb = ctx.enter_context(nc.sbuf_tensor(name + "_bias", [P, 2, width], F32))
        block = ctx.enter_context(nc.Block())
        loads = 1 + len(bias or ())

        @block.sync
        def _(sp):
            sp.dma_start(W[:, :, :], w_dram.rearrange("(k p) n -> p k n", p=P)).then_inc(w_in, 16)
            if bias is not None:
                for n, b in enumerate(bias):
                    sp.dma_start(bias_sb[:, n, :], b).then_inc(w_in, 16)
            if after is not None:
                after(sp)
            sp.wait_ge(w_in, 16 * loads)

        @block.scalar
        def _(act):
            def tile_pair(i):
                for u in range(2):
                    if H is not None:
                        act.wait_ge(h_done, i + u + 1)
                        nc.scalar.activation(H[:, i + u, 0:D], h[u][:, :], ACT.Copy,
                                             scale=H_SCALE).then_inc(hi_ready, 1)
                for u in range(2):
                    act.wait_ge(turned, i + u + 1)
                    wait(act, projected, i + u - 1)
                    nc.scalar.copy(hT[u][:, :, :].rearrange("p k n -> p (k n)"), psT[u][:, 0:D]).then_inc(hT_ready, 1)
                    if HT is not None:
                        nc.scalar.copy(HT[:, :, ds((i + u) * P, P)],
                                       psT[u][:, 0:D].rearrange("p (k n) -> p k n", k=KD)).then_inc(copied, 1)

            norm.deviation(act)
            pairs(act, tile_pair)

        @block.tensor
        def _(pe):
            def tile_pair(i):
                for u in range(2):
                    pe.wait_ge(h_done, i + u + 1)
                    wait(pe, copied if HT is not None else hT_ready, i + u - 1)
                    for k in range(KD):
                        mm = nc.tensor.transpose(psT[u][:, k * P:(k + 1) * P], h[u][:, k * P:(k + 1) * P],
                                                 ident[:, :])
                    mm.then_inc(turned, 1)
                for u in range(2):
                    pe.wait_ge(hT_ready, i + u + 1)
                    wait(pe, out_ready, i + u - 1)
                    for k in range(KD):
                        mm = nc.tensor.matmul(psO[u][:, 0:width], hT[u][:, k, :], W[:, k, :], start=(k == 0),
                                              stop=(k == KD - 1))
                    mm.then_inc(projected, 1)

            pe.wait_ge(w_in, 16 * loads)
            pairs(pe, tile_pair)

        @block.vector
        def _(dve):
            def produce(i):
                for u in range(2):
                    wait(dve, turned, i + u - 1)
                    if H is not None:
                        wait(dve, lo_ready, i + u - 1)
                    norm.normalise(h[u][:, :], X[:, i + u, :], i + u).then_inc(h_done, 1)
                for u in range(2):
                    if H is not None:
                        dve.wait_ge(hi_ready, i + u + 1)
                        nc.vector.scalar_tensor_tensor(H[:, i + u, D + 2:2 * D + 2], h[u][:, :], H_SCALE,
                                                       H[:, i + u, 0:D], ALU.mult, ALU.subtract).then_inc(lo_ready, 1)

            def collect(i):
                for u in range(2):
                    dve.wait_ge(projected, i + u + 1)
                    if bias is not None:
                        nc.vector.tensor_tensor(out[:, i + u, :], psO[u][:, 0:width], bias_sb[:, 0, :],
                                                ALU.add).then_inc(out_ready, 1)
                    else:
                        nc.vector.tensor_copy(out[:, i + u, :], psO[u][:, 0:width]).then_inc(out_ready, 1)

            norm.finish(dve)
            if bias is not None:
                dve.wait_ge(w_in, 16 * loads)
                if len(bias) == 2:
                    nc.vector.tensor_tensor(bias_sb[:, 0, :], bias_sb[:, 0, :], bias_sb[:, 1, :],
                                            ALU.add).then_inc(bias_ready, 1)
                    dve.wait_ge(bias_ready, 1)
            produce(0)
            with dve.Fori(2, T - 1, 2) as i:
                produce(i)
                collect(i - 2)
            collect(T - 2)


def wide(ap, shape):
    return ap.unsqueeze(2).to_broadcast(shape)


class TopTwo:

    def __init__(self, nc, ctx, name, E):
        sb = lambda n, s, d=F32: ctx.enter_context(nc.sbuf_tensor(f"{name}_{n}", s, d))
        self.nc, self.E = nc, E
        self.descending = sb("descending", [P, E])
        self.score = sb("score", [P, T, E])
        self.rest = sb("rest", [P, T, E])
        self.rank = sb("rank", [P, T])
        self.best = [sb(f"best{k}", [P, T]) for k in range(2)]
        self.one_hot = [sb(f"one_hot{k}", [P, T, E]) for k in range(2)]

    def steps(self, step, logits):
        nc, E, v = self.nc, self.E, self.nc.vector
        full = [P, T, E]
        for k in range(2):
            src = logits if k == 0 else self.rest
            step(v.tensor_reduce(self.best[k][:, :], src[:, :, :], AX_X, ALU.max))
            step(v.tensor_tensor(self.score[:, :, :], src[:, :, :], wide(self.best[k][:, :], full), ALU.is_equal))
            step(v.tensor_tensor(self.score[:, :, :], self.score[:, :, :],
                                 self.descending[:, :].unsqueeze(1).to_broadcast(full), ALU.mult))
            step(v.tensor_reduce(self.rank[:, :], self.score[:, :, :], AX_X, ALU.max))
            step(v.tensor_tensor(self.one_hot[k][:, :, :], self.score[:, :, :], wide(self.rank[:, :], full),
                                 ALU.is_equal))
            if k == 0:
                step(v.scalar_tensor_tensor(self.rest[:, :, :], self.one_hot[0][:, :, :], -FAR * FAR,
                                            logits[:, :, :], ALU.mult, ALU.add))


E0 = 64
CAP = 256
F0 = 1024
MF = F0 // P
CH = 256
NCH = NP // CH
RC = 4
E1 = 8
F1 = 512
KF = F1 // P
NS = (2 * NP - E1) // P + E1
SLOT_TILES = E1 * T
W_PEAK = float(2 ** 14)
assert NS * P >= 2 * NP
assert NP % CH == 0 and T * E0 % RC == 0 and T * E0 // RC <= 512


def capacity_ffn(nc, t, dram):
    with ExitStack() as ctx:
        sb = lambda n, s, d=F32: ctx.enter_context(nc.sbuf_tensor(n, s, d))
        sem = semaphores(nc, ctx)
        X, HT, L = t["X"], t["HT"], t["L0"]
        w1 = sb("w1", [P, KD, F0])
        w2 = sb("w2", [P, MF, D])
        b1 = sb("b1", [P, MF])
        b2 = sb("b2", [P, D])
        G = [sb(f"G{u}", [P, MF, CH]) for u in range(2)]
        Y = sb("Y", [P, T, D])
        top = TopTwo(nc, ctx, "r0", E0)
        chosen = sb("chosen", [P, T, E0], F16)
        before = sb("before", [P, T, E0])
        sums = [sb(f"sums{k}", [P, T, E0]) for k in range(2)]
        tri = sb("tri", [P, P], F16)
        ones = sb("ones16", [P, P], F16)
        z, rz, e2, gate, held = (sb(n, [P, T]) for n in ("z", "rz", "e2", "gate", "held"))
        share = [sb(f"share{k}", [P, T]) for k in range(2)]
        ps = lambda n, s: ctx.enter_context(nc.psum_tensor(n, s, F32))
        psH = [ps(f"psH{u}", [P, 512]) for u in range(2)]
        psY = [ps(f"psY{u}", [P, 512]) for u in range(2)]
        psC = ps("psC", [P, RC, 512])
        w_in, r_in = sem("c_w"), sem("c_r")
        hidden, active, y_done, y_copied = sem("c_hidden"), sem("c_active"), sem("c_y"), sem("c_ycp")
        chain, chosen_ready, counted, before_ready, exp_in, exp_out = (sem("c_chain"), sem("c_chosen"), sem("c_counted"),
                                                               sem("c_before"), sem("c_expin"), sem("c_expout"))
        stats_done = sem("c_stats")
        biased, x_ready = sem("c_biased"), sem("c_x")
        stage = [sb(f"stage{u}", [P, KD * 2 * F1]) for u in range(2)]
        parts = [sb(f"parts{u}", [P, KD, 2, 2 * F1], F16) for u in range(2)]
        peak = [sb(f"peak{u}", [P, 1]) for u in range(2)]
        peaks = [sb(f"peaks{u}", [P, P]) for u in range(2)]
        top_peak, guarded, rpeak, w_scale = (sb(n, [P, 1]) for n in ("top_peak", "guarded", "rpeak", "w_scale"))
        stage_in = [sem(f"c_stage{u}") for u in range(2)]
        peak_in = [sem(f"c_peaks{u}") for u in range(2)]
        parts_stored = [sem(f"c_stored{u}") for u in range(2)]
        peak_ready, peak_waits, peak_out, scaled = sem("c_peak"), sem("c_peak_waits"), sem("c_peak_out"), sem("c_scaled")
        parts_hi, parts_ready = sem("c_parts_hi"), sem("c_parts")
        block = ctx.enter_context(nc.Block())
        W = T * E0 // RC

        @block.sync
        def _(sp):
            sp.dma_start(top.descending[:, :], dram["desc0"]).then_inc(r_in, 16)
            sp.dma_start(tri[:, :], dram["tri"]).then_inc(r_in, 16)
            sp.dma_start(ones[:, :], dram["ones"]).then_inc(r_in, 16)
            sp.dma_start(w1[:, :, :], dram["w1T"].rearrange("(k p) n -> p k n", p=P)).then_inc(w_in, 16)
            sp.dma_start(w2[:, :, :], dram["w2T"].rearrange("(k p) n -> p k n", p=P)).then_inc(w_in, 16)
            sp.dma_start(b1[:, :], dram["b1c"]).then_inc(w_in, 16)
            sp.dma_start(b2[:, :], dram["b2"]).then_inc(w_in, 16)

            def weights(e, u):
                if not isinstance(e, int) or e < E1:
                    wait(sp, parts_ready, e - 1)
                    sp.dma_start(stage[u][:, :], dram["eW1"][:, ds(e, 1), :].rearrange("p e n -> p (e n)")
                                 ).then_inc(stage_in[u], 16)
                if not isinstance(e, int) or e > 0:
                    sp.wait_ge(parts_ready, e)
                    sp.dma_start(dram["w1_parts"][:, ds(e - 1, 1), :].rearrange("p e n -> p (e n)"),
                                 parts[1 - u][:, :, :, :].rearrange("p k h n -> p (k h n)")
                                 ).then_inc(parts_stored[1 - u], 16)

            steps(sp, weights, 2, E1, E1 + 1)
            sp.wait_ge(r_in, 48)
            sp.wait_ge(w_in, 64)
            for u in range(2):
                sp.wait_ge(parts_stored[u], 8 * E1)

        @block.gpsimd
        def _(pool):
            def share_peak(e, u):
                settled(pool, peak_waits, (peak_ready, e + 1))
                pool.dma_start(dram["peaks"][ds(e, 1), :].rearrange("e p -> p e"), peak[u][:, :]).then_inc(peak_out, 16)
                settled(pool, peak_waits, (peak_out, 16 * (e + 1)))
                pool.dma_start(peaks[u][:, :], dram["peaks"][ds(e, 1), :].to_broadcast([P, P])).then_inc(peak_in[u], 16)

            steps(pool, share_peak, 2, E1, E1)

        @block.tensor
        def _(pe):
            def hidden_part(c, u, m):
                b = m // 2
                if m % 2 == 0:
                    wait(pe, active, MF * c + m - 2)
                for k in range(KD):
                    mm = nc.tensor.matmul(psH[b % 2][:, (m % 2) * CH:(m % 2 + 1) * CH], w1[:, k, m * P:(m + 1) * P],
                                          HT[:, k, ds(c * CH, CH)], start=(k == 0), stop=(k == KD - 1))
                mm.then_inc(hidden, 1)

            def output_part(c, u, s):
                pe.wait_ge(active, MF * (c + 1))
                wait(pe, y_copied, 2 * c + s - 1)
                for m in range(MF):
                    mm = nc.tensor.matmul(psY[s][:, 0:D], G[u][:, m, s * P:(s + 1) * P], w2[:, m, :],
                                          start=(m == 0), stop=(m == MF - 1))
                mm.then_inc(y_done, 1)

            def iteration(c, u):
                if not isinstance(c, int) or c < NCH:
                    for m in range(MF):
                        hidden_part(c, u, m)
                if not isinstance(c, int) or c > 0:
                    for s in range(2):
                        output_part(c - 1, 1 - u, s)

            pe.wait_ge(w_in, 64)
            iteration(0, 0)
            iteration(1, 1)
            iteration(2, 0)
            iteration(3, 1)
            pe.wait_ge(r_in, 48)
            pe.wait_ge(chosen_ready, 1)
            for stationary in (tri, ones):
                if stationary is ones:
                    pe.wait_ge(before_ready, 1)
                for c in range(RC):
                    flat = chosen[:, :, :].rearrange("p t e -> p (t e)")
                    mm = nc.tensor.matmul(psC[:, c, 0:W], stationary[:, :], flat[:, c * W:(c + 1) * W],
                                          start=True, stop=True)
                mm.then_inc(counted, 1)
            with pe.Fori(4, NCH - 2, 2) as c:
                for u in range(2):
                    iteration(c + u, u)
            for c in range(NCH - 1, NCH + 1):
                iteration(c, c % 2)

        @block.scalar
        def _(act):
            def iteration(c, u):
                for m in range(MF):
                    act.wait_ge(hidden, MF * c + (m // 2 + 1) * 2)
                    if m == 0:
                        wait(act, y_done, 2 * (c - 1))
                    nc.scalar.activation(G[u][:, m, :], psH[m // 2 % 2][:, (m % 2) * CH:(m % 2 + 1) * CH], ACT.Gelu,
                                         bias=b1[:, m:m + 1]).then_inc(active, 1)

            def take(c):
                for s in range(2):
                    act.wait_ge(y_done, 2 * c + s + 1)
                    nc.scalar.copy(Y[:, c * 2 + s, :], psY[s][:, 0:D]).then_inc(y_copied, 1)

            act.wait_ge(exp_in, 1)
            nc.scalar.activation(top.rest[:, :, :], top.rest[:, :, :], ACT.Exp).then_inc(exp_out, 1)
            act.wait_ge(exp_in, 2)
            nc.scalar.activation(e2[:, :], held[:, :], ACT.Exp).then_inc(exp_out, 1)
            act.wait_ge(w_in, 64)
            iteration(0, 0)
            iteration(1, 1)
            take(0)
            with act.Fori(2, NCH - 2, 2) as c:
                for u in range(2):
                    iteration(c + u, u)
                    take(c + u - 1)
            iteration(NCH - 1, (NCH - 1) % 2)
            take(NCH - 2)
            take(NCH - 1)

        @block.vector
        def _(dve):
            v = nc.vector
            step = Chain(dve, chain)
            full = [P, T, E0]
            dve.wait_ge(r_in, 48)
            top.steps(step, L)
            step(v.tensor_tensor(top.score[:, :, :], top.one_hot[0][:, :, :], top.one_hot[1][:, :, :], ALU.add))
            v.tensor_copy(chosen[:, :, :], top.score[:, :, :]).then_inc(chosen_ready, 1)
            v.tensor_tensor(top.rest[:, :, :], L[:, :, :], wide(top.best[0][:, :], full),
                            ALU.subtract).then_inc(exp_in, 1)
            v.tensor_tensor(held[:, :], top.best[1][:, :], top.best[0][:, :], ALU.subtract).then_inc(exp_in, 1)
            dve.wait_ge(exp_out, 2)
            step(v.tensor_reduce(z[:, :], top.rest[:, :, :], AX_X, ALU.add))
            step(v.reciprocal(share[0][:, :], z[:, :]))
            step(v.tensor_tensor(share[1][:, :], e2[:, :], share[0][:, :], ALU.mult))
            def peak_of(e, u):
                dve.wait_ge(stage_in[u], 8 * (e - u) + 16)
                v.tensor_reduce(peak[u][:, :], stage[u][:, :], AX_X, ALU.max,
                                apply_absolute_value=True).then_inc(peak_ready, 1)

            def split(e, u):
                dve.wait_ge(peak_in[u], 8 * (e - u) + 16)
                v.tensor_reduce(top_peak[:, :], peaks[u][:, :], AX_X, ALU.max).then_inc(scaled, 1)
                dve.wait_ge(scaled, 5 * e + 1)
                v.tensor_scalar(guarded[:, :], top_peak[:, :], 1e-30, None, ALU.max).then_inc(scaled, 1)
                dve.wait_ge(scaled, 5 * e + 2)
                v.tensor_scalar(t["w_unscale"][:, ds(e, 1)], guarded[:, :], 1.0 / (W_PEAK * H_SCALE), None,
                                ALU.mult).then_inc(scaled, 1)
                v.reciprocal(rpeak[:, :], guarded[:, :]).then_inc(scaled, 1)
                dve.wait_ge(scaled, 5 * e + 4)
                v.tensor_scalar(w_scale[:, :], rpeak[:, :], W_PEAK, None, ALU.mult).then_inc(scaled, 1)
                dve.wait_ge(scaled, 5 * e + 5)
                if not isinstance(e, int) or e > 1:
                    dve.wait_ge(parts_stored[u], 8 * (e - 2 - u) + 16)
                rows = stage[u][:, :].rearrange("p (k n) -> p k n", k=KD)
                v.tensor_scalar(parts[u][:, :, 0, :], rows, w_scale[:, :], None, ALU.mult).then_inc(parts_hi, 1)
                dve.wait_ge(parts_hi, e + 1)
                v.scalar_tensor_tensor(parts[u][:, :, 1, :], rows, w_scale[:, :], parts[u][:, :, 0, :], ALU.mult,
                                       ALU.subtract).then_inc(parts_ready, 1)

            def weights(e, u):
                if not isinstance(e, int) or e > 0:
                    split(e - 1, 1 - u)
                if not isinstance(e, int) or e < E1:
                    peak_of(e, u)

            for e in range(4):
                weights(e, e % 2)
            dve.wait_ge(counted, 1)
            flat = lambda x: x[:, :, :].rearrange("p t e -> p (t e)").rearrange("p (c w) -> p c w", c=RC)
            v.tensor_copy(flat(before), psC[:, :, 0:W]).then_inc(before_ready, 1)
            dve.wait_ge(counted, 2)
            step(v.tensor_copy(flat(sums[0]), psC[:, :, 0:W]))
            a, b, reach = sums[0], sums[1], 1
            while reach < T:
                step(v.tensor_copy(b[:, 0:reach, :], a[:, 0:reach, :]))
                step(v.tensor_tensor(b[:, reach:T, :], a[:, reach:T, :], a[:, 0:T - reach, :], ALU.add))
                a, b, reach = b, a, 2 * reach
            step(v.tensor_tensor(before[:, 1:T, :], before[:, 1:T, :], a[:, 0:T - 1, :], ALU.add))
            for k in range(2):
                step(v.tensor_tensor(top.score[:, :, :], before[:, :, :], top.one_hot[k][:, :, :], ALU.mult))
                step(v.tensor_reduce(held[:, :], top.score[:, :, :], AX_X, ALU.add))
                step(v.scalar_tensor_tensor(share[k][:, :], held[:, :], float(CAP), share[k][:, :], ALU.is_lt,
                                            ALU.mult))
            step(v.tensor_tensor(gate[:, :], share[0][:, :], share[1][:, :], ALU.add))


            def residual(i):
                dve.wait_ge(y_copied, i + 1)
                v.tensor_tensor(Y[:, i, :], Y[:, i, :], b2[:, :], ALU.add).then_inc(biased, 1)
                dve.wait_ge(biased, i + 1)
                v.scalar_tensor_tensor(X[:, i, :], Y[:, i, :], gate[:, ds(i, 1)], X[:, i, :], ALU.mult,
                                       ALU.add).then_inc(x_ready, 1)
                dve.wait_ge(x_ready, i + 1)
                v.bn_stats(t["stats"][:, i, :], X[:, i, :]).then_inc(stats_done, 1)

            dve.wait_ge(w_in, 64)
            RES = 3
            with dve.Fori(4, E1 - 1, 2) as e:
                for u in range(2):
                    weights(e + u, u)
                    for n in range(RES):
                        residual((e + u - 4) * RES + n)
            weights(E1, E1 % 2)
            with dve.Fori((E1 - 4) * RES, T) as i:
                residual(i)




def tile_pairs(eng, body, first, last, total):
    for t in range(0, first, 2):
        body(t)
    with eng.Fori(first, last - 1, 2) as t:
        body(t)
    for t in range(last, total, 2):
        body(t)


def mean_aggregation(nc, t, dram):
    with ExitStack() as ctx:
        sb = lambda n, s, d=F32: ctx.enter_context(nc.sbuf_tensor(n, s, d))
        sem = semaphores(nc, ctx)
        X, H, own, ident = t["X"], t["H"], t["own"], t["ident"]
        stats_done = sem("d_stats")
        adjf = t["adjTf"]
        adjh = [sb(f"adjTh{u}", [P, NP], F16) for u in range(2)]
        Wn = sb("Wn", [P, KD, D])
        degree = [sb(f"degree{u}", [P, 1]) for u in range(2)]
        rdegree = [sb(f"rdegree{u}", [P, 1]) for u in range(2)]
        agg = [sb(f"mean{u}", [P, D]) for u in range(2)]
        aggT = [sb(f"meanT{u}", [P, KD, P]) for u in range(2)]
        out = [sb(f"summed{u}", [P, D]) for u in range(2)]
        one_hot, best, slot_f, running = t["one_hot"], t["best"], t["slot_f"], t["running"]
        row_stats = [sb(f"row_stats{u}", [P, 6]) for u in range(2)]
        moments = sb("moments", [P, 2, 2])
        eps, std = sb("eps", [P, 1]), sb("std", [P, 2])
        mean, rstd = sb("mean_all", [P, T]), sb("rstd_all", [P, T])
        h = [sb(f"h_r{u}", [P, D]) for u in range(2)]
        hT = sb("hT_r", [P, 2, KD, P])
        rows = [sb(f"rows{u}", [P, D]) for u in range(2)]
        Wg, bg = sb("Wg", [P, KD, E1]), sb("bg", [P, 2, E1])
        descending, region = sb("descending", [P, 2, E1]), sb("region", [P, 2, E1])
        logits, score, rest, place = (sb(n, [P, 2, E1]) for n in ("logits", "score", "rest", "place"))
        rank = sb("rank", [P, 2])
        placed = sb("placed", [P, 2, 2, E1])
        chosen = sb("chosen1", [P, 2, E1], F16)
        tri, ones = sb("tri1", [P, P], F16), t["ones"]
        slot_i = sb("slot_i", [P, 2, 2], I32)
        ps = lambda n: ctx.enter_context(nc.psum_tensor(n, [P, 512], F32))
        acc = [ps(f"sum{u}") for u in range(2)]
        psA = [ps(f"psM{u}") for u in range(2)]
        psF = [ps(f"psN{u}") for u in range(2)]
        psH, psR = ps("psH_r"), ps("psR_r")
        adj_in, W1_in = t["adj_in"], t["W1_in"]
        w_in, half_ready, ones_set = sem("d_w"), sem("d_half"), sem("d_ones")
        acc_ready, deg_ready, rdeg_ready, agg_ready = sem("d_acc"), sem("d_deg"), sem("d_rdeg"), sem("d_agg")
        turned, aggT_ready, proj_ready, out_ready, x_ready = (sem("d_turned"), sem("d_aggT"), sem("d_proj"),
                                                              sem("d_out"), sem("d_x"))
        moment_waits, moments_ready, std_ready, rstd_ready = (sem("d_moment_waits"), sem("d_moments"), sem("d_std"),
                                                              sem("d_rstd"))
        h_ready, h_turned, hT_ready, logits_done = sem("d_h"), sem("d_h_turned"), sem("d_hT"), sem("d_logits")
        logits_taken, chain, chosen_ready, counted = (sem("d_taken"), sem("d_chain"), sem("d_chosen"), sem("d_counted"))
        placed_ready = sem("d_placed")
        counts_taken, rows_ready, scatter_waits, scattered = (sem("d_counts_taken"), sem("d_rows"),
                                                              sem("d_scatter_waits"), sem("d_scattered"))
        block = ctx.enter_context(nc.Block())
        adjv = dram["adjT"]
        FIRST, LAST, TOTAL = 6, T, T + 6

        def live(t):
            return not isinstance(t, int) or 0 <= t < T

        @block.sync
        def _(sp):
            sp.dma_start(Wn[:, :, :], dram["WnT"].rearrange("(k p) n -> p k n", p=P)).then_inc(w_in, 16)
            sp.dma_start(Wg[:, :, :], dram["Wg"].rearrange("(k p) n -> p k n", p=P)).then_inc(w_in, 16)
            for to, name in ((bg, "bg"), (descending, "desc1"), (region, "region"), (tri, "tri"), (ones, "ones")):
                sp.dma_start(to[...], dram[name]).then_inc(w_in, 16)

            def load_pair(i, with_weights):
                for u in range(2):
                    if not (isinstance(i, int) and i + u < 2):
                        wait(sp, half_ready, i + u - 1)
                        sp.dma_start(adjf[u][:, :], adjv[i + u, :, :]).then_inc(adj_in[u], 16)
                if with_weights:
                    flat = t["W1"][:, :, :, :, :].rearrange("p e k h n -> p (e k h n)")
                    part = KD * 2 * 2 * F1
                    sp.dma_start(flat[:, ds(i * (part // 2), part)],
                                 dram["w1_parts"].rearrange("p e n -> p (e n)")[:, ds(i * (part // 2), part)]
                                 ).then_inc(W1_in, 16)

            load_pair(0, True)
            with sp.Fori(2, 2 * E1 - 1, 2) as i:
                load_pair(i, True)
            with sp.Fori(2 * E1, T - 1, 2) as i:
                load_pair(i, False)
            sp.wait_ge(w_in, 16 * 7)
            sp.wait_ge(W1_in, 16 * E1)

        @block.scalar
        def _(act):
            def half(t, u):
                act.wait_ge(adj_in[u], 8 * (t - u) + 16)
                wait(act, acc_ready, t - 1)
                nc.scalar.copy(adjh[u][:, :], adjf[u][:, :]).then_inc(half_ready, 1)

            def mean_back(t, u):
                act.wait_ge(turned, t + 1)
                wait(act, proj_ready, t - 1)
                nc.scalar.copy(aggT[u][:, :, :].rearrange("p k n -> p (k n)"), psA[u][:, 0:D]).then_inc(aggT_ready, 1)

            def body(i):
                if live(i):
                    half(i, 0)
                if live(i - 2):
                    mean_back(i - 2, 0)
                if live(i - 4):
                    act.wait_ge(moments_ready, i - 2)
                    nc.scalar.activation(std[:, :], moments[:, :, 1], ACT.Sqrt, bias=eps[:, :]).then_inc(std_ready, 2)
                if live(i):
                    half(i + 1, 1)
                if live(i - 2):
                    mean_back(i - 1, 1)
                if live(i - 4):
                    act.wait_ge(h_turned, i - 2)
                    wait(act, logits_done, i - 4)
                    nc.scalar.copy(hT[:, :, :, :].rearrange("p u k n -> p (u k n)"), psH[:, :]).then_inc(hT_ready, 2)

            act.wait_ge(ones_set, 1)
            tile_pairs(act, body, FIRST, LAST, TOTAL)

        @block.tensor
        def _(pe):
            def products(t, u):
                pe.wait_ge(half_ready, t + 1)
                wait(pe, agg_ready, t - 1)
                for j in range(T):
                    left = adjh[u][:, j * P:(j + 1) * P]
                    nc.tensor.matmul(acc[u][:, 0:D + 1], left, H[:, j, 0:D + 1], start=(j == 0), stop=False,
                                     skip_group_check=True)
                    mm = nc.tensor.matmul(acc[u][:, 0:D], left, H[:, j, D + 2:2 * D + 2], start=False, stop=(j == T - 1),
                                          skip_group_check=True)
                mm.then_inc(acc_ready, 1)

            def turn_mean(t, u):
                pe.wait_ge(agg_ready, t + 1)
                wait(pe, aggT_ready, t - 1)
                for k in range(KD):
                    mm = nc.tensor.transpose(psA[u][:, k * P:(k + 1) * P], agg[u][:, k * P:(k + 1) * P], ident[:, :])
                mm.then_inc(turned, 1)

            def project(t, u):
                pe.wait_ge(aggT_ready, t + 1)
                wait(pe, out_ready, t - 1)
                for k in range(KD):
                    mm = nc.tensor.matmul(psF[u][:, 0:D], aggT[u][:, k, :], Wn[:, k, :], start=(k == 0),
                                          stop=(k == KD - 1))
                mm.then_inc(proj_ready, 1)

            def turn_rows(i):
                pe.wait_ge(h_ready, i + 2)
                wait(pe, hT_ready, i)
                for u in range(2):
                    for k in range(KD):
                        mm = nc.tensor.transpose(psH[:, (u * KD + k) * P:(u * KD + k + 1) * P],
                                                 h[u][:, k * P:(k + 1) * P], ident[:, :])
                mm.then_inc(h_turned, 2)

            def route(i):
                pe.wait_ge(hT_ready, i + 2)
                wait(pe, logits_taken, i)
                wait(pe, counts_taken, i - 2)
                for u in range(2):
                    for k in range(KD):
                        mm = nc.tensor.matmul(psR[:, u * E1:(u + 1) * E1], hT[:, u, k, :], Wg[:, k, :], start=(k == 0),
                                              stop=(k == KD - 1))
                mm.then_inc(logits_done, 2)

            def count(i):
                pe.wait_ge(chosen_ready, i + 2)
                for u in range(2):
                    terms = [(tri, chosen[:, u, :]), (ones, running[:, :])] + [(ones, chosen[:, 0, :])] * u
                    for n, (left, right) in enumerate(terms):
                        mm = nc.tensor.matmul(psR[:, (2 + u) * E1:(3 + u) * E1], left[:, :], right, start=(n == 0),
                                              stop=(n == len(terms) - 1))
                mm.then_inc(counted, 2)

            def body(i):
                if live(i):
                    products(i, 0)
                if live(i - 2):
                    turn_mean(i - 1, 1)
                    project(i - 2, 0)
                if live(i - 4):
                    turn_rows(i - 4)
                if live(i):
                    products(i + 1, 1)
                    turn_mean(i, 0)
                if live(i - 2):
                    project(i - 1, 1)
                if live(i - 4):
                    route(i - 4)
                if live(i - 6):
                    count(i - 6)

            pe.wait_ge(w_in, 16 * 7)
            pe.wait_ge(ones_set, 3)
            tile_pairs(pe, body, FIRST, LAST, TOTAL)

        @block.vector
        def _(dve):
            v = nc.vector
            v.memset(eps[:, :], EPS).then_inc(ones_set, 1)
            v.memset(H[:, :, D:D + 1], 1.0).then_inc(ones_set, 1)
            v.memset(running[:, :], 0.0).then_inc(ones_set, 1)
            dve.wait_ge(w_in, 16 * 7)

            def aggregate(t, u):
                dve.wait_ge(acc_ready, t + 1)
                v.tensor_scalar(degree[u][:, :], acc[u][:, D:D + 1], EPS, None, ALU.add).then_inc(deg_ready, 1)
                dve.wait_ge(deg_ready, t + 1)
                v.reciprocal(rdegree[u][:, :], degree[u][:, :]).then_inc(rdeg_ready, 1)
                dve.wait_ge(rdeg_ready, t + 1)
                wait(dve, turned, t - 1)
                v.tensor_scalar(agg[u][:, :], acc[u][:, 0:D], rdegree[u][:, :], 1.0 / H_SCALE, ALU.mult,
                                ALU.mult).then_inc(agg_ready, 1)

            def residual(t, u):
                dve.wait_ge(proj_ready, t + 1)
                wait(dve, x_ready, t - 1)
                v.tensor_tensor(out[u][:, :], psF[u][:, 0:D], own[:, t, :], ALU.add).then_inc(out_ready, 1)
                dve.wait_ge(out_ready, t + 1)
                v.scalar_tensor_tensor(X[:, t, :], out[u][:, :], 0.0, X[:, t, :], ALU.max, ALU.add).then_inc(x_ready, 1)

            def normalise(to, t):
                return v.tensor_scalar(to[:, :], X[:, t, :], mean[:, ds(t, 1)], rstd[:, ds(t, 1)], ALU.subtract,
                                       ALU.mult)

            def row_norm(i):
                for u in range(2):
                    settled(dve, moment_waits, (x_ready, i + u + 1), (moments_ready, i))
                    v.bn_stats(row_stats[u][:, :], X[:, i + u, :]).then_inc(stats_done, 1)
                for u in range(2):
                    settled(dve, moment_waits, (stats_done, i + u + 1), (rstd_ready, 2 * i))
                    v.bn_aggr(moments[:, u, :], row_stats[u][:, :]).then_inc(moments_ready, 1)
                dve.wait_ge(moments_ready, i + 2)
                v.tensor_copy(mean[:, ds(i, 2)], moments[:, :, 0]).then_inc(rstd_ready, 2)
                dve.wait_ge(std_ready, i + 2)
                v.reciprocal(rstd[:, ds(i, 2)], std[:, :]).then_inc(rstd_ready, 2)
                dve.wait_ge(rstd_ready, 2 * i + 4)
                wait(dve, h_turned, i)
                for u in range(2):
                    normalise(h[u], i + u).then_inc(h_ready, 1)

            STEPS = 10

            def two_best(i):
                at = i * (STEPS // 2)
                done = [0]

                def step(instruction):
                    done[0] += 1
                    instruction.then_inc(chain, 1)
                    dve.wait_ge(chain, at + done[0])

                pair = [P, 2, E1]
                dve.wait_ge(logits_done, i + 2)
                v.tensor_tensor(logits[:, :, :].rearrange("p u e -> p (u e)"), psR[:, 0:2 * E1],
                                bg[:, :, :].rearrange("p u e -> p (u e)"), ALU.add).then_inc(logits_taken, 2)
                dve.wait_ge(logits_taken, i + 2)
                for k in range(2):
                    src = (logits, rest)[k]
                    largest, hot = best[:, k, ds(i, 2)], one_hot[:, k, ds(i, 2), :]
                    step(v.tensor_reduce(largest, src[:, :, :], AX_X, ALU.max))
                    step(v.tensor_tensor(score[:, :, :], src[:, :, :], wide(largest, pair), ALU.is_equal))
                    step(v.tensor_tensor(score[:, :, :], score[:, :, :], descending[:, :, :], ALU.mult))
                    step(v.tensor_reduce(rank[:, :], score[:, :, :], AX_X, ALU.max))
                    if k == 0:
                        step(v.tensor_tensor(hot, score[:, :, :], wide(rank[:, :], pair), ALU.is_equal))
                        v.scalar_tensor_tensor(rest[:, :, :], hot, -FAR * FAR, logits[:, :, :], ALU.mult,
                                               ALU.add).then_inc(chain, 1)
                        dve.wait_ge(chain, at + 6)
                        done[0] = 6
                    else:
                        v.tensor_tensor(hot, score[:, :, :], wide(rank[:, :], pair), ALU.is_equal).then_inc(chosen_ready, 1)
                dve.wait_ge(chosen_ready, i + 1)
                wait(dve, counts_taken, i)
                v.tensor_tensor(chosen[:, :, :], one_hot[:, 0, ds(i, 2), :], one_hot[:, 1, ds(i, 2), :],
                                ALU.add).then_inc(chosen_ready, 1)

            def write_slots(i):
                wait(dve, scattered, 32 * i)
                for u in range(2):
                    normalise(rows[u], i + u).then_inc(rows_ready, 1)
                dve.wait_ge(counted, i + 2)
                v.tensor_tensor(place[:, :, :].rearrange("p u e -> p (u e)"), psR[:, 2 * E1:4 * E1],
                                region[:, :, :].rearrange("p u e -> p (u e)"), ALU.add).then_inc(placed_ready, 1)
                v.tensor_tensor(running[:, :], running[:, :], chosen[:, 0, :], ALU.add).then_inc(placed_ready, 1)
                dve.wait_ge(placed_ready, 3 * i + 2)
                v.tensor_tensor(running[:, :], running[:, :], chosen[:, 1, :], ALU.add).then_inc(counts_taken, 2)
                for k in range(2):
                    v.tensor_tensor(placed[:, k, :, :], place[:, :, :], one_hot[:, k, ds(i, 2), :],
                                    ALU.mult).then_inc(placed_ready, 1)
                dve.wait_ge(placed_ready, 3 * i + 4)
                for k in range(2):
                    v.tensor_reduce(slot_f[:, k, ds(i, 2)], placed[:, k, :, :], AX_X, ALU.add).then_inc(placed_ready, 1)
                dve.wait_ge(placed_ready, 3 * i + 6)
                v.tensor_copy(slot_i[:, :, :], slot_f[:, :, ds(i, 2)]).then_inc(rows_ready, 2)

            def body(i):
                if live(i):
                    aggregate(i, 0)
                if live(i - 2):
                    residual(i - 2, 0)
                if live(i - 6):
                    two_best(i - 6)
                if live(i):
                    aggregate(i + 1, 1)
                if live(i - 2):
                    residual(i - 1, 1)
                    row_norm(i - 2)
                if live(i - 6):
                    write_slots(i - 6)

            tile_pairs(dve, body, FIRST, LAST, TOTAL)

        @block.gpsimd
        def _(pool):
            def body(i):
                settled(pool, scatter_waits, (rows_ready, 2 * i + 4))
                for k in range(2):
                    for u in range(2):
                        pool.indirect_dma_start(out=dram["slot_rows"], in_=rows[u][:, :], in_offset=None,
                                                out_offset=bass.IndirectOffsetOnAxis(ap=slot_i[:, k, u:u + 1], axis=0)
                                                ).then_inc(scattered, 16)

            body(0)
            with pool.Fori(2, T - 1, 2) as i:
                body(i)
            pool.wait_ge(scattered, 16 * 2 * T)


def expert_ffn(nc, t, dram):
    with ExitStack() as ctx:
        sb = lambda n, s, d=F32: ctx.enter_context(nc.sbuf_tensor(n, s, d))
        sem = semaphores(nc, ctx)
        W1, ident, ones = t["W1"], t["ident"], t["ones"]
        W2 = sb("W2", [P, E1, KF, D])
        one_hot, best, slot_f, slots, share = t["one_hot"], t["best"], t["slot_f"], t["slots"], t["share"]
        expert, source = sb("expert", [P, NS], I32), sb("source", [P, NS], I32)
        limits, over = sb("limits", [P, E1, T]), sb("over", [P, E1, T])
        tile_no, passed = sb("tile_no", [P, NS, E1]), sb("passed", [P, NS, E1])
        tile_f, expert_f, shift = (sb(n, [P, NS]) for n in ("tile_f", "expert_f", "shift"))
        totals, tiles, move, base = (sb(n, [P, E1]) for n in ("totals", "tiles", "move", "base"))
        ends = [sb(f"ends{k}", [P, E1]) for k in range(2)]
        region = sb("region_e", [P, E1])
        moved = sb("moved", [P, T, E1])
        offset = sb("offset", [P, T])
        gap, grown, denominator = sb("gap", [P, T]), sb("odds", [P, T]), sb("denominator", [P, T])
        b1 = sb("eb1", [P, E1, 2 * F1])
        b2 = sb("eb2", [P, E1, D])
        xs = [sb(f"xs{u}", [P, D]) for u in range(2)]
        xT_hi = [sb(f"xT_hi{u}", [P, KD, P], F16) for u in range(2)]
        xT_lo = [sb(f"xT_lo{u}", [P, KD, P], F16) for u in range(2)]
        hb = [sb(f"hb{u}", [P, 2 * F1]) for u in range(2)]
        silu = [sb(f"silu{u}", [P, F1]) for u in range(2)]
        act_sb = [sb(f"act{u}", [P, F1]) for u in range(2)]
        actT = [sb(f"actT{u}", [P, KF, P]) for u in range(2)]
        ys = [sb(f"ys{u}", [P, D]) for u in range(2)]
        ps = lambda n, w: ctx.enter_context(nc.psum_tensor(n, [P, w], F32))
        psH = [ps(f"ePsH{u}", 2 * F1) for u in range(2)]
        psX, psA = ps("ePsX", 512), ps("ePsA", 512)
        psY = [ps(f"ePsY{u}", 512) for u in range(2)]
        b_in = sem("f_b")
        x_in = [sem(f"f_x{u}") for u in range(2)]
        stored = [sem(f"f_stored{u}") for u in range(2)]
        lo_ready = sem("f_lo")
        x_turned, hi_ready, h_ready, hb_ready, silu_ready, act_ready = (sem("f_xt"), sem("f_xT"), sem("f_h"), sem("f_hb"),
                                                                        sem("f_silu"), sem("f_act"))
        a_turned, actT_ready, y_ready, ys_ready = sem("f_at"), sem("f_aT"), sem("f_y"), sem("f_ys")
        c_in, chain, total_ready, tables_ready = sem("f_in"), sem("f_chain"), sem("f_total"), sem("f_tables")
        gap_ready, grown_ready, W2_in, store_waits = (sem("f_gap"), sem("f_grown"), sem("f_W2"), sem("f_store_waits"))
        block = ctx.enter_context(nc.Block())
        src = dram["slot_rows"].rearrange("(s p) d -> s p d", p=P)
        dst = dram["slot_out"].rearrange("(s p) d -> s p d", p=P)
        FIRST, LAST, TOTAL = 4, NS - 3 + (NS - 1) % 2, NS + 3

        def live(s):
            return not isinstance(s, int) or 0 <= s < NS

        def tile_expert(eng, s):
            return eng.value_load(expert[0:1, ds(s, 1)], min_val=0, max_val=E1 - 1)

        @block.sync
        def _(sp):
            for to, name in ((limits, "limits"), (tile_no, "tile_no"), (region, "region_e"), (tile_f, "tile_f")):
                sp.dma_start(to[...], dram[name]).then_inc(c_in, 16)
            sp.dma_start(b1[:, :, :], dram["eb1"]).then_inc(b_in, 16)
            sp.dma_start(W2[:, :, :, :], dram["eW2"]).then_inc(W2_in, 16)
            sp.dma_start(b2[:, :, :], dram["eb2"]).then_inc(b_in, 16)
            sp.wait_ge(tables_ready, 2)

            def load(s, u):
                row_tile = sp.value_load(source[0:1, ds(s, 1)], min_val=0, max_val=SLOT_TILES - 1)
                wait(sp, x_turned, s - 1)
                sp.dma_start(xs[u][:, :], src[ds(row_tile, 1), :, :].rearrange("s p d -> p (s d)")
                             ).then_inc(x_in[u], 16)

            steps(sp, load, 2, NS - 1, NS)
            sp.wait_ge(b_in, 32)
            sp.wait_ge(c_in, 64)
            sp.wait_ge(W2_in, 16)

        @block.gpsimd
        def _(pool):
            def store(s, u):
                settled(pool, store_waits, (ys_ready, s + 1))
                pool.dma_start(dst[s, :, :], ys[u][:, :]).then_inc(stored[u], 16)

            steps(pool, store, 2, NS - 1, NS)
            for u in range(2):
                pool.wait_ge(stored[u], 16 * ((NS + 1 - u) // 2))

        @block.tensor
        def _(pe):
            def turn_rows(s, u):
                pe.wait_ge(x_in[u], 8 * (s - u) + 16)
                wait(pe, lo_ready, s)
                for k in range(KD):
                    mm = nc.tensor.transpose(psX[:, k * P:(k + 1) * P], xs[u][:, k * P:(k + 1) * P], ident[:, :])
                mm.then_inc(x_turned, 1)

            def iteration(s, u):
                if live(s):
                    e = tile_expert(pe, s)
                    pe.wait_ge(lo_ready, s + 1)
                    wait(pe, hb_ready, s - 1)
                    terms = [(left, k, part) for left, part in ((xT_hi, 0), (xT_hi, 1), (xT_lo, 0)) for k in range(KD)]
                    for n in range(2):
                        for m, (left, k, part) in enumerate(terms):
                            mm = nc.tensor.matmul(psH[u][:, n * F1:(n + 1) * F1], left[u][:, k, :],
                                                  W1[:, e, k, part, n * F1:(n + 1) * F1], start=(m == 0),
                                                  stop=(m == len(terms) - 1))
                    mm.then_inc(h_ready, 1)
                if live(s + 1):
                    turn_rows(s + 1, 1 - u)
                if live(s - 1):
                    pe.wait_ge(act_ready, s)
                    wait(pe, actT_ready, s - 1)
                    for k in range(KF):
                        mm = nc.tensor.transpose(psA[:, k * P:(k + 1) * P], act_sb[1 - u][:, k * P:(k + 1) * P],
                                                 ident[:, :])
                    mm.then_inc(a_turned, 1)
                if live(s - 2):
                    e = tile_expert(pe, s - 2)
                    if isinstance(s, int) and s == 2:
                        pe.wait_ge(W2_in, 16)
                    pe.wait_ge(actT_ready, s - 1)
                    wait(pe, ys_ready, s - 3)
                    for k in range(KF):
                        mm = nc.tensor.matmul(psY[u][:, 0:D], actT[u][:, k, :], W2[:, e, k, :], start=(k == 0),
                                              stop=(k == KF - 1))
                    mm.then_inc(y_ready, 1)

            nc.tensor.matmul(psY[0][:, 0:E1], ones[:, :], t["running"][:, :], start=True,
                             stop=True).then_inc(total_ready, 1)
            pe.wait_ge(tables_ready, 2)
            turn_rows(0, 0)
            steps(pe, iteration, FIRST, LAST, TOTAL)

        @block.scalar
        def _(act):
            def rows_back(s, u):
                act.wait_ge(x_turned, s + 1)
                wait(act, h_ready, s - 1)
                nc.scalar.activation(xT_hi[u][:, :, :].rearrange("p k n -> p (k n)"), psX[:, 0:D], ACT.Copy,
                                     scale=H_SCALE).then_inc(hi_ready, 1)

            def iteration(s, u):
                if live(s + 1):
                    rows_back(s + 1, 1 - u)
                if live(s - 1):
                    act.wait_ge(a_turned, s)
                    wait(act, y_ready, s - 3)
                    nc.scalar.copy(actT[1 - u][:, :, :].rearrange("p k n -> p (k n)"), psA[:, :]).then_inc(actT_ready, 1)
                if live(s):
                    act.wait_ge(hb_ready, s + 1)
                    wait(act, act_ready, s - 1)
                    nc.scalar.activation(silu[u][:, :], hb[u][:, 0:F1], ACT.Silu).then_inc(silu_ready, 1)

            act.wait_ge(gap_ready, 1)
            nc.scalar.activation(grown[:, :], gap[:, :], ACT.Exp).then_inc(grown_ready, 1)
            rows_back(0, 0)
            steps(act, iteration, FIRST, LAST, TOTAL)

        @block.vector
        def _(dve):
            v = nc.vector

            def rows_lo(s, u):
                dve.wait_ge(hi_ready, s + 1)
                wait(dve, h_ready, s - 1)
                v.scalar_tensor_tensor(xT_lo[u][:, :, :].rearrange("p k n -> p (k n)"), psX[:, 0:D], H_SCALE,
                                       xT_hi[u][:, :, :].rearrange("p k n -> p (k n)"), ALU.mult,
                                       ALU.subtract).then_inc(lo_ready, 1)

            def iteration(s, u):
                if live(s):
                    e = tile_expert(dve, s)
                    dve.wait_ge(h_ready, s + 1)
                    wait(dve, act_ready, s - 1)
                    v.scalar_tensor_tensor(hb[u][:, :], psH[u][:, :], t["w_unscale"][:, ds(e, 1)], b1[:, e, :], ALU.mult,
                                           ALU.add).then_inc(hb_ready, 1)
                if live(s + 1):
                    rows_lo(s + 1, 1 - u)
                if live(s):
                    dve.wait_ge(silu_ready, s + 1)
                    wait(dve, a_turned, s - 1)
                    v.tensor_tensor(act_sb[u][:, :], silu[u][:, :], hb[u][:, F1:2 * F1], ALU.mult).then_inc(act_ready, 1)
                if live(s - 2):
                    e = tile_expert(dve, s - 2)
                    dve.wait_ge(y_ready, s - 1)
                    if live(s - 4):
                        dve.wait_ge(stored[u], 8 * (s - 4 - u) + 16)
                    v.tensor_tensor(ys[u][:, :], psY[u][:, 0:D], b2[:, e, :], ALU.add).then_inc(ys_ready, 1)

            step = Chain(dve, chain)
            v.tensor_tensor(gap[:, :], best[:, 1, :], best[:, 0, :], ALU.subtract).then_inc(gap_ready, 1)
            dve.wait_ge(c_in, 64)
            dve.wait_ge(total_ready, 1)
            step(v.tensor_copy(totals[:, :], psY[0][:, 0:E1]))
            step(v.tensor_tensor(over[:, :, :], wide(totals[:, :], [P, E1, T]), limits[:, :, :], ALU.is_gt))
            step(v.tensor_reduce(tiles[:, :], over[:, :, :], AX_X, ALU.add))
            step(v.tensor_copy(ends[0][:, :], tiles[:, :]))
            a, b, reach = ends[0], ends[1], 1
            while reach < E1:
                step(v.tensor_copy(b[:, 0:reach], a[:, 0:reach]))
                step(v.tensor_tensor(b[:, reach:E1], a[:, reach:E1], a[:, 0:E1 - reach], ALU.add))
                a, b, reach = b, a, 2 * reach
            step(v.tensor_tensor(passed[:, :, :], tile_no[:, :, :],
                                 a[:, :].unsqueeze(1).to_broadcast([P, NS, E1]), ALU.is_ge))
            step(v.tensor_reduce(expert_f[:, :], passed[:, :, :], AX_X, ALU.add))
            step(v.tensor_scalar(expert_f[:, :], expert_f[:, :], float(E1 - 1), None, ALU.min))
            v.tensor_copy(expert[:, :], expert_f[:, :]).then_inc(tables_ready, 1)
            step(v.tensor_scalar(move[:, :], tiles[:, :], -1.0, float(T), ALU.mult, ALU.add))
            step(v.tensor_tensor(passed[:, :, :], passed[:, :, :],
                                 move[:, :].unsqueeze(1).to_broadcast([P, NS, E1]), ALU.mult))
            step(v.tensor_reduce(shift[:, :], passed[:, :, :], AX_X, ALU.add))
            step(v.tensor_tensor(shift[:, :], shift[:, :], tile_f[:, :], ALU.add))
            step(v.tensor_scalar(shift[:, :], shift[:, :], float(SLOT_TILES - 1), None, ALU.min))
            v.tensor_copy(source[:, :], shift[:, :]).then_inc(tables_ready, 1)
            step(v.tensor_tensor(base[:, :], a[:, :], tiles[:, :], ALU.subtract))
            step(v.scalar_tensor_tensor(base[:, :], base[:, :], float(P), region[:, :], ALU.mult, ALU.subtract))
            for k in range(2):
                step(v.tensor_tensor(moved[:, :, :], one_hot[:, k, :, :],
                                     base[:, :].unsqueeze(1).to_broadcast([P, T, E1]), ALU.mult))
                step(v.tensor_reduce(offset[:, :], moved[:, :, :], AX_X, ALU.add))
                step(v.tensor_tensor(offset[:, :], offset[:, :], slot_f[:, k, :], ALU.add))
                step(v.tensor_copy(slots[k][:, :], offset[:, :]))
            dve.wait_ge(grown_ready, 1)
            step(v.tensor_scalar(denominator[:, :], grown[:, :], 1.0, None, ALU.add))
            step(v.reciprocal(share[0][:, :], denominator[:, :]))
            step(v.tensor_tensor(share[1][:, :], grown[:, :], share[0][:, :], ALU.mult))
            dve.wait_ge(tables_ready, 2)
            dve.wait_ge(b_in, 32)
            rows_lo(0, 0)
            steps(dve, iteration, FIRST, LAST, TOTAL)


def combine_and_store(nc, t, dram, out):
    with ExitStack() as ctx:
        sem = semaphores(nc, ctx)
        X, slots, share = t["X"], t["slots"], t["share"]
        results = ctx.enter_context(nc.sbuf_tensor("results", [P, T, 2, D], F32))
        groups = [(n, min(n + 4, T)) for n in range(0, T, 4)]
        fetched = [sem(f"g_fetched{n}") for n in range(len(groups))]
        added, done, stored = sem("g_added"), sem("g_done"), sem("g_stored")
        block = ctx.enter_context(nc.Block())

        @block.gpsimd
        def _(pool):
            for n in range(T):
                for k in range(2):
                    pool.indirect_dma_start(out=results[:, n, k, :], in_=dram["slot_out"], out_offset=None,
                                            in_offset=bass.IndirectOffsetOnAxis(ap=slots[k][:, n:n + 1], axis=0)
                                            ).then_inc(fetched[n // 4], 16)

        @block.vector
        def _(dve):
            for n in range(T):
                if n % 4 == 0:
                    a, b = groups[n // 4]
                    dve.wait_ge(fetched[n // 4], 32 * (b - a))
                for k in range(2):
                    nc.vector.scalar_tensor_tensor(X[:, n, :], results[:, n, k, :], share[k][:, n:n + 1], X[:, n, :],
                                                   ALU.mult, ALU.add).then_inc(added if k == 0 else done, 1)
                    if k == 0:
                        dve.wait_ge(added, n + 1)

        @block.sync
        def _(sp):
            for n in range(T):
                sp.wait_ge(done, n + 1)
                rows = min(P, N - n * P)
                sp.dma_start(out[n * P:n * P + rows, :], X[0:rows, n, :]).then_inc(stored, 16)
            sp.wait_ge(stored, 16 * T)


def gnn_program(nc, dram, out):
    with ExitStack() as ctx:
        sb = lambda n, s, d=F32: ctx.enter_context(nc.sbuf_tensor(n, s, d))
        t = {"X": sb("X", [P, T, D]), "ident": sb("ident", [P, P]), "stats": sb("stats", [P, T, 6])}
        with ExitStack() as att:
            t["H"] = att.enter_context(nc.sbuf_tensor("H", [P, T, 2 * D], F16))
            sa = lambda n, s, d=F32: att.enter_context(nc.sbuf_tensor(n, s, d))
            t["S1"] = sa("S1", [P, T])
            t["S2row"] = sa("S2row", [P, NP])
            attention_scores(nc, t, dram)
            graph_attention(nc, t, dram)
        t["w_unscale"] = sb("w_unscale", [P, E1])
        with ExitStack() as ffn:
            t["HT"] = ffn.enter_context(nc.sbuf_tensor("HT", [P, KD, NP], F32))
            t["L0"] = ffn.enter_context(nc.sbuf_tensor("L0", [P, T, E0], F32))
            normalised_projection(nc, t, "r0p", dram["rwT"], E0, t["L0"], HT=t["HT"])
            capacity_ffn(nc, t, dram)
        t["slots"] = [sb(f"slots{k}", [P, T], I32) for k in range(2)]
        t["share"] = [sb(f"part{k}", [P, T]) for k in range(2)]
        t["one_hot"] = sb("one_hot", [P, 2, T, E1])
        t["best"] = sb("best", [P, 2, T])
        t["slot_f"] = sb("slot_f", [P, 2, T])
        t["running"] = sb("running", [P, E1], F16)
        t["ones"] = sb("ones1", [P, P], F16)
        t["W1_in"] = ctx.enter_context(nc.semaphore("W1_in"))
        t["adj_in"] = [ctx.enter_context(nc.semaphore(f"adjT_in{u}")) for u in range(2)]
        with ExitStack() as experts:
            t["W1"] = experts.enter_context(nc.sbuf_tensor("W1", [P, E1, KD, 2, 2 * F1], F16))
            with ExitStack() as agg:
                t["H"] = agg.enter_context(nc.sbuf_tensor("H2", [P, T, 2 * D + 2], F16))
                t["own"] = agg.enter_context(nc.sbuf_tensor("own", [P, T, D], F32))
                t["adjTf"] = [agg.enter_context(nc.sbuf_tensor(f"adjTf{u}", [P, NP], F32)) for u in range(2)]

                def first_tiles(sp):
                    for u in range(2):
                        sp.dma_start(t["adjTf"][u][:, :], dram["adjT"][u, :, :]).then_inc(t["adj_in"][u], 16)

                normalised_projection(nc, t, "self", dram["WsT"], D, t["own"], bias=(dram["b_self"], dram["b_neigh"]),
                                      H=t["H"], after=first_tiles)
                mean_aggregation(nc, t, dram)
            expert_ffn(nc, t, dram)
        combine_and_store(nc, t, dram, out)


def kernel(**inputs):
    import numpy as np
    import concourse.bacc as bacc
    from concourse.bass_utils import run_bass_kernel_spmd

    a = {k: np.asarray(v) for k, v in inputs.items()}
    full = lambda v, shape: np.ascontiguousarray(np.broadcast_to(v, shape))
    flip = lambda v: np.ascontiguousarray(v.T)
    adj = np.pad(a["adj"], ((0, NP - N), (0, NP - N)))
    adj_tiles = np.ascontiguousarray(adj.reshape(T, P, T, P).transpose(0, 3, 2, 1)).reshape(T, P, NP)
    arrays = {
        "x": np.pad(a["x"], ((0, NP - N), (0, 0))),
        "adj": adj,
        "WT": flip(a["L0_gnn_W"]),
        "awb": full(a["L0_gnn_a_w"].reshape(KD, P).T[:, :, None], (P, KD, P)),
        "ab": full(a["L0_gnn_a_b"].reshape(1, 1), (P, 1)),
        "ident": np.eye(P, dtype=np.float32),
        "fcw": np.ascontiguousarray(a["L0_gnn_fc_w"]),
        "fcb": full(a["L0_gnn_fc_b"], (P, D)),
        "rwT": flip(a["L0_ffn_router_w"]),
        "desc0": full(np.arange(E0, 0, -1, dtype=np.float32), (P, E0)),
        "tri": np.triu(np.ones((P, P), np.float16), 1),
        "ones": np.ones((P, P), np.float16),
        "w1T": flip(a["L0_ffn_w1"]),
        "w2T": flip(a["L0_ffn_w2"]),
        "b1c": flip(a["L0_ffn_b1"].reshape(MF, P)),
        "b2": full(a["L0_ffn_b2"], (P, D)),
        "WsT": flip(a["L1_gnn_W_self"]),
        "WnT": flip(a["L1_gnn_W_neigh"]),
        "adjT": adj_tiles,
        "Wg": a["L1_ffn_Wg"],
        "bg": full(a["L1_ffn_bg"], (P, 2, E1)),
        "desc1": full(np.arange(E1, 0, -1, dtype=np.float32), (P, 2, E1)),
        "region": full(NP * np.arange(E1, dtype=np.float32), (P, 2, E1)),
        "region_e": full(NP * np.arange(E1, dtype=np.float32), (P, E1)),
        "tile_f": full(np.arange(NS, dtype=np.float32), (P, NS)),
        "limits": full(P * np.arange(T, dtype=np.float32), (P, E1, T)),
        "tile_no": full(np.arange(NS, dtype=np.float32)[:, None], (P, NS, E1)),
        "eW1": np.ascontiguousarray(a["L1_ffn_W1"].reshape(E1, KD, P, 2 * F1).transpose(2, 0, 1, 3)
                                    ).reshape(P, E1, KD * 2 * F1),
        "eW2": np.ascontiguousarray(a["L1_ffn_W2"].reshape(E1, KF, P, D).transpose(2, 0, 1, 3)),
        "eb1": full(a["L1_ffn_b1"], (P, E1, 2 * F1)),
        "eb2": full(a["L1_ffn_b2"], (P, E1, D)),
        "b_self": full(a["L1_gnn_b_self"], (P, D)),
        "b_neigh": full(a["L1_gnn_b_neigh"], (P, D)),
    }
    nc = bacc.Bacc("TRN2", target_bir_lowering=False, num_devices=1)
    dram = {k: nc.dram_tensor(k + "_dram", v.shape, mybir.dt.from_np(v.dtype), kind="ExternalInput").ap()
            for k, v in arrays.items()}
    for name, tiles in (("slot_rows", SLOT_TILES), ("slot_out", NS)):
        dram[name] = nc.dram_tensor(name, (tiles * P, D), F32, kind="Internal").ap()
    dram["w1_parts"] = nc.dram_tensor("w1_parts", (P, E1, KD * 2 * 2 * F1), F16, kind="Internal").ap()
    dram["peaks"] = nc.dram_tensor("peaks", (E1, P), F32, kind="Internal").ap()
    out = nc.dram_tensor("out_dram", (N, D), F32, kind="ExternalOutput").ap()
    gnn_program(nc, dram, out)
    r = run_bass_kernel_spmd(nc, [{k + "_dram": v for k, v in arrays.items()}], core_ids=[0])
    return r.results[0]["out_dram"]
```

```python
from contextlib import ExitStack

import concourse.bass as bass
from concourse import mybir

ALU = mybir.AluOpType
ACT = mybir.ActivationFunctionType
AX_X = mybir.AxisListType.X
F32 = mybir.dt.float32
F16 = mybir.dt.float16
BF16 = mybir.dt.bfloat16
I32 = mybir.dt.int32
ds = bass.ds

P = 128
N = 3327
T = -(-N // P)
NP = T * P
D = 256
KD = D // P
EPS = 1e-5
ALPHA = 0.2
FAR = float(2 ** 53)
EDGE_SCALE = float(2 ** 126)
H_SCALE = float(2 ** 11)
P_SCALE = float(2 ** 15)
assert T % 2 == 0 and NP - N < P


def wait(eng, sem, value):
    if not (isinstance(value, int) and value <= 0):
        eng.wait_ge(sem, value)


def steps(eng, body, first, last, total, unroll=2):
    assert (last - first) % unroll == 0 and unroll % 2 == 0
    for t in range(first):
        body(t, t % 2)
    with eng.Fori(first, last - unroll + 1, unroll) as i:
        for u in range(unroll):
            body(i + u, (first + u) % 2)
    for t in range(last, total):
        body(t, t % 2)


def pairs(eng, body):
    body(0)
    with eng.Fori(2, T - 1, 2) as t:
        body(t)


def semaphores(nc, ctx):
    made = []

    def make(name):
        made.append(nc.alloc_semaphore(name))
        return made[-1]

    def give_back():
        nc.clear_and_free_semaphores(made)
        nc.all_engine_barrier()

    ctx.callback(give_back)
    return make


def settled(eng, passed, *waits):
    for sem, count in waits:
        wait(eng, sem, count)
    eng.sem_inc(passed, 1)


class RowNorm:

    def __init__(self, nc, ctx, make, name, stats):
        sb = lambda n: ctx.enter_context(nc.sbuf_tensor(f"{name}_{n}", [P, T], F32))
        self.nc, self.stats = nc, stats
        self.sum, self.mean, self.gap, self.gap2, self.m2, self.var_in, self.var, self.std, self.rstd = (
            sb(n) for n in ("sum", "mean", "gap", "gap2", "m2", "var_in", "var", "std", "rstd"))
        self.chain, self.var_done, self.std_done = (make(f"{name}_{n}") for n in ("chain", "var_done", "std_done"))

    def deviation(self, act):
        act.wait_ge(self.var_done, 1)
        self.nc.scalar.activation(self.std[:, :], self.var[:, :], ACT.Sqrt).then_inc(self.std_done, 1)

    def finish(self, dve):
        v = self.nc.vector
        step = Chain(dve, self.chain)
        even, odd = (lambda n: self.stats[:, :, n]), (lambda n: self.stats[:, :, 3 + n])
        v.tensor_tensor(self.sum[:, :], even(1), odd(1), ALU.add).then_inc(self.chain, 1)
        v.tensor_tensor(self.gap[:, :], even(1), odd(1), ALU.subtract).then_inc(self.chain, 1)
        v.tensor_tensor(self.m2[:, :], even(2), odd(2), ALU.add).then_inc(self.chain, 1)
        step.count = 3
        dve.wait_ge(self.chain, 3)
        v.tensor_scalar(self.mean[:, :], self.sum[:, :], 0.5, None, ALU.mult).then_inc(self.chain, 1)
        v.tensor_tensor(self.gap2[:, :], self.gap[:, :], self.gap[:, :], ALU.mult).then_inc(self.chain, 1)
        v.tensor_scalar(self.var_in[:, :], self.m2[:, :], 1.0 / D, EPS, ALU.mult, ALU.add).then_inc(self.chain, 1)
        step.count = 6
        dve.wait_ge(self.chain, 6)
        v.scalar_tensor_tensor(self.var[:, :], self.gap2[:, :], 0.25, self.var_in[:, :], ALU.mult,
                               ALU.add).then_inc(self.var_done, 1)
        dve.wait_ge(self.std_done, 1)
        step(v.reciprocal(self.rstd[:, :], self.std[:, :]))

    def normalise(self, h, rows, t):
        return self.nc.vector.tensor_scalar(h, rows, self.mean[:, ds(t, 1)], self.rstd[:, ds(t, 1)],
                                            ALU.subtract, ALU.mult)


class Chain:

    def __init__(self, eng, sem):
        self.eng, self.sem, self.count = eng, sem, 0

    def __call__(self, instruction):
        self.count += 1
        instruction.then_inc(self.sem, 1)
        self.eng.wait_ge(self.sem, self.count)


def attention_scores(nc, t, dram):
    with ExitStack() as ctx:
        sb = lambda n, s, d=F32: ctx.enter_context(nc.sbuf_tensor(n, s, d))
        sem = semaphores(nc, ctx)
        X, H, S1, S2row, ident = t["X"], t["H"], t["S1"], t["S2row"], t["ident"]
        WT = sb("WT", [P, KD, 2 * D])
        awb = sb("awb", [P, KD, P])
        ab = sb("ab", [P, 1])
        ones = sb("ones", [P, P])
        U = sb("U", [P, 2 * D])
        norm = RowNorm(nc, ctx, sem, "ln0", t["stats"])
        h = [sb(f"h{u}", [P, D]) for u in range(2)]
        s12 = [sb(f"s12_{u}", [P, 2]) for u in range(2)]
        junk = sb("junk_a", [P, 4, D])
        diag = sb("diag", [P, T, P])
        psU = ctx.enter_context(nc.psum_tensor("psU", [P, 2 * D], F32))
        psR = ctx.enter_context(nc.psum_tensor("psR", [P, 2, 512], F32))
        XG = [(0, 7), (7, 14), (14, 20), (20, T)]
        x_in = [sem(f"x_in{n}") for n in range(len(XG))]
        w_in, h_done, stats_done = sem("aw_in"), sem("a_h"), sem("a_stats")
        u_done, u_copied, ones_set, s1_done = sem("u_done"), sem("u_copied"), sem("ones_set"), sem("a_s1")
        hi_done, lo_done, s_done, diag_done = sem("a_hi"), sem("a_lo"), sem("a_s"), sem("a_diag")
        row_done, row_copied = sem("a_row"), sem("a_rowcp")
        block = ctx.enter_context(nc.Block())
        xv = dram["x"].rearrange("(t p) d -> p t d", p=P)

        @block.sync
        def _(sp):
            for n, (a, b) in enumerate(XG):
                sp.dma_start(X[:, a:b, :], xv[:, a:b, :]).then_inc(x_in[n], 16)
            sp.dma_start(awb[:, :, :], dram["awb"]).then_inc(w_in, 16)
            sp.dma_start(ab[:, :], dram["ab"]).then_inc(w_in, 16)
            sp.dma_start(ident[:, :], dram["ident"]).then_inc(w_in, 16)
            for u in range(2):
                sp.dma_start(t["adjf"][u][:, :], dram["adj"][u * P:(u + 1) * P, :]).then_inc(t["adj_in0"][u], 16)
            for n in range(len(XG)):
                sp.wait_ge(x_in[n], 16)
            sp.wait_ge(w_in, 64)

        @block.tensor
        def _(pe):
            pe.wait_ge(w_in, 64)
            for k in range(KD):
                mm = nc.tensor.matmul(psU[:, :], awb[:, k, :], WT[:, k, :], start=(k == 0), stop=(k == KD - 1))
            mm.then_inc(u_done, 1)
            pe.wait_ge(ones_set, 1)

            def row(t, u):
                pe.wait_ge(diag_done, t + 1)
                wait(pe, row_copied, t - 1)
                nc.tensor.matmul(psR[:, u, 0:P], ones[:, :], diag[:, t, :], start=True, stop=True).then_inc(row_done, 1)

            steps(pe, row, 2, T, T)

        @block.scalar
        def _(act):
            act.dma_start(WT[:, :, :], dram["WT"].rearrange("(k p) n -> p k n", p=P)).then_inc(w_in, 16)
            act.wait_ge(u_done, 1)
            nc.scalar.copy(U[:, :], psU[:, :]).then_inc(u_copied, 1)
            norm.deviation(act)

            def row_pair(i):
                for u in range(2):
                    act.wait_ge(row_done, i + u + 1)
                    nc.scalar.copy(S2row[:, ds((i + u) * P, P)], psR[:, u, 0:P]).then_inc(row_copied, 1)

            def tile_pair(i):
                for u in range(2):
                    act.wait_ge(h_done, i + u + 1)
                    nc.scalar.activation(H[:, i + u, 0:D], h[u][:, :], ACT.Copy, scale=H_SCALE).then_inc(hi_done, 1)
                for u in range(2):
                    act.wait_ge(s_done, 2 * (i + u + 1))
                    nc.scalar.activation(S1[:, ds(i + u, 1)], s12[u][:, 0:1], ACT.Identity,
                                         bias=ab[:, :]).then_inc(s1_done, 1)
                    nc.scalar.activation(diag[:, i + u, :], ident[:, :], ACT.Copy,
                                         scale=s12[u][:, 1:2]).then_inc(diag_done, 1)

                if not isinstance(i, int):
                    row_pair(i - 2)

            act.wait_ge(w_in, 64)
            pairs(act, tile_pair)
            row_pair(T - 2)

        @block.vector
        def _(dve):
            nc.vector.memset(ones[:, :], 1.0).then_inc(ones_set, 1)
            for n, (a, b) in enumerate(XG):
                dve.wait_ge(x_in[n], 16)
                for i in range(a, b):
                    nc.vector.bn_stats(t["stats"][:, i, :], X[:, i, :]).then_inc(stats_done, 1)
            dve.wait_ge(stats_done, T)
            norm.finish(dve)
            dve.wait_ge(u_copied, 1)
            dve.wait_ge(w_in, 64)

            def tile_pair(i):
                for u in range(2):
                    wait(dve, s_done, 2 * (i + u) - 2)
                    wait(dve, lo_done, i + u - 1)
                    norm.normalise(h[u][:, :], X[:, i + u, :], i + u).then_inc(h_done, 1)
                for u in range(2):
                    dve.wait_ge(h_done, i + u + 1)
                    wait(dve, s1_done, i + u - 1)
                    wait(dve, diag_done, i + u - 1)
                    nc.vector.tensor_tensor_reduce(junk[:, 2 * u, :], h[u][:, :], U[:, 0:D], 1.0, 0.0, ALU.mult,
                                                   ALU.add, s12[u][:, 0:1]).then_inc(s_done, 1)
                    nc.vector.tensor_tensor_reduce(junk[:, 2 * u + 1, :], h[u][:, :], U[:, D:2 * D], 1.0, 0.0, ALU.mult,
                                                   ALU.add, s12[u][:, 1:2]).then_inc(s_done, 1)
                for u in range(2):
                    dve.wait_ge(hi_done, i + u + 1)
                    nc.vector.scalar_tensor_tensor(H[:, i + u, D:2 * D], h[u][:, :], H_SCALE, H[:, i + u, 0:D],
                                                   ALU.mult, ALU.subtract).then_inc(lo_done, 1)

            pairs(dve, tile_pair)


TG = [(0, 8), (8, 16), (16, 24), (24, T)]
NG = len(TG)


def graph_attention(nc, t, dram):
    with ExitStack() as ctx:
        sb = lambda n, s, d=F32: ctx.enter_context(nc.sbuf_tensor(n, s, d))
        sem = semaphores(nc, ctx)
        X, H, S1, S2row, ident, stats = t["X"], t["H"], t["S1"], t["S2row"], t["ident"], t["stats"]
        stats_done = sem("b_stats")
        adjf = t["adjf"]
        bias = [sb(f"maskbias{u}", [P, NP], BF16) for u in range(2)]
        score = [sb(f"score{u}", [P, NP]) for u in range(2)]
        probs = [sb(f"probs{u}", [P, NP]) for u in range(2)]
        PThi = [sb(f"PThi{u}", [P, NP], F16) for u in range(2)]
        PTlo = [sb(f"PTlo{u}", [P, NP], F16) for u in range(2)]
        fcw = sb("fcw", [P, KD, D])
        fcb = sb("fcb", [P, D])
        big = sb("big", [P, 1])
        rowmax = [sb(f"rowmax{u}", [P, 1]) for u in range(2)]
        shifted = [sb(f"shifted{u}", [P, 1]) for u in range(2)]
        leaky = [sb(f"leaky{u}", [P, 1]) for u in range(2)]
        straight = [sb(f"straight{u}", [P, 1]) for u in range(2)]
        sloped = [sb(f"sloped{u}", [P, 1]) for u in range(2)]
        total = [sb(f"total{u}", [P, 1]) for u in range(2)]
        rtotal = sb("rtotal", [P, T])
        rscale = sb("rscale", [P, T])
        agg = [sb(f"agg{u}", [P, D]) for u in range(2)]
        aggT = [sb(f"aggT{u}", [P, KD, P]) for u in range(2)]
        ps = lambda n, s: ctx.enter_context(nc.psum_tensor(n, s, F32))
        psT = [ps(f"psT{u}", [P, 8 * P]) for u in range(2)]
        acc = [ps(f"acc{u}", [P, 2 * D]) for u in range(2)]
        psA = ps("psA", [P, 512])
        psF = ps("psF", [P, 512])
        blank = sb("blank", [P, D + 1])
        zeroed, spare_in = sem("b_zeroed"), sem("b_spare")
        adj_in = t["adj_in0"]
        w_in, pad_set, mask_waits = sem("b_w"), sem("b_pad"), sem("b_mask_waits")
        mask_ready, masked_ready, small, shift_ready = sem("b_mask"), sem("b_masked"), sem("b_small"), sem("b_shift")
        straight_ready, sloped_ready = sem("b_straight"), sem("b_sloped")
        probs_ready, turned, hi_ready, lo_ready = (sem("b_probs"), sem("b_turned"),
                                                                sem("b_hi"), sem("b_lo"))
        acc_ready, scale_ready, agg_ready = sem("b_acc"), sem("b_scale"), sem("b_agg")
        agg_turned, aggT_ready, fc_ready, biased, x_ready = (sem("b_aggt"), sem("b_aggT"), sem("b_fc"),
                                                             sem("b_biased"), sem("b_x"))
        block = ctx.enter_context(nc.Block())
        adjv = dram["adj"].rearrange("(t p) j -> t p j", p=P)
        slots = dram["slot_rows"].rearrange("(t s p) d -> t p s d", p=P, s=E1)
        FIRST, LAST, TOTAL = 4, T - 4, T + 3

        def live(t):
            return not isinstance(t, int) or 0 <= t < T

        @block.sync
        def _(sp):
            sp.dma_start(fcw[:, :, :], dram["fcw"].rearrange("(k p) n -> p k n", p=P)).then_inc(w_in, 16)
            sp.dma_start(fcb[:, :], dram["fcb"]).then_inc(w_in, 16)

            def load(t, u):
                if live(t):
                    if not isinstance(t, int) or t > 1:
                        sp.wait_ge(mask_ready, t - 1)
                        sp.dma_start(adjf[u][:, :], adjv[t, :, :]).then_inc(adj_in[u], 16)
                    sp.dma_start(slots[t, :, :, :], blank[:, :].unsqueeze(1).to_broadcast([P, E1, D + 1])
                                 ).then_inc(zeroed, 16)

            sp.dma_start(blank[:, D:D + 1], dram["spare"]).then_inc(spare_in, 16)
            sp.wait_ge(spare_in, 16)
            sp.wait_ge(pad_set, 4)
            steps(sp, load, FIRST, LAST, T)
            sp.wait_ge(w_in, 32)
            sp.wait_ge(zeroed, 16 * T)

        @block.gpsimd
        def _(pool):
            pool.wait_ge(w_in, 32)
            with pool.Fori(0, T) as i:
                nc.gpsimd.tensor_tensor(X[:, i, :], X[:, i, :], fcb[:, :], ALU.add).then_inc(biased, 1)

        @block.scalar
        def _(act):
            def hi(t, u, g):
                a, b = TG[g]
                act.wait_ge(turned, NG * t + g + 1)
                if g == 0:
                    wait(act, acc_ready, t - 1)
                nc.scalar.activation(PThi[u][:, a * P:b * P], psT[g % 2][:, 0:(b - a) * P], ACT.Copy,
                                     scale=P_SCALE).then_inc(hi_ready, 1)

            def no_edge(t, u):
                act.wait_ge(adj_in[u], 8 * (t - u) + 16)
                wait(act, masked_ready, t - 1)
                nc.scalar.activation(bias[u][:, 0:N], adjf[u][:, 0:N], ACT.Relu, bias=big[:, :],
                                     scale=-EDGE_SCALE).then_inc(mask_ready, 1)

            def straight_exp(t, u):
                act.wait_ge(shift_ready, 2 * t + 2)
                wait(act, turned, NG * (t - 1))
                nc.scalar.activation(probs[u][:, 0:N], score[u][:, 0:N], ACT.Exp,
                                     bias=straight[u][:, :]).then_inc(straight_ready, 1)

            def sloped_exp(t, u):
                act.wait_ge(straight_ready, t + 1)
                nc.scalar.activation(score[u][:, 0:N], score[u][:, 0:N], ACT.Exp, bias=sloped[u][:, :],
                                     scale=ALPHA).then_inc(sloped_ready, 1)

            def iteration(t, u):
                if live(t + 1):
                    straight_exp(t + 1, 1 - u)
                if live(t):
                    hi(t, u, 0)
                    hi(t, u, 1)
                if live(t + 1):
                    sloped_exp(t + 1, 1 - u)
                if live(t):
                    hi(t, u, 2)
                    hi(t, u, 3)
                if live(t - 2):
                    act.wait_ge(agg_turned, t - 1)
                    wait(act, fc_ready, t - 3)
                    nc.scalar.copy(aggT[u][:, :, :].rearrange("p k n -> p (k n)"), psA[:, 0:D]).then_inc(aggT_ready, 1)
                if live(t + 3):
                    no_edge(t + 3, 1 - u)

            act.wait_ge(pad_set, 4)
            no_edge(0, 0)
            no_edge(1, 1)
            straight_exp(0, 0)
            sloped_exp(0, 0)
            no_edge(2, 0)
            steps(act, iteration, FIRST, LAST, TOTAL)

        @block.vector
        def _(dve):
            nc.vector.memset(big[:, :], FAR).then_inc(pad_set, 1)
            nc.vector.memset(blank[:, 0:D], 0.0).then_inc(pad_set, 1)
            for u in range(2):
                nc.vector.memset(probs[u][:, N:NP], 0.0).then_inc(pad_set, 1)

            def masked(t, u):
                settled(dve, mask_waits, (mask_ready, t + 1), (probs_ready, t - 1))
                nc.vector.tensor_tensor_reduce(score[u][:, 0:N], S2row[:, 0:N], bias[u][:, 0:N], 1.0, -2 * FAR,
                                               ALU.subtract, ALU.max, rowmax[u][:, :]).then_inc(masked_ready, 1)

            def shift(t, u):
                dve.wait_ge(masked_ready, t + 1)
                nc.vector.tensor_tensor(shifted[u][:, :], rowmax[u][:, :], S1[:, ds(t, 1)],
                                        ALU.add).then_inc(small, 1)

            def leak(t, u):
                dve.wait_ge(small, 2 * t + 1)
                nc.vector.scalar_tensor_tensor(leaky[u][:, :], shifted[u][:, :], ALPHA, shifted[u][:, :],
                                               ALU.mult, ALU.max).then_inc(small, 1)

            def exp_biases(t, u):
                dve.wait_ge(small, 2 * t + 2)
                nc.vector.tensor_tensor(straight[u][:, :], S1[:, ds(t, 1)], leaky[u][:, :],
                                        ALU.subtract).then_inc(shift_ready, 1)
                nc.vector.scalar_tensor_tensor(sloped[u][:, :], S1[:, ds(t, 1)], ALPHA, leaky[u][:, :], ALU.mult,
                                               ALU.subtract).then_inc(shift_ready, 1)

            def combine(t, u):
                dve.wait_ge(sloped_ready, t + 1)
                nc.vector.scalar_tensor_tensor(probs[u][:, 0:N], score[u][:, 0:N], 1.0, probs[u][:, 0:N], ALU.mult,
                                               ALU.max, accum_out=total[u][:, :]).then_inc(probs_ready, 1)

            def lo(t, u, g):
                a, b = TG[g]
                dve.wait_ge(hi_ready, NG * t + g + 1)
                nc.vector.scalar_tensor_tensor(PTlo[u][:, a * P:b * P], psT[g % 2][:, 0:(b - a) * P], P_SCALE,
                                               PThi[u][:, a * P:b * P], ALU.mult, ALU.subtract).then_inc(lo_ready, 1)

            def invert_total(t, u):
                dve.wait_ge(probs_ready, t + 1)
                nc.vector.reciprocal(rtotal[:, ds(t, 1)], total[u][:, :]).then_inc(scale_ready, 1)

            def row_scale(t, u):
                dve.wait_ge(scale_ready, 2 * t + 1)
                nc.vector.tensor_scalar(rscale[:, ds(t, 1)], rtotal[:, ds(t, 1)], 1.0 / (H_SCALE * P_SCALE), None,
                                        ALU.mult).then_inc(scale_ready, 1)

            def aggregate(t, u):
                dve.wait_ge(scale_ready, 2 * t + 2)
                dve.wait_ge(acc_ready, t + 1)
                wait(dve, agg_turned, t - 1)
                nc.vector.tensor_scalar(agg[u][:, :], acc[u][:, 0:D], rscale[:, ds(t, 1)], None,
                                        ALU.mult).then_inc(agg_ready, 1)

            def add_projection(t):
                dve.wait_ge(biased, t + 1)
                dve.wait_ge(fc_ready, t + 1)
                nc.vector.tensor_tensor(X[:, t, :], psF[:, 0:D], X[:, t, :], ALU.add).then_inc(x_ready, 1)

            def row_stats(t):
                dve.wait_ge(x_ready, t + 1)
                nc.vector.bn_stats(stats[:, t, :], X[:, t, :]).then_inc(stats_done, 1)

            def iteration(t, u):
                if live(t + 2):
                    masked(t + 2, u)
                if live(t):
                    row_scale(t, u)
                if live(t - 2):
                    aggregate(t - 2, u)
                if live(t - 3):
                    add_projection(t - 3)
                if live(t):
                    lo(t, u, 0)
                if live(t - 3):
                    row_stats(t - 3)
                if live(t + 2):
                    shift(t + 2, u)
                if live(t):
                    lo(t, u, 1)
                if live(t + 2):
                    leak(t + 2, u)
                if live(t + 2):
                    exp_biases(t + 2, u)
                if live(t + 1):
                    combine(t + 1, 1 - u)
                if live(t):
                    lo(t, u, 2)
                    lo(t, u, 3)
                if live(t + 1):
                    invert_total(t + 1, 1 - u)

            for t, u in ((0, 0), (1, 1)):
                masked(t, u)
                shift(t, u)
                leak(t, u)
                exp_biases(t, u)
            combine(0, 0)
            invert_total(0, 0)
            dve.wait_ge(w_in, 32)
            steps(dve, iteration, FIRST, LAST, TOTAL)

        @block.tensor
        def _(pe):
            def turn(t, u, g):
                a, b = TG[g]
                if g == 0:
                    pe.wait_ge(probs_ready, t + 1)
                wait(pe, hi_ready, NG * t + g - 1)
                wait(pe, lo_ready, NG * t + g - 1)
                for j in range(a, b):
                    mm = nc.tensor.transpose(psT[g % 2][:, (j - a) * P:(j - a + 1) * P],
                                             probs[u][:, j * P:(j + 1) * P], ident[:, :])
                mm.then_inc(turned, 1)

            def products(t, u, g):
                a, b = TG[g]
                pe.wait_ge(lo_ready, NG * t + g + 1)
                if g == 0:
                    wait(pe, agg_ready, t - 1)
                for j in range(a, b):
                    high, low = PThi[u][:, j * P:(j + 1) * P], PTlo[u][:, j * P:(j + 1) * P]
                    for n, (left, right) in enumerate(((high, H[:, j, 0:D]), (high, H[:, j, D:2 * D]),
                                                       (low, H[:, j, 0:D]))):
                        mm = nc.tensor.matmul(acc[u][:, 0:D], left, right, start=(j == 0 and n == 0),
                                              stop=(j == T - 1 and n == 2))
                if g == NG - 1:
                    mm.then_inc(acc_ready, 1)

            def iteration(t, u):
                if live(t):
                    turn(t, u, 0)
                    turn(t, u, 1)
                if live(t - 1):
                    products(t - 1, 1 - u, 0)
                if live(t - 2):
                    pe.wait_ge(agg_ready, t - 1)
                    wait(pe, aggT_ready, t - 2)
                    for k in range(KD):
                        mm = nc.tensor.transpose(psA[:, k * P:(k + 1) * P], agg[u][:, k * P:(k + 1) * P], ident[:, :])
                    mm.then_inc(agg_turned, 1)
                if live(t):
                    turn(t, u, 2)
                if live(t):
                    turn(t, u, 3)
                if live(t - 1):
                    products(t - 1, 1 - u, 1)
                    products(t - 1, 1 - u, 2)
                if live(t - 2):
                    pe.wait_ge(aggT_ready, t - 1)
                    wait(pe, x_ready, t - 2)
                    for k in range(KD):
                        mm = nc.tensor.matmul(psF[:, 0:D], aggT[u][:, k, :], fcw[:, k, :], start=(k == 0),
                                              stop=(k == KD - 1))
                    mm.then_inc(fc_ready, 1)
                if live(t - 1):
                    products(t - 1, 1 - u, 3)

            pe.wait_ge(w_in, 32)
            pe.wait_ge(pad_set, 4)
            steps(pe, iteration, FIRST, LAST, TOTAL)


def normalised_projection(nc, t, name, w_dram, width, out, bias=None, HT=None, H=None, after=None):
    with ExitStack() as ctx:
        make = semaphores(nc, ctx)
        sem = lambda n: make(f"{name}_{n}")
        X, ident = t["X"], t["ident"]
        norm = RowNorm(nc, ctx, make, name + "_ln", t["stats"])
        h = [ctx.enter_context(nc.sbuf_tensor(f"{name}_h{u}", [P, D], F32)) for u in range(2)]
        h_done = sem("h_done")
        W = ctx.enter_context(nc.sbuf_tensor(name + "_W", [P, KD, width], F32))
        hT = [ctx.enter_context(nc.sbuf_tensor(f"{name}_hT{u}", [P, KD, P], F32)) for u in range(2)]
        psT = [ctx.enter_context(nc.psum_tensor(f"{name}_psT{u}", [P, 512], F32)) for u in range(2)]
        psO = [ctx.enter_context(nc.psum_tensor(f"{name}_psO{u}", [P, 512], F32)) for u in range(2)]
        w_in, turned, hT_ready, copied, projected, out_ready = (sem("w"), sem("turned"), sem("hT"), sem("copied"),
                                                                sem("projected"), sem("out"))
        hi_ready, lo_ready, bias_ready = sem("hi"), sem("lo"), sem("bias")
        if bias is not None:
            bias_sb = ctx.enter_context(nc.sbuf_tensor(name + "_bias", [P, 2, width], F32))
        block = ctx.enter_context(nc.Block())
        loads = 1 + len(bias or ())

        @block.sync
        def _(sp):
            sp.dma_start(W[:, :, :], w_dram.rearrange("(k p) n -> p k n", p=P)).then_inc(w_in, 16)
            if bias is not None:
                for n, b in enumerate(bias):
                    sp.dma_start(bias_sb[:, n, :], b).then_inc(w_in, 16)
            if after is not None:
                after(sp)
            sp.wait_ge(w_in, 16 * loads)

        @block.scalar
        def _(act):
            def tile_pair(i):
                for u in range(2):
                    if H is not None:
                        act.wait_ge(h_done, i + u + 1)
                        nc.scalar.activation(H[:, i + u, 0:D], h[u][:, :], ACT.Copy,
                                             scale=H_SCALE).then_inc(hi_ready, 1)
                    act.wait_ge(turned, i + u + 1)
                    wait(act, projected, i + u - 1)
                    nc.scalar.copy(hT[u][:, :, :].rearrange("p k n -> p (k n)"), psT[u][:, 0:D]).then_inc(hT_ready, 1)
                    if HT is not None:
                        nc.scalar.copy(HT[:, :, ds((i + u) * P, P)],
                                       psT[u][:, 0:D].rearrange("p (k n) -> p k n", k=KD)).then_inc(copied, 1)

            norm.deviation(act)
            pairs(act, tile_pair)

        @block.tensor
        def _(pe):
            def turn(t, u):
                pe.wait_ge(h_done, t + 1)
                wait(pe, copied if HT is not None else hT_ready, t - 1)
                for k in range(KD):
                    mm = nc.tensor.transpose(psT[u][:, k * P:(k + 1) * P], h[u][:, k * P:(k + 1) * P], ident[:, :])
                mm.then_inc(turned, 1)

            def iteration(t, u):
                if not isinstance(t, int) or t + 1 < T:
                    turn(t + 1, 1 - u)
                pe.wait_ge(hT_ready, t + 1)
                wait(pe, out_ready, t - 1)
                for k in range(KD):
                    mm = nc.tensor.matmul(psO[u][:, 0:width], hT[u][:, k, :], W[:, k, :], start=(k == 0),
                                          stop=(k == KD - 1))
                mm.then_inc(projected, 1)

            turn(0, 0)
            pe.wait_ge(w_in, 16 * loads)
            steps(pe, iteration, 2, T - 4, T, unroll=4)

        @block.vector
        def _(dve):
            def normalise(t, u):
                wait(dve, turned, t - 1)
                if H is not None:
                    wait(dve, lo_ready, t - 1)
                norm.normalise(h[u][:, :], X[:, t, :], t).then_inc(h_done, 1)

            def collect(t, u):
                dve.wait_ge(projected, t + 1)
                if bias is not None:
                    nc.vector.tensor_tensor(out[:, t, :], psO[u][:, 0:width], bias_sb[:, 0, :],
                                            ALU.add).then_inc(out_ready, 1)
                else:
                    nc.vector.tensor_copy(out[:, t, :], psO[u][:, 0:width]).then_inc(out_ready, 1)

            def iteration(t, u):
                if not isinstance(t, int) or t + 1 < T:
                    normalise(t + 1, 1 - u)
                if H is not None and (not isinstance(t, int) or t < T):
                    dve.wait_ge(hi_ready, t + 1)
                    nc.vector.scalar_tensor_tensor(H[:, t, D + 2:2 * D + 2], h[u][:, :], H_SCALE, H[:, t, 0:D],
                                                   ALU.mult, ALU.subtract).then_inc(lo_ready, 1)
                if not isinstance(t, int) or t > 0:
                    collect(t - 1, 1 - u)

            norm.finish(dve)
            if bias is not None:
                dve.wait_ge(w_in, 16 * loads)
                if len(bias) == 2:
                    nc.vector.tensor_tensor(bias_sb[:, 0, :], bias_sb[:, 0, :], bias_sb[:, 1, :],
                                            ALU.add).then_inc(bias_ready, 1)
                    dve.wait_ge(bias_ready, 1)
            normalise(0, 0)
            steps(dve, iteration, 2, T - 4, T + 1, unroll=4)


def wide(ap, shape):
    return ap.unsqueeze(2).to_broadcast(shape)


class TopTwo:

    def __init__(self, nc, ctx, name, E):
        sb = lambda n, s, d=F32: ctx.enter_context(nc.sbuf_tensor(f"{name}_{n}", s, d))
        self.nc, self.E = nc, E
        self.descending = sb("descending", [P, E])
        self.score = sb("score", [P, T, E])
        self.rest = sb("rest", [P, T, E])
        self.rank = sb("rank", [P, T])
        self.best = [sb(f"best{k}", [P, T]) for k in range(2)]
        self.one_hot = [sb(f"one_hot{k}", [P, T, E]) for k in range(2)]

    def steps(self, step, logits):
        nc, E, v = self.nc, self.E, self.nc.vector
        full = [P, T, E]
        for k in range(2):
            src = logits if k == 0 else self.rest
            step(v.tensor_reduce(self.best[k][:, :], src[:, :, :], AX_X, ALU.max))
            step(v.tensor_tensor(self.score[:, :, :], src[:, :, :], wide(self.best[k][:, :], full), ALU.is_equal))
            step(v.tensor_tensor(self.score[:, :, :], self.score[:, :, :],
                                 self.descending[:, :].unsqueeze(1).to_broadcast(full), ALU.mult))
            step(v.tensor_reduce(self.rank[:, :], self.score[:, :, :], AX_X, ALU.max))
            step(v.tensor_tensor(self.one_hot[k][:, :, :], self.score[:, :, :], wide(self.rank[:, :], full),
                                 ALU.is_equal))
            if k == 0:
                step(v.scalar_tensor_tensor(self.rest[:, :, :], self.one_hot[0][:, :, :], -FAR * FAR,
                                            logits[:, :, :], ALU.mult, ALU.add))


E0 = 64
CAP = 256
F0 = 1024
MF = F0 // P
CH = 256
NCH = NP // CH
RC = 4
E1 = 8
F1 = 512
KF = F1 // P
NS = (2 * NP - E1) // P + E1
SLOT_TILES = E1 * T
W_PEAK = float(2 ** 14)
assert NS * P >= 2 * NP
assert NP % CH == 0 and T * E0 % RC == 0 and T * E0 // RC <= 512


def capacity_ffn(nc, t, dram):
    with ExitStack() as ctx:
        sb = lambda n, s, d=F32: ctx.enter_context(nc.sbuf_tensor(n, s, d))
        sem = semaphores(nc, ctx)
        X, HT, L = t["X"], t["HT"], t["L0"]
        w1, w1_in = t["w1"], t["w1_in"]
        w2 = sb("w2", [P, MF, D])
        b1 = t["b1"]
        b2 = sb("b2", [P, D])
        G = [sb(f"G{u}", [P, MF, CH]) for u in range(2)]
        Y = sb("Y", [P, T, D])
        top = TopTwo(nc, ctx, "r0", E0)
        chosen = sb("chosen", [P, T, E0], F16)
        before = sb("before", [P, T, E0])
        sums = [sb(f"sums{k}", [P, T, E0]) for k in range(2)]
        tri = sb("tri", [P, P], F16)
        ones = sb("ones16", [P, P], F16)
        z, rz, e2, gate, held = (sb(n, [P, T]) for n in ("z", "rz", "e2", "gate", "held"))
        share = [sb(f"share{k}", [P, T]) for k in range(2)]
        ps = lambda n, s: ctx.enter_context(nc.psum_tensor(n, s, F32))
        psH = [ps(f"psH{u}", [P, 512]) for u in range(2)]
        psY = [ps(f"psY{u}", [P, 512]) for u in range(2)]
        psC = ps("psC", [P, RC, 512])
        w_in, r_in = sem("c_w"), sem("c_r")
        hidden, active, y_done, y_copied = sem("c_hidden"), sem("c_active"), sem("c_y"), sem("c_ycp")
        chain, chosen_ready, counted, before_ready, exp_in, exp_out = (sem("c_chain"), sem("c_chosen"), sem("c_counted"),
                                                               sem("c_before"), sem("c_expin"), sem("c_expout"))
        stats_done = sem("c_stats")
        biased, x_ready = sem("c_biased"), sem("c_x")
        stage = [sb(f"stage{u}", [P, KD * 2 * F1]) for u in range(2)]
        parts = [sb(f"parts{u}", [P, KD, 2, 2 * F1], F16) for u in range(2)]
        peak = [sb(f"peak{u}", [P, 1]) for u in range(2)]
        peaks = [sb(f"peaks{u}", [P, P]) for u in range(2)]
        top_peak, guarded, rpeak, w_scale = (sb(n, [P, 1]) for n in ("top_peak", "guarded", "rpeak", "w_scale"))
        stage_in = [sem(f"c_stage{u}") for u in range(2)]
        peak_in = [sem(f"c_peaks{u}") for u in range(2)]
        parts_stored = [sem(f"c_stored{u}") for u in range(2)]
        peak_ready, peak_waits, peak_out, scaled = sem("c_peak"), sem("c_peak_waits"), sem("c_peak_out"), sem("c_scaled")
        parts_hi, parts_ready = sem("c_parts_hi"), sem("c_parts")
        block = ctx.enter_context(nc.Block())
        W = T * E0 // RC

        @block.sync
        def _(sp):
            sp.dma_start(top.descending[:, :], dram["desc0"]).then_inc(r_in, 16)
            sp.dma_start(tri[:, :], dram["tri"]).then_inc(r_in, 16)
            sp.dma_start(ones[:, :], dram["ones"]).then_inc(r_in, 16)
            sp.dma_start(w2[:, :, :], dram["w2T"].rearrange("(k p) n -> p k n", p=P)).then_inc(w_in, 16)
            sp.dma_start(b2[:, :], dram["b2"]).then_inc(w_in, 16)

            def weights(e, u):
                if not isinstance(e, int) or e < E1:
                    wait(sp, parts_ready, e - 1)
                    sp.dma_start(stage[u][:, :], dram["eW1"][:, ds(e, 1), :].rearrange("p e n -> p (e n)")
                                 ).then_inc(stage_in[u], 16)
                if not isinstance(e, int) or e > 0:
                    sp.wait_ge(parts_ready, e)
                    sp.dma_start(dram["w1_parts"][:, ds(e - 1, 1), :].rearrange("p e n -> p (e n)"),
                                 parts[1 - u][:, :, :, :].rearrange("p k h n -> p (k h n)")
                                 ).then_inc(parts_stored[1 - u], 16)

            steps(sp, weights, 2, E1, E1 + 1)
            sp.wait_ge(r_in, 48)
            sp.wait_ge(w_in, 32)
            for u in range(2):
                sp.wait_ge(parts_stored[u], 8 * E1)

        @block.gpsimd
        def _(pool):
            def share_peak(e, u):
                settled(pool, peak_waits, (peak_ready, e + 1))
                pool.dma_start(dram["peaks"][ds(e, 1), :].rearrange("e p -> p e"), peak[u][:, :]).then_inc(peak_out, 16)
                settled(pool, peak_waits, (peak_out, 16 * (e + 1)))
                pool.dma_start(peaks[u][:, :], dram["peaks"][ds(e, 1), :].to_broadcast([P, P])).then_inc(peak_in[u], 16)

            steps(pool, share_peak, 2, E1, E1)

        @block.tensor
        def _(pe):
            def hidden_part(c, u, m):
                b = m // 2
                if m % 2 == 0:
                    wait(pe, active, MF * c + m - 2)
                for k in range(KD):
                    mm = nc.tensor.matmul(psH[b % 2][:, (m % 2) * CH:(m % 2 + 1) * CH], w1[:, k, m * P:(m + 1) * P],
                                          HT[:, k, ds(c * CH, CH)], start=(k == 0), stop=(k == KD - 1))
                mm.then_inc(hidden, 1)

            def output_part(c, u, s):
                pe.wait_ge(active, MF * (c + 1))
                wait(pe, y_copied, 2 * c + s - 1)
                for m in range(MF):
                    mm = nc.tensor.matmul(psY[s][:, 0:D], G[u][:, m, s * P:(s + 1) * P], w2[:, m, :],
                                          start=(m == 0), stop=(m == MF - 1))
                mm.then_inc(y_done, 1)

            def iteration(c, u):
                if not isinstance(c, int) or c < NCH:
                    for m in range(MF):
                        hidden_part(c, u, m)
                if not isinstance(c, int) or c > 0:
                    for s in range(2):
                        output_part(c - 1, 1 - u, s)

            pe.wait_ge(w1_in, 32)
            iteration(0, 0)
            pe.wait_ge(w_in, 32)
            iteration(1, 1)
            for c in range(2, 6):
                iteration(c, c % 2)
            pe.wait_ge(r_in, 48)
            pe.wait_ge(chosen_ready, 1)
            for stationary in (tri, ones):
                if stationary is ones:
                    pe.wait_ge(before_ready, 1)
                for c in range(RC):
                    flat = chosen[:, :, :].rearrange("p t e -> p (t e)")
                    mm = nc.tensor.matmul(psC[:, c, 0:W], stationary[:, :], flat[:, c * W:(c + 1) * W],
                                          start=True, stop=True)
                mm.then_inc(counted, 1)
            with pe.Fori(6, NCH - 2, 2) as c:
                for u in range(2):
                    iteration(c + u, u)
            for c in range(NCH - 1, NCH + 1):
                iteration(c, c % 2)

        @block.scalar
        def _(act):
            def iteration(c, u):
                for m in range(MF):
                    act.wait_ge(hidden, MF * c + (m // 2 + 1) * 2)
                    if m == 0:
                        wait(act, y_done, 2 * (c - 1))
                    nc.scalar.activation(G[u][:, m, :], psH[m // 2 % 2][:, (m % 2) * CH:(m % 2 + 1) * CH], ACT.Gelu,
                                         bias=b1[:, m:m + 1]).then_inc(active, 1)

            def take(c):
                for s in range(2):
                    act.wait_ge(y_done, 2 * c + s + 1)
                    nc.scalar.copy(Y[:, c * 2 + s, :], psY[s][:, 0:D]).then_inc(y_copied, 1)

            act.wait_ge(w1_in, 32)
            iteration(0, 0)
            iteration(1, 1)
            take(0)
            act.wait_ge(exp_in, 1)
            nc.scalar.activation(top.rest[:, :, :], top.rest[:, :, :], ACT.Exp).then_inc(exp_out, 1)
            act.wait_ge(exp_in, 2)
            nc.scalar.activation(e2[:, :], held[:, :], ACT.Exp).then_inc(exp_out, 1)
            with act.Fori(2, NCH - 2, 2) as c:
                for u in range(2):
                    iteration(c + u, u)
                    take(c + u - 1)
            iteration(NCH - 1, (NCH - 1) % 2)
            take(NCH - 2)
            take(NCH - 1)

        @block.vector
        def _(dve):
            v = nc.vector
            step = Chain(dve, chain)
            full = [P, T, E0]
            dve.wait_ge(r_in, 48)
            top.steps(step, L)
            step(v.tensor_tensor(top.score[:, :, :], top.one_hot[0][:, :, :], top.one_hot[1][:, :, :], ALU.add))
            v.tensor_copy(chosen[:, :, :], top.score[:, :, :]).then_inc(chosen_ready, 1)
            v.tensor_tensor(top.rest[:, :, :], L[:, :, :], wide(top.best[0][:, :], full),
                            ALU.subtract).then_inc(exp_in, 1)
            v.tensor_tensor(held[:, :], top.best[1][:, :], top.best[0][:, :], ALU.subtract).then_inc(exp_in, 1)
            def peak_of(e, u):
                dve.wait_ge(stage_in[u], 8 * (e - u) + 16)
                v.tensor_reduce(peak[u][:, :], stage[u][:, :], AX_X, ALU.max,
                                apply_absolute_value=True).then_inc(peak_ready, 1)

            def split(e, u):
                dve.wait_ge(peak_in[u], 8 * (e - u) + 16)
                v.tensor_reduce(top_peak[:, :], peaks[u][:, :], AX_X, ALU.max).then_inc(scaled, 1)
                dve.wait_ge(scaled, 5 * e + 1)
                v.tensor_scalar(guarded[:, :], top_peak[:, :], 1e-30, None, ALU.max).then_inc(scaled, 1)
                dve.wait_ge(scaled, 5 * e + 2)
                v.tensor_scalar(t["w_unscale"][:, ds(e, 1)], guarded[:, :], 1.0 / (W_PEAK * H_SCALE), None,
                                ALU.mult).then_inc(scaled, 1)
                v.reciprocal(rpeak[:, :], guarded[:, :]).then_inc(scaled, 1)
                dve.wait_ge(scaled, 5 * e + 4)
                v.tensor_scalar(w_scale[:, :], rpeak[:, :], W_PEAK, None, ALU.mult).then_inc(scaled, 1)
                dve.wait_ge(scaled, 5 * e + 5)
                if not isinstance(e, int) or e > 1:
                    dve.wait_ge(parts_stored[u], 8 * (e - 2 - u) + 16)
                rows = stage[u][:, :].rearrange("p (k n) -> p k n", k=KD)
                v.tensor_scalar(parts[u][:, :, 0, :], rows, w_scale[:, :], None, ALU.mult).then_inc(parts_hi, 1)
                dve.wait_ge(parts_hi, e + 1)
                v.scalar_tensor_tensor(parts[u][:, :, 1, :], rows, w_scale[:, :], parts[u][:, :, 0, :], ALU.mult,
                                       ALU.subtract).then_inc(parts_ready, 1)

            def weights(e, u):
                if not isinstance(e, int) or e > 0:
                    split(e - 1, 1 - u)
                if not isinstance(e, int) or e < E1:
                    peak_of(e, u)

            for e in range(4):
                weights(e, e % 2)
            dve.wait_ge(exp_out, 2)
            step(v.tensor_reduce(z[:, :], top.rest[:, :, :], AX_X, ALU.add))
            step(v.reciprocal(share[0][:, :], z[:, :]))
            step(v.tensor_tensor(share[1][:, :], e2[:, :], share[0][:, :], ALU.mult))
            dve.wait_ge(counted, 1)
            flat = lambda x: x[:, :, :].rearrange("p t e -> p (t e)").rearrange("p (c w) -> p c w", c=RC)
            v.tensor_copy(flat(before), psC[:, :, 0:W]).then_inc(before_ready, 1)
            dve.wait_ge(counted, 2)
            step(v.tensor_copy(flat(sums[0]), psC[:, :, 0:W]))
            a, b, reach = sums[0], sums[1], 1
            while reach < T:
                step(v.tensor_copy(b[:, 0:reach, :], a[:, 0:reach, :]))
                step(v.tensor_tensor(b[:, reach:T, :], a[:, reach:T, :], a[:, 0:T - reach, :], ALU.add))
                a, b, reach = b, a, 2 * reach
            step(v.tensor_tensor(before[:, 1:T, :], before[:, 1:T, :], a[:, 0:T - 1, :], ALU.add))
            for k in range(2):
                step(v.tensor_tensor(top.score[:, :, :], before[:, :, :], top.one_hot[k][:, :, :], ALU.mult))
                step(v.tensor_reduce(held[:, :], top.score[:, :, :], AX_X, ALU.add))
                step(v.scalar_tensor_tensor(share[k][:, :], held[:, :], float(CAP), share[k][:, :], ALU.is_lt,
                                            ALU.mult))
            step(v.tensor_tensor(gate[:, :], share[0][:, :], share[1][:, :], ALU.add))


            def residual(first, count):
                tiles = [first + n for n in range(count)]
                for i in tiles:
                    dve.wait_ge(y_copied, i + 1)
                    v.tensor_tensor(Y[:, i, :], Y[:, i, :], b2[:, :], ALU.add).then_inc(biased, 1)
                for i in tiles:
                    dve.wait_ge(biased, i + 1)
                    v.scalar_tensor_tensor(X[:, i, :], Y[:, i, :], gate[:, ds(i, 1)], X[:, i, :], ALU.mult,
                                           ALU.add).then_inc(x_ready, 1)
                for i in tiles:
                    dve.wait_ge(x_ready, i + 1)
                    v.bn_stats(t["stats"][:, i, :], X[:, i, :]).then_inc(stats_done, 1)

            dve.wait_ge(w_in, 32)
            RES = 3
            with dve.Fori(4, E1 - 1, 2) as e:
                for u in range(2):
                    weights(e + u, u)
                    residual((e + u - 4) * RES, RES)
            weights(E1, E1 % 2)
            with dve.Fori((E1 - 4) * RES, T - 1, 2) as i:
                residual(i, 2)




def tile_pairs(eng, body, first, last, total):
    for t in range(0, first, 2):
        body(t)
    with eng.Fori(first, last - 1, 2) as t:
        body(t)
    for t in range(last, total, 2):
        body(t)


def mean_aggregation(nc, t, dram):
    with ExitStack() as ctx:
        sb = lambda n, s, d=F32: ctx.enter_context(nc.sbuf_tensor(n, s, d))
        sem = semaphores(nc, ctx)
        X, H, own, ident = t["X"], t["H"], t["own"], t["ident"]
        stats_done = sem("d_stats")
        adjf = t["adjTf"]
        adjh = [sb(f"adjTh{u}", [P, NP], F16) for u in range(2)]
        Wn = sb("Wn", [P, KD, D])
        degree = [sb(f"degree{u}", [P, 1]) for u in range(2)]
        rdegree = [sb(f"rdegree{u}", [P, 1]) for u in range(2)]
        agg = [sb(f"mean{u}", [P, D]) for u in range(2)]
        aggT = [sb(f"meanT{u}", [P, KD, P]) for u in range(2)]
        out = [sb(f"summed{u}", [P, D]) for u in range(2)]
        one_hot, best, slot_f, running = t["one_hot"], t["best"], t["slot_f"], t["running"]
        row_stats = [sb(f"row_stats{u}", [P, 6]) for u in range(2)]
        moments = sb("moments", [P, 2, 2])
        eps, std = sb("eps", [P, 1]), sb("std", [P, 2])
        mean, rstd = sb("mean_all", [P, T]), sb("rstd_all", [P, T])
        h = [sb(f"h_r{u}", [P, D]) for u in range(2)]
        hT = sb("hT_r", [P, 2, KD, P])
        rows = [sb(f"rows{u}", [P, 2, D + 1]) for u in range(2)]
        places = sb("places", [P, T, 2])
        Wg, bg = sb("Wg", [P, KD, E1]), sb("bg", [P, 2, E1])
        descending, region = sb("descending", [P, 2, E1]), sb("region", [P, 2, E1])
        logits, score, rest, place = (sb(n, [P, 2, E1]) for n in ("logits", "score", "rest", "place"))
        rank = sb("rank", [P, 2])
        placed = sb("placed", [P, 2, 2, E1])
        chosen = sb("chosen1", [P, 2, E1], F16)
        tri, ones = sb("tri1", [P, P], F16), t["ones"]
        slot_i = sb("slot_i", [P, 2, 2], I32)
        ps = lambda n: ctx.enter_context(nc.psum_tensor(n, [P, 512], F32))
        acc = [ps(f"sum{u}") for u in range(2)]
        psA = [ps(f"psM{u}") for u in range(2)]
        psF = [ps(f"psN{u}") for u in range(2)]
        psH, psR = ps("psH_r"), ps("psR_r")
        adj_in, W1_in = t["adj_in"], t["W1_in"]
        w_in, half_ready, ones_set = sem("d_w"), sem("d_half"), sem("d_ones")
        acc_ready, deg_ready, rdeg_ready, agg_ready = sem("d_acc"), sem("d_deg"), sem("d_rdeg"), sem("d_agg")
        turned, aggT_ready, proj_ready, out_ready, x_ready = (sem("d_turned"), sem("d_aggT"), sem("d_proj"),
                                                              sem("d_out"), sem("d_x"))
        moment_waits, moments_ready, std_ready, rstd_ready = (sem("d_moment_waits"), sem("d_moments"), sem("d_std"),
                                                              sem("d_rstd"))
        h_ready, h_turned, hT_ready, logits_done = sem("d_h"), sem("d_h_turned"), sem("d_hT"), sem("d_logits")
        logits_taken, chain, chosen_ready, counted = (sem("d_taken"), sem("d_chain"), sem("d_chosen"), sem("d_counted"))
        placed_ready = sem("d_placed")
        counts_taken, rows_ready, scatter_waits, scattered = (sem("d_counts_taken"), sem("d_rows"),
                                                              sem("d_scatter_waits"), sem("d_scattered"))
        block = ctx.enter_context(nc.Block())
        adjv = dram["adjT"]
        FIRST, LAST, TOTAL = 6, T, T + 6

        def live(t):
            return not isinstance(t, int) or 0 <= t < T

        @block.sync
        def _(sp):
            sp.dma_start(Wn[:, :, :], dram["WnT"].rearrange("(k p) n -> p k n", p=P)).then_inc(w_in, 16)
            sp.dma_start(Wg[:, :, :], dram["Wg"].rearrange("(k p) n -> p k n", p=P)).then_inc(w_in, 16)
            for to, name in ((bg, "bg"), (descending, "desc1"), (region, "region"), (tri, "tri"), (ones, "ones"),
                             (places, "places")):
                sp.dma_start(to[...], dram[name]).then_inc(w_in, 16)

            def load_pair(i, with_weights):
                for u in range(2):
                    if not (isinstance(i, int) and i + u < 2):
                        wait(sp, half_ready, i + u - 1)
                        sp.dma_start(adjf[u][:, :], adjv[i + u, :, :]).then_inc(adj_in[u], 16)
                if with_weights:
                    flat = t["W1"][:, :, :, :, :].rearrange("p e k h n -> p (e k h n)")
                    part = KD * 2 * 2 * F1
                    sp.dma_start(flat[:, ds(i * (part // 2), part)],
                                 dram["w1_parts"].rearrange("p e n -> p (e n)")[:, ds(i * (part // 2), part)]
                                 ).then_inc(W1_in, 16)

            load_pair(0, True)
            with sp.Fori(2, 2 * E1 - 1, 2) as i:
                load_pair(i, True)
            with sp.Fori(2 * E1, T - 1, 2) as i:
                load_pair(i, False)
            sp.wait_ge(w_in, 16 * 8)
            sp.wait_ge(W1_in, 16 * E1)

        @block.scalar
        def _(act):
            def half(t, u):
                act.wait_ge(adj_in[u], 8 * (t - u) + 16)
                wait(act, acc_ready, t - 1)
                nc.scalar.copy(adjh[u][:, :], adjf[u][:, :]).then_inc(half_ready, 1)

            def mean_back(t, u):
                act.wait_ge(turned, t + 1)
                wait(act, proj_ready, t - 1)
                nc.scalar.copy(aggT[u][:, :, :].rearrange("p k n -> p (k n)"), psA[u][:, 0:D]).then_inc(aggT_ready, 1)

            def body(i):
                if live(i):
                    half(i, 0)
                if live(i - 2):
                    mean_back(i - 2, 0)
                if live(i - 4):
                    act.wait_ge(moments_ready, i - 2)
                    nc.scalar.activation(std[:, :], moments[:, :, 1], ACT.Sqrt, bias=eps[:, :]).then_inc(std_ready, 2)
                if live(i):
                    half(i + 1, 1)
                if live(i - 2):
                    mean_back(i - 1, 1)
                if live(i - 4):
                    act.wait_ge(h_turned, i - 2)
                    wait(act, logits_done, i - 4)
                    nc.scalar.copy(hT[:, :, :, :].rearrange("p u k n -> p (u k n)"), psH[:, :]).then_inc(hT_ready, 2)

            act.wait_ge(ones_set, 1)
            tile_pairs(act, body, FIRST, LAST, TOTAL)

        @block.tensor
        def _(pe):
            def products(t, u):
                pe.wait_ge(half_ready, t + 1)
                wait(pe, agg_ready, t - 1)
                for j in range(T):
                    left = adjh[u][:, j * P:(j + 1) * P]
                    nc.tensor.matmul(acc[u][:, 0:D + 1], left, H[:, j, 0:D + 1], start=(j == 0), stop=False,
                                     skip_group_check=True)
                    mm = nc.tensor.matmul(acc[u][:, 0:D], left, H[:, j, D + 2:2 * D + 2], start=False, stop=(j == T - 1),
                                          skip_group_check=True)
                mm.then_inc(acc_ready, 1)

            def turn_mean(t, u):
                pe.wait_ge(agg_ready, t + 1)
                wait(pe, aggT_ready, t - 1)
                for k in range(KD):
                    mm = nc.tensor.transpose(psA[u][:, k * P:(k + 1) * P], agg[u][:, k * P:(k + 1) * P], ident[:, :])
                mm.then_inc(turned, 1)

            def project(t, u):
                pe.wait_ge(aggT_ready, t + 1)
                wait(pe, out_ready, t - 1)
                for k in range(KD):
                    mm = nc.tensor.matmul(psF[u][:, 0:D], aggT[u][:, k, :], Wn[:, k, :], start=(k == 0),
                                          stop=(k == KD - 1))
                mm.then_inc(proj_ready, 1)

            def turn_rows(i):
                pe.wait_ge(h_ready, i + 2)
                wait(pe, hT_ready, i)
                for u in range(2):
                    for k in range(KD):
                        mm = nc.tensor.transpose(psH[:, (u * KD + k) * P:(u * KD + k + 1) * P],
                                                 h[u][:, k * P:(k + 1) * P], ident[:, :])
                mm.then_inc(h_turned, 2)

            def route(i):
                pe.wait_ge(hT_ready, i + 2)
                wait(pe, logits_taken, i)
                wait(pe, counts_taken, i - 2)
                for u in range(2):
                    for k in range(KD):
                        mm = nc.tensor.matmul(psR[:, u * E1:(u + 1) * E1], hT[:, u, k, :], Wg[:, k, :], start=(k == 0),
                                              stop=(k == KD - 1))
                mm.then_inc(logits_done, 2)

            def count(i):
                pe.wait_ge(chosen_ready, i + 2)
                for u in range(2):
                    terms = [(tri, chosen[:, u, :]), (ones, running[:, :])] + [(ones, chosen[:, 0, :])] * u
                    for n, (left, right) in enumerate(terms):
                        mm = nc.tensor.matmul(psR[:, (2 + u) * E1:(3 + u) * E1], left[:, :], right, start=(n == 0),
                                              stop=(n == len(terms) - 1))
                mm.then_inc(counted, 2)

            def body(i):
                if live(i):
                    products(i, 0)
                if isinstance(i, int) and i == 0:
                    pe.wait_ge(w_in, 16 * 8)
                if live(i - 2):
                    turn_mean(i - 1, 1)
                    project(i - 2, 0)
                if live(i - 4):
                    turn_rows(i - 4)
                if live(i):
                    products(i + 1, 1)
                    turn_mean(i, 0)
                if live(i - 2):
                    project(i - 1, 1)
                if live(i - 4):
                    route(i - 4)
                if live(i - 6):
                    count(i - 6)

            pe.wait_ge(ones_set, 3)
            tile_pairs(pe, body, FIRST, LAST, TOTAL)

        @block.vector
        def _(dve):
            v = nc.vector
            v.memset(eps[:, :], EPS).then_inc(ones_set, 1)
            v.memset(H[:, :, D:D + 1], 1.0).then_inc(ones_set, 1)
            v.memset(running[:, :], 0.0).then_inc(ones_set, 1)

            def aggregate(t, u):
                dve.wait_ge(acc_ready, t + 1)
                v.tensor_scalar(degree[u][:, :], acc[u][:, D:D + 1], EPS, None, ALU.add).then_inc(deg_ready, 1)
                dve.wait_ge(deg_ready, t + 1)
                v.reciprocal(rdegree[u][:, :], degree[u][:, :]).then_inc(rdeg_ready, 1)
                dve.wait_ge(rdeg_ready, t + 1)
                wait(dve, turned, t - 1)
                v.tensor_scalar(agg[u][:, :], acc[u][:, 0:D], rdegree[u][:, :], 1.0 / H_SCALE, ALU.mult,
                                ALU.mult).then_inc(agg_ready, 1)

            def residual(t, u):
                dve.wait_ge(proj_ready, t + 1)
                wait(dve, x_ready, t - 1)
                v.tensor_tensor(out[u][:, :], psF[u][:, 0:D], own[:, t, :], ALU.add).then_inc(out_ready, 1)
                dve.wait_ge(out_ready, t + 1)
                v.scalar_tensor_tensor(X[:, t, :], out[u][:, :], 0.0, X[:, t, :], ALU.max, ALU.add).then_inc(x_ready, 1)

            def normalise(to, t):
                return v.tensor_scalar(to, X[:, t, :], mean[:, ds(t, 1)], rstd[:, ds(t, 1)], ALU.subtract,
                                       ALU.mult)

            def row_norm(i):
                for u in range(2):
                    settled(dve, moment_waits, (x_ready, i + u + 1), (moments_ready, i))
                    v.bn_stats(row_stats[u][:, :], X[:, i + u, :]).then_inc(stats_done, 1)
                for u in range(2):
                    settled(dve, moment_waits, (stats_done, i + u + 1), (rstd_ready, 2 * i))
                    v.bn_aggr(moments[:, u, :], row_stats[u][:, :]).then_inc(moments_ready, 1)
                dve.wait_ge(moments_ready, i + 2)
                v.tensor_copy(mean[:, ds(i, 2)], moments[:, :, 0]).then_inc(rstd_ready, 2)
                dve.wait_ge(std_ready, i + 2)
                v.reciprocal(rstd[:, ds(i, 2)], std[:, :]).then_inc(rstd_ready, 2)
                dve.wait_ge(rstd_ready, 2 * i + 4)
                wait(dve, h_turned, i)
                for u in range(2):
                    normalise(h[u][:, :], i + u).then_inc(h_ready, 1)

            STEPS = 10

            def two_best(i):
                at = i * (STEPS // 2)
                done = [0]

                def step(instruction):
                    done[0] += 1
                    instruction.then_inc(chain, 1)
                    dve.wait_ge(chain, at + done[0])

                pair = [P, 2, E1]
                dve.wait_ge(logits_done, i + 2)
                v.tensor_tensor(logits[:, :, :].rearrange("p u e -> p (u e)"), psR[:, 0:2 * E1],
                                bg[:, :, :].rearrange("p u e -> p (u e)"), ALU.add).then_inc(logits_taken, 2)
                dve.wait_ge(logits_taken, i + 2)
                for k in range(2):
                    src = (logits, rest)[k]
                    largest, hot = best[:, k, ds(i, 2)], one_hot[:, k, ds(i, 2), :]
                    step(v.tensor_reduce(largest, src[:, :, :], AX_X, ALU.max))
                    step(v.tensor_tensor(score[:, :, :], src[:, :, :], wide(largest, pair), ALU.is_equal))
                    step(v.tensor_tensor(score[:, :, :], score[:, :, :], descending[:, :, :], ALU.mult))
                    step(v.tensor_reduce(rank[:, :], score[:, :, :], AX_X, ALU.max))
                    if k == 0:
                        step(v.tensor_tensor(hot, score[:, :, :], wide(rank[:, :], pair), ALU.is_equal))
                        v.scalar_tensor_tensor(rest[:, :, :], hot, -FAR * FAR, logits[:, :, :], ALU.mult,
                                               ALU.add).then_inc(chain, 1)
                        dve.wait_ge(chain, at + 6)
                        done[0] = 6
                    else:
                        v.tensor_tensor(hot, score[:, :, :], wide(rank[:, :], pair), ALU.is_equal).then_inc(chosen_ready, 1)
                dve.wait_ge(chosen_ready, i + 1)
                wait(dve, counts_taken, i)
                v.tensor_tensor(chosen[:, :, :], one_hot[:, 0, ds(i, 2), :], one_hot[:, 1, ds(i, 2), :],
                                ALU.add).then_inc(chosen_ready, 1)

            def write_slots(i):
                dve.wait_ge(counted, i + 2)
                v.tensor_tensor(place[:, :, :].rearrange("p u e -> p (u e)"), psR[:, 2 * E1:4 * E1],
                                region[:, :, :].rearrange("p u e -> p (u e)"), ALU.add).then_inc(placed_ready, 1)
                v.tensor_tensor(running[:, :], running[:, :], chosen[:, 0, :], ALU.add).then_inc(placed_ready, 1)
                dve.wait_ge(placed_ready, 3 * i + 2)
                v.tensor_tensor(running[:, :], running[:, :], chosen[:, 1, :], ALU.add).then_inc(counts_taken, 2)
                for k in range(2):
                    v.tensor_tensor(placed[:, k, :, :], place[:, :, :], one_hot[:, k, ds(i, 2), :],
                                    ALU.mult).then_inc(placed_ready, 1)
                dve.wait_ge(placed_ready, 3 * i + 4)
                for k in range(2):
                    v.tensor_reduce(slot_f[:, k, ds(i, 2)], placed[:, k, :, :], AX_X, ALU.add).then_inc(placed_ready, 1)
                wait(dve, scattered, 32 * i)
                for u in range(2):
                    for k in range(2):
                        normalise(rows[u][:, k, 0:D], i + u).then_inc(rows_ready, 1)
                    v.tensor_copy(rows[u][:, :, D], places[:, i + u, :]).then_inc(rows_ready, 1)
                dve.wait_ge(placed_ready, 3 * i + 6)
                v.tensor_copy(slot_i[:, :, :], slot_f[:, :, ds(i, 2)]).then_inc(rows_ready, 2)

            def body(i):
                if live(i):
                    aggregate(i, 0)
                if isinstance(i, int) and i == 0:
                    dve.wait_ge(w_in, 16 * 8)
                if live(i - 2):
                    residual(i - 2, 0)
                if live(i - 6):
                    two_best(i - 6)
                if live(i):
                    aggregate(i + 1, 1)
                if live(i - 2):
                    residual(i - 1, 1)
                    row_norm(i - 2)
                if live(i - 6):
                    write_slots(i - 6)

            tile_pairs(dve, body, FIRST, LAST, TOTAL)

        @block.gpsimd
        def _(pool):
            def body(i):
                settled(pool, scatter_waits, (rows_ready, 4 * i + 8))
                for k in range(2):
                    for u in range(2):
                        pool.indirect_dma_start(out=dram["slot_rows"], in_=rows[u][:, k, :], in_offset=None,
                                                out_offset=bass.IndirectOffsetOnAxis(ap=slot_i[:, k, u:u + 1], axis=0)
                                                ).then_inc(scattered, 16)

            body(0)
            with pool.Fori(2, T - 1, 2) as i:
                body(i)
            pool.wait_ge(scattered, 16 * 2 * T)


def expert_ffn(nc, t, dram):
    with ExitStack() as ctx:
        sb = lambda n, s, d=F32: ctx.enter_context(nc.sbuf_tensor(n, s, d))
        sem = semaphores(nc, ctx)
        W1, ident, ones = t["W1"], t["ident"], t["ones"]
        W2 = sb("W2", [P, E1, KF, D])
        best, share = t["best"], t["share"]
        expert, source = sb("expert", [P, NS], I32), sb("source", [P, NS], I32)
        limits, over = sb("limits", [P, E1, T]), sb("over", [P, E1, T])
        tile_no, passed = sb("tile_no", [P, NS, E1]), sb("passed", [P, NS, E1])
        tile_f, expert_f, shift = (sb(n, [P, NS]) for n in ("tile_f", "expert_f", "shift"))
        totals, tiles, move = (sb(n, [P, E1]) for n in ("totals", "tiles", "move"))
        ends = [sb(f"ends{k}", [P, E1]) for k in range(2)]
        kept = sb("kept", [P, NS])
        place = [sb(f"place{u}", [P, 1], I32) for u in range(2)]
        gap, grown, denominator = sb("gap", [P, T]), sb("odds", [P, T]), sb("denominator", [P, T])
        b1 = sb("eb1", [P, E1, 2 * F1])
        b2 = sb("eb2", [P, E1, D])
        xs = [sb(f"xs{u}", [P, D + 1]) for u in range(2)]
        xT_hi = [sb(f"xT_hi{u}", [P, KD, P], F16) for u in range(2)]
        xT_lo = [sb(f"xT_lo{u}", [P, KD, P], F16) for u in range(2)]
        hb = [sb(f"hb{u}", [P, 2 * F1]) for u in range(2)]
        silu = [sb(f"silu{u}", [P, F1]) for u in range(2)]
        act_sb = [sb(f"act{u}", [P, F1]) for u in range(2)]
        actT = [sb(f"actT{u}", [P, KF, P]) for u in range(2)]
        ys = [sb(f"ys{u}", [P, D]) for u in range(2)]
        ps = lambda n, w: ctx.enter_context(nc.psum_tensor(n, [P, w], F32))
        psH = [ps(f"ePsH{u}", 2 * F1) for u in range(2)]
        psX, psA = ps("ePsX", 512), ps("ePsA", 512)
        psY = [ps(f"ePsY{u}", 512) for u in range(2)]
        b_in, b2_in = sem("f_b"), sem("f_b2")
        x_in = [sem(f"f_x{u}") for u in range(2)]
        stored = [sem(f"f_stored{u}") for u in range(2)]
        lo_ready, place_kept, place_ready = sem("f_lo"), sem("f_kept"), sem("f_place")
        x_turned, hi_ready, h_ready, hb_ready, silu_ready, act_ready = (sem("f_xt"), sem("f_xT"), sem("f_h"), sem("f_hb"),
                                                                        sem("f_silu"), sem("f_act"))
        a_turned, actT_ready, y_ready, ys_ready = sem("f_at"), sem("f_aT"), sem("f_y"), sem("f_ys")
        c_in, chain, total_ready, tables_ready = sem("f_in"), sem("f_chain"), sem("f_total"), sem("f_tables")
        gap_ready, grown_ready, W2_in, store_waits = (sem("f_gap"), sem("f_grown"), sem("f_W2"), sem("f_store_waits"))
        block = ctx.enter_context(nc.Block())
        src = dram["slot_rows"].rearrange("(s p) d -> s p d", p=P)
        FIRST, LAST, TOTAL = 4, NS - 3 + (NS - 1) % 2, NS + 3

        def live(s):
            return not isinstance(s, int) or 0 <= s < NS

        def tile_expert(eng, s):
            return eng.value_load(expert[0:1, ds(s, 1)], min_val=0, max_val=E1 - 1)

        @block.sync
        def _(sp):
            for to, name in ((limits, "limits"), (tile_no, "tile_no"), (tile_f, "tile_f")):
                sp.dma_start(to[...], dram[name]).then_inc(c_in, 16)
            sp.dma_start(b1[:, :, :], dram["eb1"]).then_inc(b_in, 16)
            sp.wait_ge(tables_ready, 2)

            def load(s, u):
                row_tile = sp.value_load(source[0:1, ds(s, 1)], min_val=0, max_val=SLOT_TILES - 1)
                wait(sp, x_turned, s - 1)
                wait(sp, place_kept, s - 1)
                sp.dma_start(xs[u][:, :], src[ds(row_tile, 1), :, :].rearrange("s p d -> p (s d)")
                             ).then_inc(x_in[u], 16)

            steps(sp, load, 2, NS - 1, NS)
            sp.wait_ge(c_in, 48)

        @block.gpsimd
        def _(pool):
            def store(s, u):
                settled(pool, store_waits, (ys_ready, s + 1), (place_ready, s + 1))
                if not isinstance(s, int) or s > 0:
                    settled(pool, store_waits, (stored[1 - u], 8 * (s + u)))
                pool.indirect_dma_start(out=dram["results"], in_=ys[u][:, :], in_offset=None,
                                        out_offset=bass.IndirectOffsetOnAxis(ap=place[u][:, 0:1], axis=0)
                                        ).then_inc(stored[u], 16)

            steps(pool, store, 2, NS - 1, NS)
            for u in range(2):
                pool.wait_ge(stored[u], 16 * ((NS + 1 - u) // 2))

        @block.tensor
        def _(pe):
            def turn_rows(s, u):
                pe.wait_ge(x_in[u], 8 * (s - u) + 16)
                wait(pe, lo_ready, s)
                for k in range(KD):
                    mm = nc.tensor.transpose(psX[:, k * P:(k + 1) * P], xs[u][:, k * P:(k + 1) * P], ident[:, :])
                mm.then_inc(x_turned, 1)

            def iteration(s, u):
                if live(s):
                    e = tile_expert(pe, s)
                    pe.wait_ge(lo_ready, s + 1)
                    wait(pe, hb_ready, s - 1)
                    terms = [(left, k, part) for left, part in ((xT_hi, 0), (xT_hi, 1), (xT_lo, 0)) for k in range(KD)]
                    for n in range(2):
                        for m, (left, k, part) in enumerate(terms):
                            mm = nc.tensor.matmul(psH[u][:, n * F1:(n + 1) * F1], left[u][:, k, :],
                                                  W1[:, e, k, part, n * F1:(n + 1) * F1], start=(m == 0),
                                                  stop=(m == len(terms) - 1))
                    mm.then_inc(h_ready, 1)
                if live(s + 1):
                    turn_rows(s + 1, 1 - u)
                if live(s - 1):
                    pe.wait_ge(act_ready, s)
                    wait(pe, actT_ready, s - 1)
                    for k in range(KF):
                        mm = nc.tensor.transpose(psA[:, k * P:(k + 1) * P], act_sb[1 - u][:, k * P:(k + 1) * P],
                                                 ident[:, :])
                    mm.then_inc(a_turned, 1)
                if live(s - 2):
                    e = tile_expert(pe, s - 2)
                    if isinstance(s, int) and s == 2:
                        pe.wait_ge(W2_in, 16)
                    pe.wait_ge(actT_ready, s - 1)
                    wait(pe, ys_ready, s - 3)
                    for k in range(KF):
                        mm = nc.tensor.matmul(psY[u][:, 0:D], actT[u][:, k, :], W2[:, e, k, :], start=(k == 0),
                                              stop=(k == KF - 1))
                    mm.then_inc(y_ready, 1)

            nc.tensor.matmul(psY[0][:, 0:E1], ones[:, :], t["running"][:, :], start=True,
                             stop=True).then_inc(total_ready, 1)
            pe.wait_ge(tables_ready, 2)
            turn_rows(0, 0)
            steps(pe, iteration, FIRST, LAST, TOTAL)

        @block.scalar
        def _(act):
            def rows_back(s, u):
                act.wait_ge(x_turned, s + 1)
                wait(act, h_ready, s - 1)
                nc.scalar.activation(xT_hi[u][:, :, :].rearrange("p k n -> p (k n)"), psX[:, 0:D], ACT.Copy,
                                     scale=H_SCALE).then_inc(hi_ready, 1)

            def iteration(s, u):
                if live(s + 1):
                    rows_back(s + 1, 1 - u)
                if live(s - 1):
                    act.wait_ge(a_turned, s)
                    wait(act, y_ready, s - 3)
                    nc.scalar.copy(actT[1 - u][:, :, :].rearrange("p k n -> p (k n)"), psA[:, :]).then_inc(actT_ready, 1)
                if live(s):
                    act.wait_ge(hb_ready, s + 1)
                    wait(act, act_ready, s - 1)
                    nc.scalar.activation(silu[u][:, :], hb[u][:, 0:F1], ACT.Silu).then_inc(silu_ready, 1)

            act.wait_ge(c_in, 48)
            act.wait_ge(b_in, 16)
            act.dma_start(W2[:, :, :, :], dram["eW2"]).then_inc(W2_in, 16)
            act.dma_start(b2[:, :, :], dram["eb2"]).then_inc(b2_in, 16)
            act.wait_ge(gap_ready, 1)
            nc.scalar.activation(grown[:, :], gap[:, :], ACT.Exp).then_inc(grown_ready, 1)
            rows_back(0, 0)
            steps(act, iteration, FIRST, LAST, TOTAL)
            act.wait_ge(W2_in, 16)
            act.wait_ge(b2_in, 16)

        @block.vector
        def _(dve):
            v = nc.vector

            def rows_lo(s, u):
                dve.wait_ge(hi_ready, s + 1)
                v.tensor_copy(kept[:, ds(s, 1)], xs[u][:, D:D + 1]).then_inc(place_kept, 1)
                wait(dve, h_ready, s - 1)
                v.scalar_tensor_tensor(xT_lo[u][:, :, :].rearrange("p k n -> p (k n)"), psX[:, 0:D], H_SCALE,
                                       xT_hi[u][:, :, :].rearrange("p k n -> p (k n)"), ALU.mult,
                                       ALU.subtract).then_inc(lo_ready, 1)

            def iteration(s, u):
                if live(s):
                    e = tile_expert(dve, s)
                    dve.wait_ge(h_ready, s + 1)
                    wait(dve, act_ready, s - 1)
                    v.scalar_tensor_tensor(hb[u][:, :], psH[u][:, :], t["w_unscale"][:, ds(e, 1)], b1[:, e, :], ALU.mult,
                                           ALU.add).then_inc(hb_ready, 1)
                if live(s + 1):
                    rows_lo(s + 1, 1 - u)
                if live(s):
                    dve.wait_ge(silu_ready, s + 1)
                    wait(dve, a_turned, s - 1)
                    v.tensor_tensor(act_sb[u][:, :], silu[u][:, :], hb[u][:, F1:2 * F1], ALU.mult).then_inc(act_ready, 1)
                if live(s - 2):
                    e = tile_expert(dve, s - 2)
                    dve.wait_ge(y_ready, s - 1)
                    if isinstance(s, int) and s == 2:
                        dve.wait_ge(b2_in, 16)
                    if live(s - 4):
                        dve.wait_ge(stored[u], 8 * (s - 4 - u) + 16)
                    dve.wait_ge(place_kept, s - 1)
                    v.tensor_copy(place[u][:, :], kept[:, ds(s - 2, 1)]).then_inc(place_ready, 1)
                    v.tensor_tensor(ys[u][:, :], psY[u][:, 0:D], b2[:, e, :], ALU.add).then_inc(ys_ready, 1)

            step = Chain(dve, chain)
            v.tensor_tensor(gap[:, :], best[:, 1, :], best[:, 0, :], ALU.subtract).then_inc(gap_ready, 1)
            dve.wait_ge(c_in, 48)
            dve.wait_ge(total_ready, 1)
            step(v.tensor_copy(totals[:, :], psY[0][:, 0:E1]))
            step(v.tensor_tensor(over[:, :, :], wide(totals[:, :], [P, E1, T]), limits[:, :, :], ALU.is_gt))
            step(v.tensor_reduce(tiles[:, :], over[:, :, :], AX_X, ALU.add))
            step(v.tensor_copy(ends[0][:, :], tiles[:, :]))
            a, b, reach = ends[0], ends[1], 1
            while reach < E1:
                step(v.tensor_copy(b[:, 0:reach], a[:, 0:reach]))
                step(v.tensor_tensor(b[:, reach:E1], a[:, reach:E1], a[:, 0:E1 - reach], ALU.add))
                a, b, reach = b, a, 2 * reach
            step(v.tensor_tensor(passed[:, :, :], tile_no[:, :, :],
                                 a[:, :].unsqueeze(1).to_broadcast([P, NS, E1]), ALU.is_ge))
            step(v.tensor_reduce(expert_f[:, :], passed[:, :, :], AX_X, ALU.add))
            step(v.tensor_scalar(expert_f[:, :], expert_f[:, :], float(E1 - 1), None, ALU.min))
            v.tensor_copy(expert[:, :], expert_f[:, :]).then_inc(tables_ready, 1)
            step(v.tensor_scalar(move[:, :], tiles[:, :], -1.0, float(T), ALU.mult, ALU.add))
            step(v.tensor_tensor(passed[:, :, :], passed[:, :, :],
                                 move[:, :].unsqueeze(1).to_broadcast([P, NS, E1]), ALU.mult))
            step(v.tensor_reduce(shift[:, :], passed[:, :, :], AX_X, ALU.add))
            step(v.tensor_tensor(shift[:, :], shift[:, :], tile_f[:, :], ALU.add))
            step(v.tensor_scalar(shift[:, :], shift[:, :], float(SLOT_TILES - 1), None, ALU.min))
            v.tensor_copy(source[:, :], shift[:, :]).then_inc(tables_ready, 1)
            dve.wait_ge(tables_ready, 2)
            rows_lo(0, 0)
            dve.wait_ge(b_in, 16)
            steps(dve, iteration, FIRST, LAST, TOTAL)
            dve.wait_ge(grown_ready, 1)
            step(v.tensor_scalar(denominator[:, :], grown[:, :], 1.0, None, ALU.add))
            step(v.reciprocal(share[0][:, :], denominator[:, :]))
            step(v.tensor_tensor(share[1][:, :], grown[:, :], share[0][:, :], ALU.mult))


def combine_and_store(nc, t, dram, out):
    with ExitStack() as ctx:
        sem = semaphores(nc, ctx)
        X, share = t["X"], t["share"]
        results = ctx.enter_context(nc.sbuf_tensor("results", [P, T, 2, D], F32))
        groups = [(n, min(n + 4, T)) for n in range(0, T, 4)]
        fetched = [sem(f"g_fetched{n}") for n in range(len(groups))]
        added, done, stored = sem("g_added"), sem("g_done"), sem("g_stored")
        block = ctx.enter_context(nc.Block())

        @block.scalar
        def _(act):
            src = dram["results"][0:2 * NP, :].rearrange("(k t p) d -> k p t d", k=2, p=P)
            for n, (a, b) in enumerate(groups):
                for k in range(2):
                    act.dma_start(results[:, a:b, k, :], src[k, :, a:b, :]).then_inc(fetched[n], 16)

        @block.vector
        def _(dve):
            for n in range(T):
                if n % 4 == 0:
                    dve.wait_ge(fetched[n // 4], 32)
                for k in range(2):
                    nc.vector.scalar_tensor_tensor(X[:, n, :], results[:, n, k, :], share[k][:, n:n + 1], X[:, n, :],
                                                   ALU.mult, ALU.add).then_inc(added if k == 0 else done, 1)
                    if k == 0:
                        dve.wait_ge(added, n + 1)

        @block.sync
        def _(sp):
            for n in range(T):
                sp.wait_ge(done, n + 1)
                rows = min(P, N - n * P)
                sp.dma_start(out[n * P:n * P + rows, :], X[0:rows, n, :]).then_inc(stored, 16)
            sp.wait_ge(stored, 16 * T)


def gnn_program(nc, dram, out):
    with ExitStack() as ctx:
        sb = lambda n, s, d=F32: ctx.enter_context(nc.sbuf_tensor(n, s, d))
        t = {"X": sb("X", [P, T, D]), "ident": sb("ident", [P, P]), "stats": sb("stats", [P, T, 6])}
        t["adj_in0"] = [ctx.enter_context(nc.semaphore(f"adj_in{u}")) for u in range(2)]
        with ExitStack() as att:
            t["H"] = att.enter_context(nc.sbuf_tensor("H", [P, T, 2 * D], F16))
            sa = lambda n, s, d=F32: att.enter_context(nc.sbuf_tensor(n, s, d))
            t["S1"] = sa("S1", [P, T])
            t["S2row"] = sa("S2row", [P, NP])
            t["adjf"] = [sa(f"adjf{u}", [P, NP]) for u in range(2)]
            attention_scores(nc, t, dram)
            graph_attention(nc, t, dram)
        t["w_unscale"] = sb("w_unscale", [P, E1])
        t["w1_in"] = ctx.enter_context(nc.semaphore("w1_in"))
        with ExitStack() as ffn:
            t["HT"] = ffn.enter_context(nc.sbuf_tensor("HT", [P, KD, NP], F32))
            t["L0"] = ffn.enter_context(nc.sbuf_tensor("L0", [P, T, E0], F32))
            t["w1"] = ffn.enter_context(nc.sbuf_tensor("w1", [P, KD, F0], F32))
            t["b1"] = ffn.enter_context(nc.sbuf_tensor("b1", [P, MF], F32))

            def first_weights(sp):
                sp.dma_start(t["w1"][:, :, :], dram["w1T"].rearrange("(k p) n -> p k n", p=P)).then_inc(t["w1_in"], 16)
                sp.dma_start(t["b1"][:, :], dram["b1c"]).then_inc(t["w1_in"], 16)

            normalised_projection(nc, t, "r0p", dram["rwT"], E0, t["L0"], HT=t["HT"], after=first_weights)
            capacity_ffn(nc, t, dram)
        t["share"] = [sb(f"part{k}", [P, T]) for k in range(2)]
        t["one_hot"] = sb("one_hot", [P, 2, T, E1])
        t["best"] = sb("best", [P, 2, T])
        t["slot_f"] = sb("slot_f", [P, 2, T])
        t["running"] = sb("running", [P, E1], F16)
        t["ones"] = sb("ones1", [P, P], F16)
        t["W1_in"] = ctx.enter_context(nc.semaphore("W1_in"))
        t["adj_in"] = [ctx.enter_context(nc.semaphore(f"adjT_in{u}")) for u in range(2)]
        with ExitStack() as experts:
            t["W1"] = experts.enter_context(nc.sbuf_tensor("W1", [P, E1, KD, 2, 2 * F1], F16))
            with ExitStack() as agg:
                t["H"] = agg.enter_context(nc.sbuf_tensor("H2", [P, T, 2 * D + 2], F16))
                t["own"] = agg.enter_context(nc.sbuf_tensor("own", [P, T, D], F32))
                t["adjTf"] = [agg.enter_context(nc.sbuf_tensor(f"adjTf{u}", [P, NP], F32)) for u in range(2)]

                def first_tiles(sp):
                    for u in range(2):
                        sp.dma_start(t["adjTf"][u][:, :], dram["adjT"][u, :, :]).then_inc(t["adj_in"][u], 16)

                normalised_projection(nc, t, "self", dram["WsT"], D, t["own"], bias=(dram["b_self"], dram["b_neigh"]),
                                      H=t["H"], after=first_tiles)
                mean_aggregation(nc, t, dram)
            expert_ffn(nc, t, dram)
        combine_and_store(nc, t, dram, out)


def kernel(**inputs):
    import numpy as np
    import concourse.bacc as bacc
    from concourse.bass_utils import run_bass_kernel_spmd

    a = {k: np.asarray(v) for k, v in inputs.items()}
    full = lambda v, shape: np.ascontiguousarray(np.broadcast_to(v, shape))
    flip = lambda v: np.ascontiguousarray(v.T)
    adj = np.pad(a["adj"], ((0, NP - N), (0, NP - N)))
    adj_tiles = np.ascontiguousarray(adj.reshape(T, P, T, P).transpose(0, 3, 2, 1)).reshape(T, P, NP)
    arrays = {
        "x": np.pad(a["x"], ((0, NP - N), (0, 0))),
        "adj": adj,
        "WT": flip(a["L0_gnn_W"]),
        "awb": full(a["L0_gnn_a_w"].reshape(KD, P).T[:, :, None], (P, KD, P)),
        "ab": full(a["L0_gnn_a_b"].reshape(1, 1), (P, 1)),
        "ident": np.eye(P, dtype=np.float32),
        "fcw": np.ascontiguousarray(a["L0_gnn_fc_w"]),
        "fcb": full(a["L0_gnn_fc_b"], (P, D)),
        "rwT": flip(a["L0_ffn_router_w"]),
        "desc0": full(np.arange(E0, 0, -1, dtype=np.float32), (P, E0)),
        "tri": np.triu(np.ones((P, P), np.float16), 1),
        "ones": np.ones((P, P), np.float16),
        "w1T": flip(a["L0_ffn_w1"]),
        "w2T": flip(a["L0_ffn_w2"]),
        "b1c": flip(a["L0_ffn_b1"].reshape(MF, P)),
        "b2": full(a["L0_ffn_b2"], (P, D)),
        "WsT": flip(a["L1_gnn_W_self"]),
        "WnT": flip(a["L1_gnn_W_neigh"]),
        "adjT": adj_tiles,
        "Wg": a["L1_ffn_Wg"],
        "bg": full(a["L1_ffn_bg"], (P, 2, E1)),
        "desc1": full(np.arange(E1, 0, -1, dtype=np.float32), (P, 2, E1)),
        "region": full(NP * np.arange(E1, dtype=np.float32), (P, 2, E1)),
        "spare": np.arange(2 * NP, 2 * NP + P, dtype=np.float32).reshape(P, 1),
        "places": np.ascontiguousarray(np.arange(2 * NP, dtype=np.float32).reshape(2, T, P).transpose(2, 1, 0)),
        "tile_f": full(np.arange(NS, dtype=np.float32), (P, NS)),
        "limits": full(P * np.arange(T, dtype=np.float32), (P, E1, T)),
        "tile_no": full(np.arange(NS, dtype=np.float32)[:, None], (P, NS, E1)),
        "eW1": np.ascontiguousarray(a["L1_ffn_W1"].reshape(E1, KD, P, 2 * F1).transpose(2, 0, 1, 3)
                                    ).reshape(P, E1, KD * 2 * F1),
        "eW2": np.ascontiguousarray(a["L1_ffn_W2"].reshape(E1, KF, P, D).transpose(2, 0, 1, 3)),
        "eb1": full(a["L1_ffn_b1"], (P, E1, 2 * F1)),
        "eb2": full(a["L1_ffn_b2"], (P, E1, D)),
        "b_self": full(a["L1_gnn_b_self"], (P, D)),
        "b_neigh": full(a["L1_gnn_b_neigh"], (P, D)),
    }
    nc = bacc.Bacc("TRN2", target_bir_lowering=False, num_devices=1)
    dram = {k: nc.dram_tensor(k + "_dram", v.shape, mybir.dt.from_np(v.dtype), kind="ExternalInput").ap()
            for k, v in arrays.items()}
    dram["slot_rows"] = nc.dram_tensor("slot_rows", (SLOT_TILES * P, D + 1), F32, kind="Internal").ap()
    dram["results"] = nc.dram_tensor("results_dram", (2 * NP + P, D), F32, kind="Internal").ap()
    dram["w1_parts"] = nc.dram_tensor("w1_parts", (P, E1, KD * 2 * 2 * F1), F16, kind="Internal").ap()
    dram["peaks"] = nc.dram_tensor("peaks", (E1, P), F32, kind="Internal").ap()
    out = nc.dram_tensor("out_dram", (N, D), F32, kind="ExternalOutput").ap()
    gnn_program(nc, dram, out)
    r = run_bass_kernel_spmd(nc, [{k + "_dram": v for k, v in arrays.items()}], core_ids=[0])
    return r.results[0]["out_dram"]
```
